# Optimizing a Trainium2 kernel written in Bass

```python
import numpy as np
import jax
import jax.numpy as jnp

def _softmax(x, axis=-1):
    return jax.nn.softmax(x, axis=axis)

def _gelu(x):
    return jax.nn.gelu(x, approximate=True)

def _silu(x):
    return jax.nn.silu(x)

def _sigmoid(x):
    return jax.nn.sigmoid(x)

def _layernorm(x, axis=-1, eps=1e-05):
    m = jnp.mean(x, axis=axis, keepdims=True)
    v = jnp.var(x, axis=axis, keepdims=True)
    return (x - m) / jnp.sqrt(v + eps)

def _scatter_add(tgt, idx, src, axis=0):
    return tgt.at[idx].add(src)

def _segment_sum(src, seg, n):
    return jax.ops.segment_sum(src, seg, n)
kernel_name = 'mk_audio_tower_d1_tok_audfeat512_r4_ec619f'

def setup_inputs(seed: int=0):
    np.random.seed(seed)
    _w = jnp.asarray

    def _rec_inputs():
        import jax
        import jax.numpy as jnp
        _rk = jax.random.key(seed)
        x = 7.22013e-05 + 1.00017 * jax.random.normal(jax.random.fold_in(_rk, 1), (32, 125, 64), jnp.float32)
        return x
    x = _rec_inputs()

    def _L0_tok_setup():
        import jax, jax.numpy as jnp
        import numpy as np
        EPS = 1e-07
        C_CURV = 1.0
        LAM_HALF = 1.0 / (1.0 + EPS)
        key = jax.random.key(seed)
        k1, k2 = jax.random.split(key)
        B, L, Cin, K, F = (32, 256, 64, 9, 128)
        x = jax.random.normal(k1, (B, L, Cin), dtype=jnp.float32)
        lim = float(np.sqrt(6.0 / (K * Cin + F)))
        kernel = jax.random.uniform(k2, (K, Cin, F), dtype=jnp.float32, minval=-lim, maxval=lim)
        bias = jnp.zeros((F,), dtype=jnp.float32)
        return {'x': x, 'kernel': kernel, 'bias': bias}
    _L0_tok_all = _L0_tok_setup()
    _L0_tok_in = {k: v for k, v in _L0_tok_all.items() if k in ('kernel', 'bias')}
    del _L0_tok_all

    def _L0_attn_setup():
        import jax, jax.numpy as jnp
        import numpy as np
        from jax import lax
        DIM = 128
        BATCH = 8
        SEQ = 512
        LR = 0.1
        DECAY = 0.9

        def _reference_tuple_inner(x, Wk, bk, Wv, bv, Wq, bq, Wo, bo):
            B, S, D = x.shape
            k = x @ Wk + bk
            v = x @ Wv + bv
            q = x @ Wq + bq
            state0 = jnp.zeros((B, D, D), dtype=x.dtype)

            def step(state, kvq):
                k_t, v_t, q_t = kvq
                mem = jnp.einsum('bd,bde->be', q_t, state)
                new_state = DECAY * state + LR * jnp.einsum('bd,be->bde', k_t, v_t)
                return (new_state, mem)
            kT = jnp.swapaxes(k, 0, 1)
            vT = jnp.swapaxes(v, 0, 1)
            qT = jnp.swapaxes(q, 0, 1)
            final_state, mems = lax.scan(step, state0, (kT, vT, qT))
            outputs = jnp.swapaxes(mems, 0, 1)
            out = outputs @ Wo + bo
            return (out, final_state)
        key = jax.random.key(seed)
        ks = jax.random.split(key, 5)
        scale = DIM ** (-0.5)
        return {'x': jax.random.normal(ks[0], (BATCH, SEQ, DIM), dtype=jnp.float32), 'Wk': jax.random.normal(ks[1], (DIM, DIM), dtype=jnp.float32) * scale, 'bk': jnp.zeros((DIM,), dtype=jnp.float32), 'Wv': jax.random.normal(ks[2], (DIM, DIM), dtype=jnp.float32) * scale, 'bv': jnp.zeros((DIM,), dtype=jnp.float32), 'Wq': jax.random.normal(ks[3], (DIM, DIM), dtype=jnp.float32) * scale, 'bq': jnp.zeros((DIM,), dtype=jnp.float32), 'Wo': jax.random.normal(ks[4], (DIM, DIM), dtype=jnp.float32) * scale, 'bo': jnp.zeros((DIM,), dtype=jnp.float32)}
    _L0_attn_all = _L0_attn_setup()
    _L0_attn_in = {k: v for k, v in _L0_attn_all.items() if k in ('Wk', 'bk', 'Wv', 'bv', 'Wq', 'bq', 'Wo', 'bo')}
    del _L0_attn_all

    def _L0_ffn_setup():
        import jax, jax.numpy as jnp
        import numpy as np
        GRID_SIZE = 5
        SPLINE_ORDER = 3
        NUM_EXPERTS = 8
        TOP_K = 2
        HIDDEN = 128
        D_FF = 256
        N_BASES = GRID_SIZE + SPLINE_ORDER

        def _grid():
            h = 2.0 / GRID_SIZE
            g = jnp.arange(-SPLINE_ORDER, GRID_SIZE + SPLINE_ORDER + 1, dtype=jnp.float32) * h - 1.0
            return g[None, :]

        def b_splines(x, grid):
            xe = x[..., None]
            bases = ((xe >= grid[:, :-1]) & (xe < grid[:, 1:])).astype(x.dtype)
            for j in range(1, SPLINE_ORDER + 1):
                left = (xe - grid[:, :-(j + 1)]) / (grid[:, j:-1] - grid[:, :-(j + 1)])
                right = (grid[:, j + 1:] - xe) / (grid[:, j + 1:] - grid[:, 1:-j])
                bases = left * bases[..., :-1] + right * bases[..., 1:]
            return bases

        def kan_linear(x, base_w, spline_w, scaler, grid):
            base = jax.nn.silu(x) @ base_w.T
            sb = b_splines(x, grid)
            spline = jnp.einsum('nic,oic->no', sb, spline_w * scaler[..., None])
            return base + spline

        def expert_ffn(x, b1, s1, c1, b2, s2, c2, b3, s3, c3, gh, gf):
            h1 = kan_linear(x, b1, s1, c1, gh)
            h2 = kan_linear(x, b2, s2, c2, gh)
            return kan_linear(h1 * h2, b3, s3, c3, gf)
        key = jax.random.key(seed)
        ks = jax.random.split(key, 8)
        x = jax.random.normal(ks[0], (2, 256, HIDDEN), dtype=jnp.float32)
        gate_w = jax.random.normal(ks[1], (NUM_EXPERTS, HIDDEN), dtype=jnp.float32) * HIDDEN ** (-0.5)
        base_w1 = jax.random.normal(ks[2], (NUM_EXPERTS, D_FF, HIDDEN), dtype=jnp.float32) * HIDDEN ** (-0.5)
        spline_w1 = jax.random.normal(ks[3], (NUM_EXPERTS, D_FF, HIDDEN, N_BASES), dtype=jnp.float32) * 0.02
        scaler_w1 = jnp.ones((NUM_EXPERTS, D_FF, HIDDEN), dtype=jnp.float32)
        base_w2 = jax.random.normal(ks[4], (NUM_EXPERTS, D_FF, HIDDEN), dtype=jnp.float32) * HIDDEN ** (-0.5)
        spline_w2 = jax.random.normal(ks[5], (NUM_EXPERTS, D_FF, HIDDEN, N_BASES), dtype=jnp.float32) * 0.02
        scaler_w2 = jnp.ones((NUM_EXPERTS, D_FF, HIDDEN), dtype=jnp.float32)
        base_w3 = jax.random.normal(ks[6], (NUM_EXPERTS, HIDDEN, D_FF), dtype=jnp.float32) * D_FF ** (-0.5)
        spline_w3 = jax.random.normal(ks[7], (NUM_EXPERTS, HIDDEN, D_FF, N_BASES), dtype=jnp.float32) * 0.02
        scaler_w3 = jnp.ones((NUM_EXPERTS, HIDDEN, D_FF), dtype=jnp.float32)
        return {'x': x, 'gate_w': gate_w, 'base_w1': base_w1, 'spline_w1': spline_w1, 'scaler_w1': scaler_w1, 'base_w2': base_w2, 'spline_w2': spline_w2, 'scaler_w2': scaler_w2, 'base_w3': base_w3, 'spline_w3': spline_w3, 'scaler_w3': scaler_w3}
    _L0_ffn_all = _L0_ffn_setup()
    _L0_ffn_in = {k: v for k, v in _L0_ffn_all.items() if k in ('gate_w', 'base_w1', 'spline_w1', 'scaler_w1', 'base_w2', 'spline_w2', 'scaler_w2', 'base_w3', 'spline_w3', 'scaler_w3')}
    del _L0_ffn_all
    return {'x': x, 'L0_tok_kernel': _L0_tok_in['kernel'], 'L0_tok_bias': _L0_tok_in['bias'], 'L0_attn_Wk': _L0_attn_in['Wk'], 'L0_attn_bk': _L0_attn_in['bk'], 'L0_attn_Wv': _L0_attn_in['Wv'], 'L0_attn_bv': _L0_attn_in['bv'], 'L0_attn_Wq': _L0_attn_in['Wq'], 'L0_attn_bq': _L0_attn_in['bq'], 'L0_attn_Wo': _L0_attn_in['Wo'], 'L0_attn_bo': _L0_attn_in['bo'], 'L0_ffn_gate_w': _L0_ffn_in['gate_w'], 'L0_ffn_base_w1': _L0_ffn_in['base_w1'], 'L0_ffn_spline_w1': _L0_ffn_in['spline_w1'], 'L0_ffn_scaler_w1': _L0_ffn_in['scaler_w1'], 'L0_ffn_base_w2': _L0_ffn_in['base_w2'], 'L0_ffn_spline_w2': _L0_ffn_in['spline_w2'], 'L0_ffn_scaler_w2': _L0_ffn_in['scaler_w2'], 'L0_ffn_base_w3': _L0_ffn_in['base_w3'], 'L0_ffn_spline_w3': _L0_ffn_in['spline_w3'], 'L0_ffn_scaler_w3': _L0_ffn_in['scaler_w3']}

def reference(x, L0_tok_kernel, L0_tok_bias, L0_attn_Wk, L0_attn_bk, L0_attn_Wv, L0_attn_bv, L0_attn_Wq, L0_attn_bq, L0_attn_Wo, L0_attn_bo, L0_ffn_gate_w, L0_ffn_base_w1, L0_ffn_spline_w1, L0_ffn_scaler_w1, L0_ffn_base_w2, L0_ffn_spline_w2, L0_ffn_scaler_w2, L0_ffn_base_w3, L0_ffn_spline_w3, L0_ffn_scaler_w3):
    import jax
    import jax.numpy as jnp

    def _L0_tok_ref(x, kernel, bias):
        import jax, jax.numpy as jnp
        import numpy as np
        EPS = 1e-07
        C_CURV = 1.0
        LAM_HALF = 1.0 / (1.0 + EPS)
        B, L, Cin = x.shape
        K, _, F = kernel.shape
        Lout = L - K + 1
        sq = jnp.sum(x * x, axis=-1)
        cs = jnp.concatenate([jnp.zeros((B, 1), x.dtype), jnp.cumsum(sq, axis=1)], axis=1)
        wsq = cs[:, K:] - cs[:, :Lout]
        wnorm = jnp.sqrt(jnp.maximum(wsq, 0.0))
        scale = jnp.where(wnorm < 1.0, 1.0, 1.0 / (wnorm + EPS))[..., None]
        conv = jax.lax.conv_general_dilated(x, kernel, window_strides=(1,), padding='VALID', dimension_numbers=('NWC', 'WIO', 'NWC'))
        v = conv * scale
        v_norm = jnp.maximum(jnp.abs(v), EPS)
        y = jnp.tanh(v_norm * LAM_HALF) * (v / v_norm)
        return jax.nn.relu(y + bias)

    def _L0_attn_ref(x, Wk, bk, Wv, bv, Wq, bq, Wo, bo):
        import jax, jax.numpy as jnp
        import numpy as np
        from jax import lax
        DIM = 128
        BATCH = 8
        SEQ = 512
        LR = 0.1
        DECAY = 0.9

        def _reference_tuple_inner(x, Wk, bk, Wv, bv, Wq, bq, Wo, bo):
            B, S, D = x.shape
            k = x @ Wk + bk
            v = x @ Wv + bv
            q = x @ Wq + bq
            state0 = jnp.zeros((B, D, D), dtype=x.dtype)

            def step(state, kvq):
                k_t, v_t, q_t = kvq
                mem = jnp.einsum('bd,bde->be', q_t, state)
                new_state = DECAY * state + LR * jnp.einsum('bd,be->bde', k_t, v_t)
                return (new_state, mem)
            kT = jnp.swapaxes(k, 0, 1)
            vT = jnp.swapaxes(v, 0, 1)
            qT = jnp.swapaxes(q, 0, 1)
            final_state, mems = lax.scan(step, state0, (kT, vT, qT))
            outputs = jnp.swapaxes(mems, 0, 1)
            out = outputs @ Wo + bo
            return (out, final_state)
        return _reference_tuple_inner(x, Wk, bk, Wv, bv, Wq, bq, Wo, bo)[0]

    def _L0_ffn_ref(x, gate_w, base_w1, spline_w1, scaler_w1, base_w2, spline_w2, scaler_w2, base_w3, spline_w3, scaler_w3):
        import jax, jax.numpy as jnp
        import numpy as np
        GRID_SIZE = 5
        SPLINE_ORDER = 3
        NUM_EXPERTS = 8
        TOP_K = 2
        HIDDEN = 128
        D_FF = 256
        N_BASES = GRID_SIZE + SPLINE_ORDER

        def _grid():
            h = 2.0 / GRID_SIZE
            g = jnp.arange(-SPLINE_ORDER, GRID_SIZE + SPLINE_ORDER + 1, dtype=jnp.float32) * h - 1.0
            return g[None, :]

        def b_splines(x, grid):
            xe = x[..., None]
            bases = ((xe >= grid[:, :-1]) & (xe < grid[:, 1:])).astype(x.dtype)
            for j in range(1, SPLINE_ORDER + 1):
                left = (xe - grid[:, :-(j + 1)]) / (grid[:, j:-1] - grid[:, :-(j + 1)])
                right = (grid[:, j + 1:] - xe) / (grid[:, j + 1:] - grid[:, 1:-j])
                bases = left * bases[..., :-1] + right * bases[..., 1:]
            return bases

        def kan_linear(x, base_w, spline_w, scaler, grid):
            base = jax.nn.silu(x) @ base_w.T
            sb = b_splines(x, grid)
            spline = jnp.einsum('nic,oic->no', sb, spline_w * scaler[..., None])
            return base + spline

        def expert_ffn(x, b1, s1, c1, b2, s2, c2, b3, s3, c3, gh, gf):
            h1 = kan_linear(x, b1, s1, c1, gh)
            h2 = kan_linear(x, b2, s2, c2, gh)
            return kan_linear(h1 * h2, b3, s3, c3, gf)
        B, S, H = x.shape
        gh, gf = (_grid(), _grid())
        xt = x.reshape(-1, H)
        logits = xt @ gate_w.T
        topw, sel = jax.lax.top_k(logits, TOP_K)
        topw = jax.nn.softmax(topw.astype(jnp.float32), axis=-1).astype(x.dtype)
        out = jnp.zeros_like(xt)
        for i in range(NUM_EXPERTS):
            ey = expert_ffn(xt, base_w1[i], spline_w1[i], scaler_w1[i], base_w2[i], spline_w2[i], scaler_w2[i], base_w3[i], spline_w3[i], scaler_w3[i], gh, gf)
            gi = jnp.sum(jnp.where(sel == i, topw, 0.0), axis=-1)
            out = out + gi[:, None] * ey
        return out.reshape(B, S, H)
    h = _L0_tok_ref(x, L0_tok_kernel, L0_tok_bias)
    h = h + _L0_attn_ref(_layernorm(h, axis=-1), L0_attn_Wk, L0_attn_bk, L0_attn_Wv, L0_attn_bv, L0_attn_Wq, L0_attn_bq, L0_attn_Wo, L0_attn_bo)
    h = h + _L0_ffn_ref(_layernorm(h, axis=-1), L0_ffn_gate_w, L0_ffn_base_w1, L0_ffn_spline_w1, L0_ffn_scaler_w1, L0_ffn_base_w2, L0_ffn_spline_w2, L0_ffn_scaler_w2, L0_ffn_base_w3, L0_ffn_spline_w3, L0_ffn_scaler_w3)
    return h

_drawn_inputs = setup_inputs


def setup_inputs(seed=0):
    import zlib

    import numpy as np

    out = dict(_drawn_inputs(seed))
    spreads = {'L0_tok_bias': (0.0, 0.1),
     'L0_attn_bk': (0.0, 0.1),
     'L0_attn_bv': (0.0, 0.1),
     'L0_attn_bq': (0.0, 0.1),
     'L0_attn_bo': (0.0, 0.8),
     'L0_ffn_scaler_w1': (1.0, 0.6),
     'L0_ffn_scaler_w2': (1.0, 0.6),
     'L0_ffn_scaler_w3': (1.0, 0.6)}
    factors = {'L0_ffn_gate_w': 6.427,
     'L0_ffn_base_w1': 4.454,
     'L0_ffn_spline_w1': 8.0,
     'L0_ffn_base_w2': 3.45,
     'L0_ffn_spline_w2': 8.0,
     'L0_ffn_base_w3': 4.419,
     'L0_ffn_spline_w3': 4.015}
    for name, (base, spread) in spreads.items():
        noise = np.random.default_rng([zlib.crc32(name.encode()), seed]).standard_normal(out[name].shape)
        drawn = base * np.exp(spread * noise) if base else spread * noise
        out[name] = jnp.asarray(drawn.astype(out[name].dtype))
    for name, factor in factors.items():
        out[name] = (out[name] * factor).astype(out[name].dtype)
    return out
```

```python
from contextlib import ExitStack

import numpy as np
import concourse.bass as bass
from concourse import mybir
from concourse.alu_op_type import AluOpType as ALU

ACT = mybir.ActivationFunctionType
AX = mybir.AxisListType
F32 = mybir.dt.float32
I32 = mybir.dt.int32
U32 = mybir.dt.uint32

B, L, C = 32, 125, 64
K, D = 9, 128
S = L - K + 1
TOK = B * S
NE, TOPK, FF = 8, 2, 256
NB = 8
KC = NB + 1
NBLK = 6
BLK = KC * D
RAW = BLK + D
GB = 4
NG = B // GB
GT = GB * S
TAPS2 = (K + 1) // 2
TS = 128
NT = (TOK * TOPK + NE * (TS - 1)) // TS
REG = TOK + TS
RW = D + 2
WPG = NE * NBLK // NG
EPS_LN = 1e-5
EPS_TOK = 1e-7
LAM_HALF = 1.0 / (1.0 + EPS_TOK)
H_GRID = 2.0 / 5
assert NT % 2 == 0 and NG % 2 == 0 and WPG % 3 == 0

_cols = {}
_at = 0
for _name, _n in (("ident", D), ("decay", S), ("before", S), ("ones", D), ("expert", NE), ("padrow", NE),
                  ("dump", 1), ("token", B), ("tile", NT + 1), ("half", GB), ("minushalf", GB),
                  ("b_tok", D), ("b_v", D), ("b_o", D), ("region", NE)):
    _cols[_name] = (_at, _at + _n)
    _at += _n
NCONST = _at


def constants():
    c = np.zeros((D, NCONST), np.float32)

    def put(name, a):
        c[:a.shape[0], _cols[name][0]:_cols[name][1]] = a

    put("ident", np.eye(D))
    s, t = np.arange(S)[:, None], np.arange(S)[None, :]
    put("decay", np.where(t > s, 0.1 * 0.9 ** np.maximum(t - 1 - s, 0), 0.0))
    put("before", (s < t).astype(np.float32))
    put("ones", np.ones((D, D)))
    put("expert", np.tile(np.arange(NE), (D, 1)))
    put("padrow", np.arange(NE)[None, :] * REG + np.arange(D)[:, None])
    put("dump", TOK + np.arange(D)[:, None])
    put("token", np.arange(B)[None, :] * S + np.arange(D)[:, None])
    put("tile", np.tile(np.arange(NT + 1), (D, 1)))
    put("half", np.full((D, GB), 0.5))
    put("minushalf", np.full((D, GB), -0.5))
    put("region", np.tile(np.arange(NE) * REG, (D, 1)))
    return c


def audio_tower(nc, x2, wconv, wattn, battn, wgate, wraw, consts, out):
    with ExitStack() as ctx:
        groups_memory = ExitStack()
        held_by = [ctx]

        def sb(name, shape, dt=F32):
            return held_by[0].enter_context(nc.sbuf_tensor(name, shape, dt))

        def ps(name, shape):
            return ctx.enter_context(nc.psum_tensor(name, shape, F32))

        def sem(name):
            return ctx.enter_context(nc.semaphore(name))

        w_scaled = nc.dram_tensor("w_scaled", (NE * NBLK, D, BLK), F32).ap()
        routed = nc.dram_tensor("routed", (NE * REG + TS, RW), F32).ap()

        cst = sb("cst", [D, NCONST])

        def const(name, rows=D):
            return cst[0:rows, _cols[name][0]:_cols[name][1]]

        wc = sb("wc", [D, TAPS2 * D])
        wa = sb("wa", [D, 4 * D])
        ba = sb("ba", [D, 2])
        wg = sb("wg", [D, NE])

        count = [sb(f"count{p}", [D, NE]) for p in range(2)]
        padrow = sb("padrow", [D, RW])
        padf = sb("padf", [D, NE])
        padi = sb("padi", [D, NE], I32)
        cnt_i = sb("cnt_i", [D, NE], I32)
        nt_i = sb("nt_i", [D, NE], I32)
        nt_f = sb("nt_f", [D, NE])
        end_a = sb("end_a", [D, NE])
        end_b = sb("end_b", [D, NE])
        first = sb("first", [D, NE])
        base = sb("base", [D, NE + 1])
        past = sb("past", [1, NT + 1, NE])
        past_n = sb("past_n", [1, NT + 1])
        is_e = sb("is_e", [1, NT + 1, NE + 1])
        rs_e = sb("rs_e", [1, NT + 1, NE + 1])
        rs_f = sb("rs_f", [1, NT + 1])
        eidx = sb("eidx", [1, NT + 1])
        expert9 = sb("expert9", [1, NE + 1])
        tile_row = sb("tile_row", [1, NT + 1], I32)
        tile_blk = sb("tile_blk", [1, NT + 1], I32)
        tile_new = sb("tile_new", [1, NT + 1], I32)
        held_by[0] = groups_memory
        xs = [sb(f"xs{p}", [D, GB * L]) for p in range(2)]
        xq = [sb(f"xq{p}", [D, GB * L]) for p in range(2)]
        xq2 = [sb(f"xq2{p}", [D, GB * L]) for p in range(2)]
        xq4 = [sb(f"xq4{p}", [D, GB * L]) for p in range(2)]
        wsq = [sb(f"wsq{p}", [S, GB]) for p in range(2)]
        wnorm = [sb(f"wnorm{p}", [S, GB]) for p in range(2)]
        wnorm_e = [sb(f"wnorm_e{p}", [S, GB]) for p in range(2)]
        winv = [sb(f"winv{p}", [S, GB]) for p in range(2)]
        wscale = [sb(f"wscale{p}", [S, GB]) for p in range(2)]
        y = [sb(f"y{p}", [S, GB, D]) for p in range(2)]
        h = [sb(f"h{p}", [S, GB, D]) for p in range(2)]
        hb = [sb(f"hb{p}", [S, GB, D]) for p in range(2)]
        st1 = [sb(f"st1{p}", [S, GB, 6]) for p in range(2)]
        mv1 = [sb(f"mv1{p}", [S, GB, 2]) for p in range(2)]
        ve1 = [sb(f"ve1{p}", [S, GB]) for p in range(2)]
        rstd1 = [sb(f"rstd1{p}", [S, GB]) for p in range(2)]
        xn = [sb(f"xn{p}", [S, GB, D]) for p in range(2)]
        xnT = [sb(f"xnT{p}", [D, GT]) for p in range(2)]
        qT = [sb(f"qT{p}", [D, GT]) for p in range(2)]
        kT = [sb(f"kT{p}", [D, GT]) for p in range(2)]
        v = [sb(f"v{p}", [S, GB, D]) for p in range(2)]
        am = [sb(f"am{p}", [S, GB, S]) for p in range(2)]
        memT = [sb(f"memT{p}", [D, GT]) for p in range(2)]
        h2 = [sb(f"h2{p}", [S, GB, D]) for p in range(2)]
        st2 = [sb(f"st2{p}", [S, GB, 6]) for p in range(2)]
        mv2 = [sb(f"mv2{p}", [S, GB, 2]) for p in range(2)]
        ve2 = [sb(f"ve2{p}", [S, GB]) for p in range(2)]
        rstd2 = [sb(f"rstd2{p}", [S, GB]) for p in range(2)]
        rows = [sb(f"rows{p}", [S, GB, TOPK, RW]) for p in range(2)]
        x2T = [sb(f"x2T{p}", [D, GT]) for p in range(2)]
        lg = [sb(f"lg{p}", [S, GB, NE]) for p in range(2)]
        top = [sb(f"top{p}", [S, GB, 8]) for p in range(2)]
        topi = [sb(f"topi{p}", [S, GB, 8], U32) for p in range(2)]
        topf = [sb(f"topf{p}", [S, GB, TOPK]) for p in range(2)]
        dlg = [sb(f"dlg{p}", [S, GB]) for p in range(2)]
        e2 = [sb(f"e2{p}", [S, GB]) for p in range(2)]
        e21 = [sb(f"e21{p}", [S, GB]) for p in range(2)]
        oh = [[sb(f"oh{k}{p}", [S, GB, NE]) for p in range(2)] for k in range(TOPK)]
        chosen = [sb(f"chosen{p}", [S, GB, NE]) for p in range(2)]
        cum = [sb(f"cum{p}", [S, GB + 1, NE]) for p in range(2)]
        place = [sb(f"place{p}", [S, GB, NE]) for p in range(2)]
        placek = [[sb(f"placek{k}{p}", [S, GB, NE]) for p in range(2)] for k in range(TOPK)]
        posf = [sb(f"posf{p}", [S, GB, TOPK]) for p in range(2)]
        pos = [sb(f"pos{p}", [S, GB * TOPK], I32) for p in range(2)]
        start_at = [sb(f"start_at{p}", [D, NE]) for p in range(2)]

        wst = [sb(f"wst{i}", [D, RAW]) for i in range(3)]

        groups_memory.close()
        held_by[0] = ctx
        wb = [sb(f"wb{k}", [D, KC, D]) for k in range(NBLK)]
        xr = [sb(f"xr{p}", [TS, RW]) for p in range(2)]
        gate = [sb(f"gate{p}", [TS, 1]) for p in range(2)]
        number = [sb(f"number{p}", [TS, 1], I32) for p in range(2)]
        u = [[sb(f"u{c}{p}", [D, TS]) for p in range(2)] for c in range(3)]
        th = [sb(f"th{c}", [D, TS]) for c in range(3)]
        feat = [[sb(f"feat{c}{p}", [D, KC, TS]) for p in range(2)] for c in range(3)]
        fa = [sb(f"fa{c}", [D, NB, TS]) for c in range(3)]
        fm2 = [sb(f"fm2{c}", [D, NB, TS]) for c in range(3)]
        fr1 = [sb(f"fr1{c}", [D, NB, TS]) for c in range(3)]
        fs2 = [sb(f"fs2{c}", [D, NB, TS]) for c in range(3)]
        fs1 = [sb(f"fs1{c}", [D, NB, TS]) for c in range(3)]
        g2 = [sb(f"g2{i}", [D, TS]) for i in range(2)]
        ye = [sb(f"ye{p}", [TS, D]) for p in range(2)]

        bank = [ps(f"bank{i}", [D, 512]) for i in range(8)]

        def tokens(b, n):
            return b[0:S, 0:GB * n].rearrange("p (b n) -> p b n", b=GB)

        conv_ps = [tokens(bank[p], D) for p in range(2)]
        xnT_ps = bank[2][:, 0:GT]
        at_ps = tokens(bank[2], S)
        qT_ps = bank[3][:, 0:GT]
        memT_ps = bank[3][:, 0:GT]
        kT_ps = bank[4][:, 0:GT]
        o_ps = tokens(bank[4], D)
        v_ps = tokens(bank[5], D)
        x2T_ps = bank[6][:, 0:GT]
        wsq_ps = bank[7][0:S, 0:GB]
        lg_ps = bank[6][0:S, 0:GB * NE].rearrange("p (b n) -> p b n", b=GB)
        place_ps = bank[6][:, 64:64 + (GB + 1) * NE].rearrange("p (b n) -> p b n", b=GB + 1)
        hid_ps = [[bank[2 * p + i][:, 0:2 * TS].rearrange("p (k n) -> p k n", k=2) for i in range(2)]
                  for p in range(2)]
        y_ps = [bank[4 + p][:, 0:D] for p in range(2)]
        xT_ps = [bank[6 + p][:, 0:TS] for p in range(2)]

        n_ld = sem("params_loaded")
        s = {n: sem(n) for n in (
            "x_squared", "sq_pairs", "sq_quads", "window_sums", "wsq_ready", "wnorm_ready",
            "wnorm_eps", "winv_ready", "wscale_ready", "conv_done", "tanh_done", "y_biased", "h_ready",
            "hb_ready", "stats1", "aggr1", "var1", "rstd1_ready", "xn_ready", "xnT_done", "xnT_ready",
            "qkv_done", "qT_ready", "kT_ready", "v_ready", "scores_done", "am_ready", "mem_done",
            "memT_ready", "o_done", "h2_ready", "stats2", "aggr2", "var2", "rstd2_ready",
            "x2_ready", "x2_copied", "ids_ready", "x2T_done", "x2T_ready", "logits_done", "lg_ready",
            "top_ready", "topi_ready", "topf_ready", "dlg_ready", "e2_ready", "e21_ready", "gate1_ready",
            "gate2_ready", "oh1_ready", "oh2_ready", "chosen_ready", "cum_ready", "places_done",
            "place_ready", "placek_ready", "posf_ready", "pos_ready", "count_ready", "start_ready",
            "w_scaled_up", "setup", "table", "tables_ready",
            "pad_sent", "dump_zeroed",
            "tags_ready", "xT_done", "hidden_done", "g2_ready", "expert_out", "ye_ready", "out_added", "pool_goes_on")}
        x_loaded = [sem(f"x_loaded{p}") for p in range(2)]
        h2_stored = [sem(f"h2_stored{p}") for p in range(2)]
        rows_sent = [sem(f"rows_sent{p}") for p in range(2)]
        row_loaded = [sem(f"row_loaded{p}") for p in range(2)]
        w_loaded = [sem(f"w_loaded{i}") for i in range(3)]
        w_stored = [sem(f"w_stored{i}") for i in range(3)]
        blk_loaded = [sem(f"blk_loaded{k}") for k in range(NBLK)]
        u_ready = [sem(f"u_ready{c}") for c in range(3)]
        abs_ready = [sem(f"abs_ready{c}") for c in range(3)]
        m2_ready = [sem(f"m2_ready{c}") for c in range(3)]
        r1_ready = [sem(f"r1_ready{c}") for c in range(3)]
        s1_ready = [sem(f"s1_ready{c}") for c in range(3)]
        s2_ready = [sem(f"s2_ready{c}") for c in range(3)]
        th_ready = [sem(f"th_ready{c}") for c in range(3)]
        c1_ready = [sem(f"c1_ready{c}") for c in range(3)]
        c2_ready = [sem(f"c2_ready{c}") for c in range(3)]
        feat_ready = [sem(f"feat_ready{c}") for c in range(3)]

        def due(n):
            return not isinstance(n, int) or n > 0

        def nth(n, p, each=1):
            return 8 * each * (n - p + 2)

        NPARAM = 5

        def held(eng):
            eng.wait_ge(n_ld, 16 * NPARAM)

        def sp_group(sp, g, p):
            if due(g - 1):
                sp.wait_ge(s["conv_done"], g - 1)
            if due(g - 1):
                sp.wait_ge(s["x_squared"], g - 1)
            sp.dma_start(xs[p][:], x2[:, bass.ds(g * GB * L, GB * L)]).then_inc(x_loaded[p], 16)

        def sp_weights(sp, g):
            for i in range(WPG):
                n = g * WPG + i
                sp.wait_ge(s["w_scaled_up"], n + 1)
                sp.dma_start(w_scaled[bass.ds(n, 1)].rearrange("o p c -> (o p) c"),
                             wst[i % 3][:, 0:BLK]).then_inc(w_stored[i % 3], 16)
                if isinstance(g, int) and not 3 <= n + 2 < NE * NBLK:
                    continue
                q = (i - 1) % 3
                if due(16 * (g * (WPG // 3) + (i + 2) // 3)):
                    sp.wait_ge(w_stored[q], 16 * (g * (WPG // 3) + (i + 2) // 3))
                sp.dma_start(wst[q][:], wraw[bass.ds(n + 2, 1)].rearrange("o p c -> (o p) c")
                             ).then_inc(w_loaded[q], 16)

        def sp_h2(sp, g, p):
            sp.wait_ge(s["h2_ready"], g + 1)
            sp.dma_start(out[bass.ds(g * GT, GT)].rearrange("(b t) d -> t b d", b=GB), h2[p][:]
                         ).then_inc(h2_stored[p], 16)

        def dve_weights(dve, g):
            for i in range(WPG):
                n = g * WPG + i
                dve.wait_ge(w_loaded[i % 3], 16 * (g * (WPG // 3) + i // 3 + 1))
                w3 = wst[i % 3][:, 0:NB * D].rearrange("p (c o) -> p c o", c=NB)
                scaler = wst[i % 3][:, BLK:RAW].unsqueeze(1).broadcast_to([D, NB, D])
                nc.vector.scalar_tensor_tensor(w3, w3, -1.0 / 6.0, scaler, ALU.mult, ALU.mult
                                               ).then_inc(s["w_scaled_up"], 1)

        def pe_window(pe, g, p):
            pe.wait_ge(s["sq_quads"], g + 1)
            if due(g):
                pe.wait_ge(s["wsq_ready"], g)
            for b in range(GB):
                pe.matmul(wsq_ps[:, b:b + 1], xq4[p][:, b * L:b * L + S], const("ones")[:, 0:1],
                          start=True, stop=False)
                mm = pe.matmul(wsq_ps[:, b:b + 1], xq[p][0:C, b * L + K - 1:b * L + K - 1 + S],
                               const("ones")[0:C, 0:1], start=False, stop=True)
            mm.then_inc(s["window_sums"], 1)

        def pe_conv(pe, g, p, b):
            if b == 0:
                pe.wait_ge(x_loaded[p], nth(g, p))
                if due(g - 1):
                    pe.wait_ge(s["tanh_done"], g - 1)
            for j in range(TAPS2):
                n = D if j < TAPS2 - 1 else C
                mm = pe.matmul(conv_ps[p][:, b, :], xs[p][0:n, b * L + 2 * j:b * L + 2 * j + S],
                               wc[0:n, j * D:(j + 1) * D], start=(j == 0), stop=(j == TAPS2 - 1))
            if b == GB - 1:
                mm.then_inc(s["conv_done"], 1)

        def pe_xnT(pe, g, p):
            pe.wait_ge(s["xn_ready"], g + 1)
            if due(g):
                pe.wait_ge(s["am_ready"], g)
            for b in range(GB):
                mm = pe.transpose(xnT_ps[:, b * S:(b + 1) * S], xn[p][:, b, :], const("ident", S)[:, 0:S])
            mm.then_inc(s["xnT_done"], 1)

        def pe_qkv(pe, g, p):
            pe.wait_ge(s["xnT_ready"], g + 1)
            if due(g):
                pe.wait_ge(s["memT_ready"], g)
            pe.matmul(qT_ps, wa[:, 2 * D:3 * D], xnT[p][:], start=True, stop=True)
            if due(g):
                pe.wait_ge(s["h2_ready"], g)
            pe.matmul(kT_ps, wa[:, 0:D], xnT[p][:], start=True, stop=True)
            if due(g):
                pe.wait_ge(s["v_ready"], g)
            for b in range(GB):
                mm = pe.matmul(v_ps[:, b, :], xnT[p][:, b * S:(b + 1) * S], wa[:, D:2 * D],
                               start=True, stop=True)
            mm.then_inc(s["qkv_done"], 1)

        def pe_scores(pe, g, p):
            pe.wait_ge(s["qT_ready"], g + 1)
            pe.wait_ge(s["kT_ready"], g + 1)
            for b in range(GB):
                mm = pe.matmul(at_ps[:, b, :], kT[p][:, b * S:(b + 1) * S], qT[p][:, b * S:(b + 1) * S],
                               start=True, stop=True)
            mm.then_inc(s["scores_done"], 1)

        def pe_mem(pe, g, p):
            pe.wait_ge(s["am_ready"], g + 1)
            pe.wait_ge(s["v_ready"], g + 1)
            for b in range(GB):
                mm = pe.matmul(memT_ps[:, b * S:(b + 1) * S], v[p][:, b, :], am[p][:, b, :],
                               start=True, stop=True)
            mm.then_inc(s["mem_done"], 1)

        def pe_o(pe, g, p):
            pe.wait_ge(s["memT_ready"], g + 1)
            for b in range(GB):
                mm = pe.matmul(o_ps[:, b, :], memT[p][:, b * S:(b + 1) * S], wa[:, 3 * D:4 * D],
                               start=True, stop=True)
            mm.then_inc(s["o_done"], 1)

        def pe_x2T(pe, g, p):
            pe.wait_ge(s["x2_ready"], g + 1)
            if due(g):
                pe.wait_ge(s["place_ready"], g)
            if due(g):
                pe.wait_ge(s["count_ready"], g)
            for b in range(GB):
                mm = pe.transpose(x2T_ps[:, b * S:(b + 1) * S], rows[p][:, b, 0, 0:D],
                                  const("ident", S)[:, 0:S])
            mm.then_inc(s["x2T_done"], 1)

        def pe_logits(pe, g, p):
            pe.wait_ge(s["x2T_ready"], g + 1)
            for b in range(GB):
                mm = pe.matmul(lg_ps[:, b, :], x2T[p][:, b * S:(b + 1) * S], wg[:], start=True, stop=True)
            mm.then_inc(s["logits_done"], 1)

        def pe_places(pe, g, p):
            pe.wait_ge(s["cum_ready"], g + 1)
            pe.matmul(place_ps[:], const("ones", S), cum[p][:], start=True, stop=True)
            pe.matmul(place_ps[0:S, 0:GB, :], const("before", S), chosen[p][:], start=False, stop=True,
                      skip_group_check=True).then_inc(s["places_done"], 1)

        def act_square(act, g, p):
            act.wait_ge(x_loaded[p], nth(g, p))
            if due(g - 1):
                act.wait_ge(s["window_sums"], g - 1)
            if due(g - 1):
                act.wait_ge(s["sq_pairs"], g - 1)
            nc.scalar.activation(xq[p][:], xs[p][:], ACT.Square).then_inc(s["x_squared"], 1)

        def act_tanh(act, g, p):
            act.wait_ge(s["conv_done"], g + 1)
            act.wait_ge(s["wscale_ready"], g + 1)
            if due(g - 1):
                act.wait_ge(s["y_biased"], g - 1)
            for b in range(GB):
                a = nc.scalar.activation(y[p][:, b, :], conv_ps[p][:, b, :], ACT.Tanh,
                                         scale=wscale[p][:, b:b + 1])
            a.then_inc(s["tanh_done"], 1)

        def act_xnT(act, g, p):
            act.wait_ge(s["xnT_done"], g + 1)
            if due(g - 1):
                act.wait_ge(s["qkv_done"], g - 1)
            nc.scalar.activation(xnT[p][:], xnT_ps, ACT.Copy).then_inc(s["xnT_ready"], 1)

        def act_qk(act, g, p):
            act.wait_ge(s["qkv_done"], g + 1)
            if due(g - 1):
                act.wait_ge(s["scores_done"], g - 1)
            nc.scalar.activation(qT[p][:], qT_ps, ACT.Identity, bias=ba[:, 1:2]).then_inc(s["qT_ready"], 1)
            nc.scalar.activation(kT[p][:], kT_ps, ACT.Identity, bias=ba[:, 0:1]).then_inc(s["kT_ready"], 1)

        def act_memT(act, g, p):
            act.wait_ge(s["mem_done"], g + 1)
            if due(g - 1):
                act.wait_ge(s["o_done"], g - 1)
            nc.scalar.activation(memT[p][:], memT_ps, ACT.Copy).then_inc(s["memT_ready"], 1)

        def act_x2(act, g, p):
            act.wait_ge(s["x2_ready"], g + 1)
            if due(nth(g - 2, p, GB * TOPK)):
                act.wait_ge(rows_sent[p], nth(g - 2, p, GB * TOPK))
            nc.scalar.activation(rows[p][:, :, 1, 0:D], rows[p][:, :, 0, 0:D], ACT.Copy
                                 ).then_inc(s["x2_copied"], 1)

        def act_x2T(act, g, p):
            act.wait_ge(s["x2T_done"], g + 1)
            if due(g - 1):
                act.wait_ge(s["logits_done"], g - 1)
            nc.scalar.activation(x2T[p][:], x2T_ps, ACT.Copy).then_inc(s["x2T_ready"], 1)

        def act_e2(act, g, p):
            act.wait_ge(s["dlg_ready"], g + 1)
            if due(g - 1):
                act.wait_ge(s["gate2_ready"], g - 1)
            nc.scalar.activation(e2[p][:], dlg[p][:], ACT.Exp).then_inc(s["e2_ready"], 1)

        def pool_sq(pool, g, p):
            w2, w4 = GB * L - 2, GB * L - 6
            pool.wait_ge(s["x_squared"], g + 1)
            if due(g - 1):
                pool.wait_ge(s["sq_quads"], g - 1)
            pool.tensor_tensor(xq2[p][:, 0:w2], xq[p][:, 0:w2], xq[p][:, 2:w2 + 2], ALU.add
                               ).then_inc(s["sq_pairs"], 1)
            pool.wait_ge(s["sq_pairs"], g + 1)
            if due(g - 1):
                pool.wait_ge(s["window_sums"], g - 1)
            pool.tensor_tensor(xq4[p][:, 0:w4], xq2[p][:, 0:w4], xq2[p][:, 4:w4 + 4], ALU.add
                               ).then_inc(s["sq_quads"], 1)

        def pool_wnorm(pool, g, p):
            pool.wait_ge(s["wsq_ready"], g + 1)
            if due(g - 1):
                pool.wait_ge(s["wnorm_eps"], g - 1)
            pool.tensor_tensor(wnorm[p][:], wsq[p][:], const("half", S), ALU.pow).then_inc(s["wnorm_ready"], 1)

        def pool_bias(pool, g, p):
            pool.wait_ge(s["tanh_done"], g + 1)
            yb = const("b_tok", S).unsqueeze(1).broadcast_to([S, GB, D])
            pool.tensor_tensor(y[p][:], y[p][:], yb, ALU.add).then_inc(s["y_biased"], 1)

        def pool_rstd1(pool, g, p):
            pool.wait_ge(s["var1"], g + 1)
            if due(g - 1):
                pool.wait_ge(s["xn_ready"], g - 1)
            pool.tensor_tensor(rstd1[p][:], ve1[p][:], const("minushalf", S), ALU.pow
                               ).then_inc(s["rstd1_ready"], 1)

        def pool_hb(pool, g, p):
            pool.wait_ge(s["h_ready"], g + 1)
            if due(g - 1):
                pool.wait_ge(s["h2_ready"], g - 1)
            ob = const("b_o", S).unsqueeze(1).broadcast_to([S, GB, D])
            pool.tensor_tensor(hb[p][:], h[p][:], ob, ALU.add).then_inc(s["hb_ready"], 1)

        def pool_rstd2(pool, g, p):
            pool.wait_ge(s["var2"], g + 1)
            if due(g - 1):
                pool.wait_ge(s["x2_ready"], g - 1)
            pool.tensor_tensor(rstd2[p][:], ve2[p][:], const("minushalf", S), ALU.pow
                               ).then_inc(s["rstd2_ready"], 1)

        def pool_rows(pool, g, p):
            held(pool)
            pool.wait_ge(s["pos_ready"], g + 1)
            pool.wait_ge(s["gate1_ready"], g + 1)
            pool.wait_ge(s["gate2_ready"], g + 1)
            pool.wait_ge(s["x2_ready"], g + 1)
            pool.wait_ge(s["x2_copied"], g + 1)
            pool.wait_ge(s["ids_ready"], g + 1)
            for b in range(GB):
                for k in range(TOPK):
                    i = b * TOPK + k
                    pool.indirect_dma_start(routed, bass.IndirectOffsetOnAxis(pos[p][:, i:i + 1], 0),
                                            rows[p][:, b, k, :], None).then_inc(rows_sent[p], 16)

        def dve_wsq(dve, g, p):
            dve.wait_ge(s["window_sums"], g + 1)
            if due(g - 1):
                dve.wait_ge(s["wnorm_ready"], g - 1)
            nc.vector.tensor_scalar(wsq[p][:], wsq_ps, 0.0, None, ALU.max).then_inc(s["wsq_ready"], 1)

        def dve_wscale(dve, g, p):
            dve.wait_ge(s["wnorm_ready"], g + 1)
            nc.vector.tensor_scalar(wnorm_e[p][:], wnorm[p][:], EPS_TOK, None, ALU.add
                                    ).then_inc(s["wnorm_eps"], 1)
            dve.wait_ge(s["wnorm_eps"], g + 1)
            nc.vector.reciprocal(winv[p][:], wnorm_e[p][:]).then_inc(s["winv_ready"], 1)
            dve.wait_ge(s["winv_ready"], g + 1)
            if due(g - 1):
                dve.wait_ge(s["tanh_done"], g - 1)
            nc.vector.tensor_scalar(wscale[p][:], winv[p][:], 1.0, LAM_HALF, ALU.min, ALU.mult
                                    ).then_inc(s["wscale_ready"], 1)

        def dve_ln(dve, g, p, src, st, mv, ve, stats, aggr, var):
            for b in range(GB):
                i = nc.vector.bn_stats(st[p][:, b, :], src[p][:, b, :])
            i.then_inc(s[stats], 1)
            held(dve)
            dve.wait_ge(s[stats], g + 1)
            for b in range(GB):
                i = nc.vector.bn_aggr(mv[p][:, b, :], st[p][:, b, :])
            i.then_inc(s[aggr], 1)
            dve.wait_ge(s[aggr], g + 1)
            nc.vector.tensor_scalar(ve[p][:], mv[p][:, :, 1], EPS_LN, None, ALU.add).then_inc(s[var], 1)

        def dve_h(dve, g, p):
            dve.wait_ge(s["y_biased"], g + 1)
            if due(g - 1):
                dve.wait_ge(s["hb_ready"], g - 1)
            nc.vector.tensor_scalar(h[p][:], y[p][:], 0.0, None, ALU.max).then_inc(s["h_ready"], 1)
            dve.wait_ge(s["h_ready"], g + 1)
            if due(g - 1):
                dve.wait_ge(s["rstd1_ready"], g - 1)
            dve_ln(dve, g, p, h, st1, mv1, ve1, "stats1", "aggr1", "var1")

        def dve_xn(dve, g, p):
            dve.wait_ge(s["rstd1_ready"], g + 1)
            if due(g - 1):
                dve.wait_ge(s["xnT_done"], g - 1)
            for b in range(GB):
                i = nc.vector.tensor_scalar(xn[p][:, b, :], h[p][:, b, :], mv1[p][:, b, 0:1],
                                            rstd1[p][:, b:b + 1], ALU.subtract, ALU.mult)
            i.then_inc(s["xn_ready"], 1)

        def dve_v(dve, g, p):
            dve.wait_ge(s["qkv_done"], g + 1)
            if due(g - 1):
                dve.wait_ge(s["mem_done"], g - 1)
            nc.vector.tensor_tensor(v[p][:], v_ps, const("b_v", S).unsqueeze(1).broadcast_to([S, GB, D]),
                                    ALU.add).then_inc(s["v_ready"], 1)

        def dve_am(dve, g, p):
            dve.wait_ge(s["scores_done"], g + 1)
            if due(g - 1):
                dve.wait_ge(s["mem_done"], g - 1)
            nc.vector.tensor_tensor(am[p][:], at_ps, const("decay", S).unsqueeze(1).broadcast_to([S, GB, S]),
                                    ALU.mult).then_inc(s["am_ready"], 1)

        def dve_h2(dve, g, p):
            dve.wait_ge(s["o_done"], g + 1)
            dve.wait_ge(s["hb_ready"], g + 1)
            if due(nth(g - 2, p)):
                dve.wait_ge(h2_stored[p], nth(g - 2, p))
            nc.vector.tensor_tensor(h2[p][:], o_ps, hb[p][:], ALU.add).then_inc(s["h2_ready"], 1)
            dve.wait_ge(s["h2_ready"], g + 1)
            if due(g - 1):
                dve.wait_ge(s["rstd2_ready"], g - 1)
            dve_ln(dve, g, p, h2, st2, mv2, ve2, "stats2", "aggr2", "var2")

        def dve_x2(dve, g, p):
            dve.wait_ge(s["rstd2_ready"], g + 1)
            if due(nth(g - 2, p, GB * TOPK)):
                dve.wait_ge(rows_sent[p], nth(g - 2, p, GB * TOPK))
            if due(g - 1):
                dve.wait_ge(s["x2T_done"], g - 1)
            for b in range(GB):
                i = nc.vector.tensor_scalar(rows[p][:, b, 0, 0:D], h2[p][:, b, :], mv2[p][:, b, 0:1],
                                            rstd2[p][:, b:b + 1], ALU.subtract, ALU.mult)
            i.then_inc(s["x2_ready"], 1)
            ids = rows[p][:].bitcast(I32)[:, :, :, D + 1]
            tok = cst[0:S, bass.ds(_cols["token"][0] + g * GB, GB)]
            for k in range(TOPK):
                i = nc.vector.tensor_copy(ids[:, :, k], tok)
            i.then_inc(s["ids_ready"], 1)

        def dve_top(dve, g, p):
            dve.wait_ge(s["logits_done"], g + 1)
            if due(g - 1):
                dve.wait_ge(s["topi_ready"], g - 1)
            nc.vector.tensor_copy(lg[p][:], lg_ps).then_inc(s["lg_ready"], 1)
            held(dve)
            dve.wait_ge(s["lg_ready"], g + 1)
            for b in range(GB):
                i = nc.vector.max(top[p][:, b, :], lg[p][:, b, :])
            i.then_inc(s["top_ready"], 1)
            dve.wait_ge(s["top_ready"], g + 1)
            nc.vector.tensor_tensor(dlg[p][:], top[p][:, :, 1], top[p][:, :, 0], ALU.subtract
                                    ).then_inc(s["dlg_ready"], 1)
            for b in range(GB):
                i = nc.vector.max_index(topi[p][:, b, :], top[p][:, b, :], lg[p][:, b, :])
            i.then_inc(s["topi_ready"], 1)
            dve.wait_ge(s["topi_ready"], g + 1)
            nc.vector.tensor_copy(topf[p][:], topi[p][:, :, 0:TOPK]).then_inc(s["topf_ready"], 1)
            dve.wait_ge(s["topf_ready"], g + 1)
            for k in range(TOPK):
                ex = const("expert", S).unsqueeze(1).broadcast_to([S, GB, NE])
                nc.vector.tensor_tensor(oh[k][p][:], ex, topf[p][:, :, k:k + 1].broadcast_to([S, GB, NE]),
                                        ALU.is_equal).then_inc(s[f"oh{k + 1}_ready"], 1)
            dve.wait_ge(s["oh1_ready"], g + 1)
            dve.wait_ge(s["oh2_ready"], g + 1)
            if due(g - 1):
                dve.wait_ge(s["places_done"], g - 1)
            nc.vector.tensor_tensor(chosen[p][:], oh[0][p][:], oh[1][p][:], ALU.add
                                    ).then_inc(s["chosen_ready"], 1)
            dve.wait_ge(s["chosen_ready"], g + 1)
            for b in range(1, GB + 1):
                if b == 1:
                    i = nc.vector.tensor_copy(cum[p][:, 1, :], chosen[p][:, 0, :])
                else:
                    i = nc.vector.tensor_tensor(cum[p][:, b, :], cum[p][:, b - 1, :], chosen[p][:, b - 1, :],
                                                ALU.add)
                i.then_inc(s["cum_ready"] if b == GB else s["table"], 1)
                if b < GB:
                    dve.wait_ge(s["table"], g * (GB - 1) + b)

        def dve_gates(dve, g, p):
            dve.wait_ge(s["e2_ready"], g + 1)
            nc.vector.tensor_scalar(e21[p][:], e2[p][:], 1.0, None, ALU.add).then_inc(s["e21_ready"], 1)
            dve.wait_ge(s["e21_ready"], g + 1)
            nc.vector.reciprocal(rows[p][:, :, 0, D], e21[p][:]).then_inc(s["gate1_ready"], 1)
            dve.wait_ge(s["gate1_ready"], g + 1)
            nc.vector.tensor_tensor(rows[p][:, :, 1, D], e2[p][:], rows[p][:, :, 0, D], ALU.mult
                                    ).then_inc(s["gate2_ready"], 1)

        def dve_places(dve, g, p):
            q = 1 - p
            dve.wait_ge(s["places_done"], g + 1)
            nc.vector.tensor_tensor(place[p][:], place_ps[0:S, 0:GB, :],
                                    start_at[p][0:S].unsqueeze(1).broadcast_to([S, GB, NE]), ALU.add
                                    ).then_inc(s["place_ready"], 1)
            nc.vector.tensor_tensor(count[q][:], place_ps[:, GB, :], count[p][:], ALU.add
                                    ).then_inc(s["count_ready"], 1)
            dve.wait_ge(s["place_ready"], g + 1)
            for k in range(TOPK):
                i = nc.vector.tensor_tensor(placek[k][p][:], place[p][:], oh[k][p][:], ALU.mult)
            i.then_inc(s["placek_ready"], 1)
            dve.wait_ge(s["count_ready"], g + 1)
            nc.vector.tensor_tensor(start_at[q][:], count[q][:], const("region"), ALU.add
                                    ).then_inc(s["start_ready"], 1)
            dve.wait_ge(s["placek_ready"], g + 1)
            for k in range(TOPK):
                i = nc.vector.tensor_reduce(posf[p][:, :, k], placek[k][p][:], AX.X, ALU.add)
            i.then_inc(s["posf_ready"], 1)
            dve.wait_ge(s["posf_ready"], g + 1)
            if due(nth(g - 2, p, GB * TOPK)):
                dve.wait_ge(rows_sent[p], nth(g - 2, p, GB * TOPK))
            nc.vector.tensor_copy(pos[p][:].rearrange("p (b k) -> p b k", b=GB), posf[p][:]
                                  ).then_inc(s["pos_ready"], 1)

        def steps(engine_step, eng):
            n = NG
            engine_step(0, 0, None, None)
            engine_step(1, 1, 0, None)
            engine_step(0, 2, 1, 0)
            engine_step(1, 3, 2, 1)
            with eng.Fori(2, n // 2) as j:
                engine_step(0, j * 2, j * 2 - 1, j * 2 - 2)
                engine_step(1, j * 2 + 1, j * 2, j * 2 - 1)
            engine_step(0, None, n - 1, n - 2)
            engine_step(1, None, None, n - 1)

        block = ctx.enter_context(nc.Block())

        @block.sync
        def _(sp):
            sp.dma_start(cst[:], consts).then_inc(n_ld, 16)
            sp.dma_start(wc[:], wconv).then_inc(n_ld, 16)
            sp.dma_start(wa[:], wattn).then_inc(n_ld, 16)
            sp.dma_start(ba[:], battn).then_inc(n_ld, 16)
            sp.dma_start(wg[:], wgate).then_inc(n_ld, 16)

            def step(par, g1, g2_, g3):
                if g1 is not None:
                    sp_group(sp, g1, par)
                    if isinstance(g1, int) and g1 == 0:
                        for i in range(3):
                            sp.dma_start(wst[i][:], wraw[i]).then_inc(w_loaded[i], 16)
                if g2_ is not None:
                    sp_weights(sp, g2_)
                if g3 is not None:
                    sp_h2(sp, g3, par)

            steps(step, sp)
            for i in range(3):
                sp.wait_ge(w_stored[i], 16 * NE * NBLK // 3)
            sp.wait_ge(s["tables_ready"], 1)
            for p in range(2):
                sp.wait_ge(rows_sent[p], nth(NG - 2 + p, p, GB * TOPK))
            sp.wait_ge(s["pad_sent"], 16 * (NE + 1))

            def load_rows(t, p):
                if due(t - 1):
                    sp.wait_ge(s["xT_done"], t - 1)
                if due(t - 1):
                    sp.wait_ge(s["tags_ready"], t - 1)
                r = sp.value_load(tile_row[0:1, bass.ds(t, 1)], min_val=0, max_val=NE * REG)
                sp.dma_start(xr[p][:], routed[bass.ds(r, TS)]).then_inc(row_loaded[p], 16)

            def load_block(k, blk, new):
                src = w_scaled[bass.ds(blk + k, 1)].rearrange("o p c -> (o p) c")
                dst = wb[k][:].rearrange("p c o -> p (c o)")
                if new is None:
                    sp.dma_start(dst, src).then_inc(blk_loaded[k], 16)
                else:
                    sp.dma_start(dst, src, cond=(new > 0)).then_inc(blk_loaded[k], 16)

            def tile_info(t):
                return (sp.value_load(tile_blk[0:1, bass.ds(t, 1)], min_val=0, max_val=(NE - 1) * NBLK),
                        sp.value_load(tile_new[0:1, bass.ds(t, 1)], min_val=0, max_val=1))

            load_rows(0, 0)
            blk0 = sp.value_load(tile_blk[0:1, 0:1], min_val=0, max_val=(NE - 1) * NBLK)
            for k in range(NBLK):
                load_block(k, blk0, None)
            load_rows(1, 1)

            def tile(t, p, more=True):
                if more:
                    load_rows(t + 2, p)
                blk, new = tile_info(t + 1)
                for k in range(4):
                    sp.wait_ge(s["hidden_done"], 4 * t + k + 1)
                    load_block(k, blk, new)
                for k in range(4, NBLK):
                    sp.wait_ge(s["expert_out"], t + 1)
                    load_block(k, blk, new)

            with sp.Fori(0, NT // 2 - 1) as j:
                tile(j * 2, 0)
                tile(j * 2 + 1, 1)
            tile(NT - 2, 0, more=False)

            for k in range(NBLK):
                sp.wait_ge(blk_loaded[k], 16 * NT)
            for p in range(2):
                sp.wait_ge(h2_stored[p], nth(NG - 2 + p, p))

        @block.tensor
        def _(pe):
            pe.wait_ge(n_ld, 16 * NPARAM)

            def step(par, g1, g2_, g3):
                if g1 is not None:
                    pe_window(pe, g1, par)
                    pe_conv(pe, g1, par, 0)
                if g2_ is not None:
                    pe_xnT(pe, g2_, 1 - par)
                if g1 is not None:
                    pe_conv(pe, g1, par, 1)
                if g2_ is not None:
                    pe_qkv(pe, g2_, 1 - par)
                if g1 is not None:
                    pe_conv(pe, g1, par, 2)
                if g3 is not None:
                    pe_x2T(pe, g3, par)
                if g2_ is not None:
                    pe_scores(pe, g2_, 1 - par)
                if g3 is not None:
                    pe_logits(pe, g3, par)
                if g1 is not None:
                    pe_conv(pe, g1, par, 3)
                if g2_ is not None:
                    pe_mem(pe, g2_, 1 - par)
                    pe_o(pe, g2_, 1 - par)
                if g3 is not None:
                    pe_places(pe, g3, par)

            steps(step, pe)

            def turn_x(t, p):
                pe.wait_ge(row_loaded[p], nth(t, p))
                if due(t - 1):
                    pe.wait_ge(u_ready[0], t - 1)
                pe.transpose(xT_ps[p], xr[p][:, 0:D], const("ident")).then_inc(s["xT_done"], 1)

            def hidden(t, p):
                pe.wait_ge(feat_ready[0], t + 1)
                for k in range(4):
                    pe.wait_ge(blk_loaded[k], 16 * (t + 1))
                    if k % 2 == 0:
                        if due(t - 1):
                            pe.wait_ge(u_ready[1 + k // 2], t - 1)
                    for c in range(KC):
                        mm = pe.matmul(hid_ps[p][k // 2][:, k % 2, :], wb[k][:, c, :], feat[0][p][:, c, :],
                                       start=(c == 0), stop=(c == KC - 1))
                    mm.then_inc(s["hidden_done"], 1)

            def last_layer(t, p):
                if due(t - 1):
                    pe.wait_ge(s["ye_ready"], t - 1)
                for f in range(2):
                    pe.wait_ge(blk_loaded[4 + f], 16 * (t + 1))
                    pe.wait_ge(feat_ready[1 + f], t + 1)
                    for c in range(KC):
                        mm = pe.matmul(y_ps[p], feat[1 + f][p][:, c, :], wb[4 + f][:, c, :],
                                       start=(f == 0 and c == 0), stop=(f == 1 and c == KC - 1))
                mm.then_inc(s["expert_out"], 1)

            turn_x(0, 0)
            turn_x(1, 1)
            hidden(0, 0)

            def pair(t):
                turn_x(t + 2, 0)
                hidden(t + 1, 1)
                last_layer(t, 0)
                turn_x(t + 3, 1)
                hidden(t + 2, 0)
                last_layer(t + 1, 1)

            pair(0)
            with pe.Fori(1, NT // 2 - 1) as j:
                pair(j * 2)
            hidden(NT - 1, 1)
            last_layer(NT - 2, 0)
            last_layer(NT - 1, 1)

        @block.scalar
        def _(act):
            act.wait_ge(n_ld, 16 * NPARAM)

            def step(par, g1, g2_, g3):
                if g1 is not None:
                    act_square(act, g1, par)
                if g2_ is not None:
                    act_xnT(act, g2_, 1 - par)
                if g3 is not None:
                    act_x2T(act, g3, par)
                if g2_ is not None:
                    act_qk(act, g2_, 1 - par)
                if g3 is not None:
                    act_x2(act, g3, par)
                    act_e2(act, g3, par)
                if g1 is not None:
                    act_tanh(act, g1, par)
                if g2_ is not None:
                    act_memT(act, g2_, 1 - par)

            steps(step, act)

            def turn(t, p):
                act.wait_ge(s["xT_done"], t + 1)
                if due(t - 1):
                    act.wait_ge(feat_ready[0], t - 1)
                nc.scalar.activation(u[0][p][:], xT_ps[p], ACT.Copy, scale=0.5).then_inc(u_ready[0], 1)

            def features(c, t, p):
                act.wait_ge(u_ready[c], t + 1)
                if due(t):
                    act.wait_ge(r1_ready[c], t)
                if due(t):
                    act.wait_ge(m2_ready[c], t)
                for i in range(NB):
                    a = nc.scalar.activation(fa[c][:, i, :], u[c][p][:], ACT.Abs,
                                             scale=2.0 / H_GRID, bias=1.0 / H_GRID - (i - 1))
                a.then_inc(abs_ready[c], 1)
                act.wait_ge(abs_ready[c], t + 1)
                if due(t):
                    act.wait_ge(c1_ready[c], t)
                nc.scalar.activation(fr1[c][:], fa[c][:], ACT.Relu, scale=-1.0, bias=1.0
                                     ).then_inc(r1_ready[c], 1)
                if due(t):
                    act.wait_ge(feat_ready[c], t)
                nc.scalar.activation(th[c][:], u[c][p][:], ACT.Tanh).then_inc(th_ready[c], 1)
                act.wait_ge(r1_ready[c], t + 1)
                nc.scalar.activation(fs1[c][:], fr1[c][:], ACT.Square, scale=2.0).then_inc(s1_ready[c], 1)
                act.wait_ge(m2_ready[c], t + 1)
                nc.scalar.activation(fs2[c][:], fm2[c][:], ACT.Square).then_inc(s2_ready[c], 1)

            def half_hidden(t, p, i):
                act.wait_ge(s["hidden_done"], 4 * t + 2 * i + 2)
                if due(t):
                    act.wait_ge(u_ready[1 + i], t)
                nc.scalar.activation(g2[i][:], hid_ps[p][i][:, 1, :], ACT.Copy, scale=0.5
                                     ).then_inc(s["g2_ready"], 1)

            def gated(t, p):
                act.wait_ge(s["expert_out"], t + 1)
                act.wait_ge(s["tags_ready"], t + 1)
                if due(16 * (t - 1)):
                    act.wait_ge(s["out_added"], 16 * (t - 1))
                nc.scalar.activation(ye[p][:], y_ps[p], ACT.Copy, scale=gate[p][:]
                                     ).then_inc(s["ye_ready"], 1)

            turn(0, 0)
            features(0, 0, 0)

            def tile(t, p, last=False, before=True):
                if not last:
                    turn(t + 1, 1 - p)
                    features(0, t + 1, 1 - p)
                half_hidden(t, p, 0)
                features(1, t, p)
                if before:
                    gated(t - 1, 1 - p)
                half_hidden(t, p, 1)
                features(2, t, p)

            tile(0, 0, before=False)
            tile(1, 1)
            tile(2, 0)
            with act.Fori(1, NT // 2 - 1) as j:
                tile(j * 2 + 1, 1)
                tile(j * 2 + 2, 0)
            tile(NT - 1, 1, last=True)
            gated(NT - 1, 1)

        @block.gpsimd
        def _(pool):
            pool.wait_ge(n_ld, 16 * NPARAM)

            def step(par, g1, g2_, g3):
                if g1 is not None:
                    pool_sq(pool, g1, par)
                    pool_wnorm(pool, g1, par)
                if g3 is not None:
                    pool_rstd2(pool, g3, par)
                if g1 is not None:
                    pool_bias(pool, g1, par)
                    pool_hb(pool, g1, par)
                    pool_rstd1(pool, g1, par)
                if g3 is not None:
                    pool_rows(pool, g3, par)

            steps(step, pool)
            pool.wait_ge(s["table"], NG * (GB - 1) + 2)
            for e in range(NE):
                pool.indirect_dma_start(routed, bass.IndirectOffsetOnAxis(padi[:, e:e + 1], 0),
                                        padrow[:], None).then_inc(s["pad_sent"], 16)
            pool.dma_start(routed[NE * REG:NE * REG + TS], padrow[:]).then_inc(s["pad_sent"], 16)
            pool.dma_start(out[TOK:TOK + TS], padrow[:, 0:D]).then_inc(s["dump_zeroed"], 16)
            pool.wait_ge(s["dump_zeroed"], 16)
            for p in range(2):
                pool.wait_ge(h2_stored[p], nth(NG - 2 + p, p))

            def add(t, p):
                pool.wait_ge(s["ye_ready"], t + 1)
                if due(16 * t):
                    pool.wait_ge(s["out_added"], 16 * t)
                pool.sem_inc(s["pool_goes_on"], 1)
                pool.indirect_dma_start(out, bass.IndirectOffsetOnAxis(
                    number[p][:], 0), ye[p][:], None, compute_op=ALU.add
                ).then_inc(s["out_added"], 16)

            def tags(t, p):
                pool.wait_ge(row_loaded[p], nth(t, p))
                if due(t - 1):
                    pool.wait_ge(s["ye_ready"], t - 1)
                if due(16 * (t - 1)):
                    pool.wait_ge(s["out_added"], 16 * (t - 1))
                pool.sem_inc(s["pool_goes_on"], 1)
                pool.tensor_copy(gate[p][:], xr[p][:, D:D + 1])
                pool.tensor_copy(number[p][:], xr[p][:, D + 1:D + 2].bitcast(I32)).then_inc(s["tags_ready"], 1)

            tags(0, 0)
            tags(1, 1)
            add(0, 0)
            tags(2, 0)
            add(1, 1)
            tags(3, 1)
            with pool.Fori(1, NT // 2 - 1) as j:
                add(j * 2, 0)
                tags(j * 2 + 2, 0)
                add(j * 2 + 1, 1)
                tags(j * 2 + 3, 1)
            add(NT - 2, 0)
            add(NT - 1, 1)
            pool.wait_ge(s["out_added"], 16 * NT)

        @block.vector
        def _(dve):
            dve.wait_ge(n_ld, 16 * NPARAM)
            for p in range(2):
                nc.vector.memset(cum[p][:, 0, :], 0.0).then_inc(s["setup"], 1)
            nc.vector.memset(count[0][:], 0.0).then_inc(s["setup"], 1)
            nc.vector.tensor_copy(start_at[0][:], const("region")).then_inc(s["setup"], 1)
            nc.vector.memset(padrow[:, 0:D + 1], 0.0).then_inc(s["setup"], 1)
            nc.vector.tensor_copy(padrow[:].bitcast(I32)[:, D + 1:D + 2], const("dump")).then_inc(s["setup"], 1)
            nc.vector.memset(expert9[:, NE:NE + 1], float(NE)).then_inc(s["setup"], 1)
            nc.vector.tensor_copy(expert9[:, 0:NE], const("expert", 1)).then_inc(s["setup"], 1)
            nc.vector.memset(base[:, NE:NE + 1], 0.0).then_inc(s["setup"], 1)
            dve.wait_ge(s["setup"], 9)

            def step(par, g1, g2_, g3):
                if g1 is not None:
                    dve_wsq(dve, g1, par)
                if g3 is not None:
                    dve_x2(dve, g3, par)
                if g1 is not None:
                    dve_wscale(dve, g1, par)
                if g2_ is not None:
                    dve_v(dve, g2_, 1 - par)
                if g3 is not None:
                    dve_top(dve, g3, par)
                if g2_ is not None:
                    dve_am(dve, g2_, 1 - par)
                if g3 is not None:
                    dve_gates(dve, g3, par)
                if g1 is not None:
                    dve_h(dve, g1, par)
                if g3 is not None:
                    dve_places(dve, g3, par)
                if g2_ is not None:
                    dve_weights(dve, g2_)
                    dve_h2(dve, g2_, 1 - par)
                if g1 is not None:
                    dve_xn(dve, g1, par)

            steps(step, dve)

            done = [NG * (GB - 1)]

            def link(i):
                i.then_inc(s["table"], 1)
                done[0] += 1
                dve.wait_ge(s["table"], done[0])

            tot = count[0]
            link(nc.vector.tensor_tensor(padf[:], const("padrow"), tot[:], ALU.add))
            link(nc.vector.tensor_copy(padi[:], padf[:]))
            link(nc.vector.tensor_scalar(cnt_i[:], tot[:], float(TS - 1), None, ALU.add))
            link(nc.vector.tensor_scalar(nt_i[:], cnt_i[:], TS.bit_length() - 1, None, ALU.logical_shift_right))
            link(nc.vector.tensor_copy(nt_f[:], nt_i[:]))
            link(nc.vector.tensor_copy(end_a[:], nt_f[:]))
            a, b = end_a, end_b
            for d in (1, 2, 4):
                link(nc.vector.tensor_copy(b[:, 0:d], a[:, 0:d]))
                link(nc.vector.tensor_tensor(b[:, d:NE], a[:, d:NE], a[:, 0:NE - d], ALU.add))
                a, b = b, a
            end = a
            link(nc.vector.tensor_tensor(first[:], end[:], nt_f[:], ALU.subtract))
            link(nc.vector.scalar_tensor_tensor(base[:, 0:NE], first[:], -float(TS), const("region"),
                                                ALU.mult, ALU.add))
            tiles = const("tile", 1)
            n1 = NT + 1
            link(nc.vector.tensor_tensor(past[:], tiles.unsqueeze(2).broadcast_to([1, n1, NE]),
                                         end[0:1].unsqueeze(1).broadcast_to([1, n1, NE]), ALU.is_ge))
            link(nc.vector.tensor_reduce(past_n[:], past[:], AX.X, ALU.add))
            link(nc.vector.tensor_tensor(is_e[:], expert9[:].unsqueeze(1).broadcast_to([1, n1, NE + 1]),
                                         past_n[:].unsqueeze(2).broadcast_to([1, n1, NE + 1]), ALU.is_equal))
            link(nc.vector.tensor_tensor(rs_e[:], is_e[:], base[0:1].unsqueeze(1).broadcast_to([1, n1, NE + 1]),
                                         ALU.mult))
            link(nc.vector.scalar_tensor_tensor(rs_e[:, :, NE], tiles, -float(TS), is_e[:, :, NE],
                                                ALU.mult, ALU.mult))
            link(nc.vector.scalar_tensor_tensor(rs_e[:, :, NE], is_e[:, :, NE], float(NE * REG),
                                                rs_e[:, :, NE], ALU.mult, ALU.add))
            link(nc.vector.tensor_reduce(rs_f[:], rs_e[:], AX.X, ALU.add))
            link(nc.vector.scalar_tensor_tensor(rs_f[:], tiles, float(TS), rs_f[:], ALU.mult, ALU.add))
            link(nc.vector.tensor_copy(tile_row[:], rs_f[:]))
            link(nc.vector.tensor_scalar(eidx[:], past_n[:], float(NE - 1), float(NBLK), ALU.min, ALU.mult))
            link(nc.vector.tensor_copy(tile_blk[:], eidx[:]))
            link(nc.vector.memset(tile_new[:, 0:1], 1))
            nc.vector.tensor_tensor(tile_new[:, 1:n1], eidx[:, 1:n1], eidx[:, 0:n1 - 1], ALU.not_equal
                                    ).then_inc(s["tables_ready"], 1)

            def cut(c, t):
                dve.wait_ge(abs_ready[c], t + 1)
                if due(t):
                    dve.wait_ge(c2_ready[c], t)
                if due(t):
                    dve.wait_ge(s2_ready[c], t)
                nc.vector.tensor_scalar(fm2[c][:], fa[c][:], 2.0, 2.0, ALU.min, ALU.subtract
                                        ).then_inc(m2_ready[c], 1)

            def features(c, t, p):
                cut(c, t)
                dve.wait_ge(th_ready[c], t + 1)
                if c == 0 and due(t - 1):
                    dve.wait_ge(s["hidden_done"], 4 * (t - 1))
                elif due(t - 1):
                    dve.wait_ge(s["expert_out"], t - 1)
                nc.vector.scalar_tensor_tensor(feat[c][p][:, NB, :], th[c][:], 1.0, u[c][p][:],
                                               ALU.add, ALU.mult)
                dve.wait_ge(s1_ready[c], t + 1)
                nc.vector.tensor_tensor(fs1[c][:], fs1[c][:], fr1[c][:], ALU.mult).then_inc(c1_ready[c], 1)
                dve.wait_ge(s2_ready[c], t + 1)
                nc.vector.tensor_tensor(fs2[c][:], fs2[c][:], fm2[c][:], ALU.mult).then_inc(c2_ready[c], 1)
                dve.wait_ge(c1_ready[c], t + 1)
                dve.wait_ge(c2_ready[c], t + 1)
                nc.vector.tensor_tensor(feat[c][p][:, 0:NB, :], fs1[c][:], fs2[c][:], ALU.add
                                        ).then_inc(feat_ready[c], 1)

            def product(t, p, i):
                dve.wait_ge(s["g2_ready"], 2 * t + i + 1)
                if due(t - 1):
                    dve.wait_ge(feat_ready[1 + i], t - 1)
                if due(t - 1):
                    dve.wait_ge(th_ready[1 + i], t - 1)
                nc.vector.tensor_tensor(u[1 + i][p][:], hid_ps[p][i][:, 0, :], g2[i][:], ALU.mult
                                        ).then_inc(u_ready[1 + i], 1)

            features(0, 0, 0)

            def tile(t, p, last=False):
                if not last:
                    features(0, t + 1, 1 - p)
                product(t, p, 0)
                features(1, t, p)
                product(t, p, 1)
                features(2, t, p)

            tile(0, 0)
            tile(1, 1)
            tile(2, 0)
            with dve.Fori(1, NT // 2 - 1) as j:
                tile(j * 2 + 1, 1)
                tile(j * 2 + 2, 0)
            tile(NT - 1, 1, last=True)


def kernel(x, L0_tok_kernel, L0_tok_bias, L0_attn_Wk, L0_attn_bk, L0_attn_Wv, L0_attn_bv, L0_attn_Wq, L0_attn_bq,
           L0_attn_Wo, L0_attn_bo, L0_ffn_gate_w, L0_ffn_base_w1, L0_ffn_spline_w1, L0_ffn_scaler_w1,
           L0_ffn_base_w2, L0_ffn_spline_w2, L0_ffn_scaler_w2, L0_ffn_base_w3, L0_ffn_spline_w3,
           L0_ffn_scaler_w3):
    import concourse.bacc as bacc
    from concourse.bass_utils import run_bass_kernel_spmd

    xt = np.asarray(x).transpose(2, 0, 1).reshape(C, B * L)
    x2 = np.zeros((2 * C, B * L), xt.dtype)
    x2[:C] = xt
    x2[C:, :-1] = xt[:, 1:]
    taps = np.zeros((2 * TAPS2, C, D), xt.dtype)
    taps[:K] = np.asarray(L0_tok_kernel)
    wconv = taps.reshape(TAPS2, 2 * C, D).transpose(1, 0, 2).reshape(2 * C, TAPS2 * D)
    wattn = np.concatenate([np.asarray(w) for w in (L0_attn_Wk, L0_attn_Wv, L0_attn_Wq, L0_attn_Wo)], axis=1)
    battn = np.stack([np.asarray(L0_attn_bk), np.asarray(L0_attn_bq)], axis=1)
    wgate = np.asarray(L0_ffn_gate_w).T
    consts = constants()
    for name, bias in (("b_tok", L0_tok_bias), ("b_v", L0_attn_bv), ("b_o", L0_attn_bo)):
        consts[:, _cols[name][0]:_cols[name][1]] = np.asarray(bias)[None, :]

    def blocks(w1, w2, w3, tail):
        def first(w, half):
            return w[:, half * D:(half + 1) * D]

        parts = [first(w1, 0), first(w2, 0), first(w1, 1), first(w2, 1), w3[:, :, :D], w3[:, :, D:]]
        a = np.stack([p.reshape(NE, D, D, tail).transpose(0, 2, 3, 1) for p in parts], axis=1)
        return a.reshape(NE * NBLK, D, tail * D)

    wraw = np.concatenate([
        blocks(*(np.asarray(w) for w in (L0_ffn_spline_w1, L0_ffn_spline_w2, L0_ffn_spline_w3)), NB),
        blocks(*(np.asarray(w) for w in (L0_ffn_base_w1, L0_ffn_base_w2, L0_ffn_base_w3)), 1),
        blocks(*(np.asarray(w) for w in (L0_ffn_scaler_w1, L0_ffn_scaler_w2, L0_ffn_scaler_w3)), 1),
    ], axis=2)

    nc = bacc.Bacc("TRN2", target_bir_lowering=False, num_devices=1)
    arrays, args = {}, []
    for name, a in (("x2", x2), ("wconv", wconv), ("wattn", wattn), ("battn", battn), ("wgate", wgate),
                    ("wraw", wraw), ("consts", consts)):
        arrays[name] = np.ascontiguousarray(a)
        args.append(nc.dram_tensor(name, a.shape, mybir.dt.from_np(arrays[name].dtype), kind="ExternalInput").ap())
    out = nc.dram_tensor("out_0", (TOK + TS, D), F32, kind="ExternalOutput").ap()
    audio_tower(nc, *args, out)
    r = run_bass_kernel_spmd(nc, [arrays], core_ids=[0])
    return r.results[0]["out_0"][:TOK].reshape(B, S, D)
```

```python
from contextlib import ExitStack

import numpy as np
import concourse.bass as bass
from concourse import mybir
from concourse.alu_op_type import AluOpType as ALU

ACT = mybir.ActivationFunctionType
AX = mybir.AxisListType
F32 = mybir.dt.float32
I32 = mybir.dt.int32
U32 = mybir.dt.uint32

B, L, C = 32, 125, 64
K, D = 9, 128
S = L - K + 1
TOK = B * S
NE, TOPK, FF = 8, 2, 256
NB = 8
KC = NB + 1
NBLK = 6
BLK = KC * D
RAW = BLK + D
GB = 4
NG = B // GB
GT = GB * S
TAPS2 = (K + 1) // 2
TS = 128
NT = (TOK * TOPK + NE * (TS - 1)) // TS
REG = TOK + TS
RW = D + 2
WPG = NE * NBLK // NG
EPS_LN = 1e-5
EPS_TOK = 1e-7
LAM_HALF = 1.0 / (1.0 + EPS_TOK)
H_GRID = 2.0 / 5
ROOT3 = 3.0 ** 0.5
assert NT % 2 == 0 and NG % 2 == 0 and WPG == NBLK

_cols = {}
_at = 0
for _name, _n in (("ident", D), ("decay", S), ("before", S), ("ones", D), ("expert", NE), ("padrow", NE),
                  ("dump", 1), ("token", B), ("tile", NT + 1), ("half", GB), ("minushalf", GB),
                  ("b_tok", D), ("b_v", D), ("b_o", D), ("region", NE)):
    _cols[_name] = (_at, _at + _n)
    _at += _n
NCONST = _at


def constants():
    c = np.zeros((D, NCONST), np.float32)

    def put(name, a):
        c[:a.shape[0], _cols[name][0]:_cols[name][1]] = a

    put("ident", np.eye(D))
    s, t = np.arange(S)[:, None], np.arange(S)[None, :]
    put("decay", np.where(t > s, 0.1 * 0.9 ** np.maximum(t - 1 - s, 0), 0.0))
    put("before", (s < t).astype(np.float32))
    put("ones", np.ones((D, D)))
    put("expert", np.tile(np.arange(NE), (D, 1)))
    put("padrow", np.arange(NE)[None, :] * REG + np.arange(D)[:, None])
    put("dump", TOK + np.arange(D)[:, None])
    put("token", np.arange(B)[None, :] * S + np.arange(D)[:, None])
    put("tile", np.tile(np.arange(NT + 1), (D, 1)))
    put("half", np.full((D, GB), 0.5))
    put("minushalf", np.full((D, GB), -0.5))
    put("region", np.tile(np.arange(NE) * REG, (D, 1)))
    return c


def audio_tower(nc, x2, wconv, wattn, battn, wgate, wraw, consts, out):
    with ExitStack() as ctx:
        groups_memory = ExitStack()
        held_by = [ctx]

        def sb(name, shape, dt=F32):
            return held_by[0].enter_context(nc.sbuf_tensor(name, shape, dt))

        def ps(name, shape):
            return ctx.enter_context(nc.psum_tensor(name, shape, F32))

        def sem(name):
            return ctx.enter_context(nc.semaphore(name))

        w_scaled = nc.dram_tensor("w_scaled", (NE * NBLK, D, BLK), F32).ap()
        routed = nc.dram_tensor("routed", (NE * REG + TS, RW), F32).ap()

        cst = sb("cst", [D, NCONST])

        def const(name, rows=D):
            return cst[0:rows, _cols[name][0]:_cols[name][1]]

        wc = sb("wc", [D, TAPS2 * D])
        wa = sb("wa", [D, 4 * D])
        ba = sb("ba", [D, 2])
        wg = sb("wg", [D, NE])

        count = [sb(f"count{p}", [D, NE]) for p in range(2)]
        padrow = sb("padrow", [D, RW])
        padf = sb("padf", [D, NE])
        padi = sb("padi", [D, NE], I32)
        cnt_i = sb("cnt_i", [D, NE], I32)
        nt_i = sb("nt_i", [D, NE], I32)
        nt_f = sb("nt_f", [D, NE])
        end_a = sb("end_a", [D, NE])
        end_b = sb("end_b", [D, NE])
        first = sb("first", [D, NE])
        base = sb("base", [D, NE + 1])
        past = sb("past", [1, NT + 1, NE])
        past_n = sb("past_n", [1, NT + 1])
        is_e = sb("is_e", [1, NT + 1, NE + 1])
        rs_e = sb("rs_e", [1, NT + 1, NE + 1])
        rs_f = sb("rs_f", [1, NT + 1])
        eidx = sb("eidx", [1, NT + 1])
        expert9 = sb("expert9", [1, NE + 1])
        tile_row = sb("tile_row", [1, NT + 1], I32)
        tile_blk = sb("tile_blk", [1, NT + 1], I32)
        tile_new = sb("tile_new", [1, NT + 1], I32)
        held_by[0] = groups_memory
        xs = [sb(f"xs{p}", [D, GB * L]) for p in range(2)]
        xq = [sb(f"xq{p}", [D, GB * L]) for p in range(2)]
        xq2 = [sb(f"xq2{p}", [D, GB * L]) for p in range(2)]
        xq4 = [sb(f"xq4{p}", [D, GB * L]) for p in range(2)]
        wsq = [sb(f"wsq{p}", [S, GB]) for p in range(2)]
        wnorm = [sb(f"wnorm{p}", [S, GB]) for p in range(2)]
        wnorm_e = [sb(f"wnorm_e{p}", [S, GB]) for p in range(2)]
        winv = [sb(f"winv{p}", [S, GB]) for p in range(2)]
        wscale = [sb(f"wscale{p}", [S, GB]) for p in range(2)]
        y = [sb(f"y{p}", [S, GB, D]) for p in range(2)]
        h = [sb(f"h{p}", [S, GB, D]) for p in range(2)]
        hb = [sb(f"hb{p}", [S, GB, D]) for p in range(2)]
        st1 = [sb(f"st1{p}", [S, GB, 6]) for p in range(2)]
        mv1 = [sb(f"mv1{p}", [S, GB, 2]) for p in range(2)]
        ve1 = [sb(f"ve1{p}", [S, GB]) for p in range(2)]
        rstd1 = [sb(f"rstd1{p}", [S, GB]) for p in range(2)]
        xn = [sb(f"xn{p}", [S, GB, D]) for p in range(2)]
        xnT = [sb(f"xnT{p}", [D, GT]) for p in range(2)]
        qT = [sb(f"qT{p}", [D, GT]) for p in range(2)]
        kT = [sb(f"kT{p}", [D, GT]) for p in range(2)]
        v = [sb(f"v{p}", [S, GB, D]) for p in range(2)]
        am = [sb(f"am{p}", [S, GB, S]) for p in range(2)]
        memT = [sb(f"memT{p}", [D, GT]) for p in range(2)]
        h2 = [sb(f"h2{p}", [S, GB, D]) for p in range(2)]
        st2 = [sb(f"st2{p}", [S, GB, 6]) for p in range(2)]
        mv2 = [sb(f"mv2{p}", [S, GB, 2]) for p in range(2)]
        ve2 = [sb(f"ve2{p}", [S, GB]) for p in range(2)]
        rstd2 = [sb(f"rstd2{p}", [S, GB]) for p in range(2)]
        rows = [sb(f"rows{p}", [S, GB, TOPK, RW]) for p in range(2)]
        x2T = [sb(f"x2T{p}", [D, GT]) for p in range(2)]
        lg = [sb(f"lg{p}", [S, GB, NE]) for p in range(2)]
        top = [sb(f"top{p}", [S, GB, 8]) for p in range(2)]
        topi = [sb(f"topi{p}", [S, GB, 8], U32) for p in range(2)]
        topf = [sb(f"topf{p}", [S, GB, TOPK]) for p in range(2)]
        dlg = [sb(f"dlg{p}", [S, GB]) for p in range(2)]
        e2 = [sb(f"e2{p}", [S, GB]) for p in range(2)]
        e21 = [sb(f"e21{p}", [S, GB]) for p in range(2)]
        oh = [[sb(f"oh{k}{p}", [S, GB, NE]) for p in range(2)] for k in range(TOPK)]
        chosen = [sb(f"chosen{p}", [S, GB, NE]) for p in range(2)]
        cum = [sb(f"cum{p}", [S, GB + 1, NE]) for p in range(2)]
        place = [sb(f"place{p}", [S, GB, NE]) for p in range(2)]
        placek = [[sb(f"placek{k}{p}", [S, GB, NE]) for p in range(2)] for k in range(TOPK)]
        posf = [sb(f"posf{p}", [S, GB, TOPK]) for p in range(2)]
        pos = [sb(f"pos{p}", [S, GB * TOPK], I32) for p in range(2)]
        start_at = [sb(f"start_at{p}", [D, NE]) for p in range(2)]

        wst = [sb(f"wst{i}", [D, RAW]) for i in range(3)]

        groups_memory.close()
        held_by[0] = ctx
        wb = [sb(f"wb{k}", [D, KC, D]) for k in range(NBLK)]
        xr = [sb(f"xr{p}", [TS, D]) for p in range(2)]
        tag = [sb(f"tag{p}", [TS, 2]) for p in range(2)]
        u_in = [sb(f"u_in{p}", [D, TS]) for p in range(2)]
        th_in = sb("th_in", [D, TS])
        feat_in = [sb(f"feat_in{p}", [D, KC, TS]) for p in range(2)]
        dist_in = sb("dist_in", [D, NB, TS])
        z_in = sb("z_in", [D, NB, TS])
        a2_in = sb("a2_in", [D, NB, TS])
        z2_in = sb("z2_in", [D, NB, TS])
        u_mid = sb("u_mid", [D, 2, TS])
        th_mid = sb("th_mid", [D, 2, TS])
        feat_mid = [sb(f"feat_mid{p}", [D, KC, 2, TS]) for p in range(2)]
        dist_mid = sb("dist_mid", [D, NB, 2, TS])
        m_mid = sb("m_mid", [D, NB, 2, TS])
        a2_mid = sb("a2_mid", [D, NB, 2, TS])
        z2_mid = sb("z2_mid", [D, NB, 2, TS])
        g2 = sb("g2", [D, 2, TS])
        ye = [sb(f"ye{p}", [TS, D]) for p in range(2)]

        bank = [ps(f"bank{i}", [D, 512]) for i in range(8)]

        def tokens(b, n):
            return b[0:S, 0:GB * n].rearrange("p (b n) -> p b n", b=GB)

        conv_ps = [tokens(bank[p], D) for p in range(2)]
        xnT_ps = bank[2][:, 0:GT]
        at_ps = tokens(bank[2], S)
        qT_ps = bank[3][:, 0:GT]
        memT_ps = bank[3][:, 0:GT]
        kT_ps = bank[4][:, 0:GT]
        o_ps = tokens(bank[4], D)
        v_ps = tokens(bank[5], D)
        x2T_ps = bank[6][:, 0:GT]
        wsq_ps = bank[7][0:S, 0:GB]
        lg_ps = bank[6][0:S, 0:GB * NE].rearrange("p (b n) -> p b n", b=GB)
        place_ps = bank[6][:, 64:64 + (GB + 1) * NE].rearrange("p (b n) -> p b n", b=GB + 1)
        hid_ps = [[bank[2 * p + i][:, 0:2 * TS].rearrange("p (k n) -> p k n", k=2) for i in range(2)]
                  for p in range(2)]
        y_ps = [bank[4 + p][:, 0:D] for p in range(2)]
        xT_ps = [bank[6 + p][:, 0:TS] for p in range(2)]

        n_ld = sem("params_loaded")
        s = {n: sem(n) for n in (
            "x_squared", "sq_pairs", "sq_quads", "window_sums", "wsq_ready", "wnorm_ready",
            "wnorm_eps", "winv_ready", "wscale_ready", "conv_done", "tanh_done", "y_biased", "h_ready",
            "hb_ready", "stats1", "aggr1", "var1", "rstd1_ready", "xn_ready", "xnT_done", "xnT_ready",
            "qkv_done", "qT_ready", "kT_ready", "v_ready", "scores_done", "am_ready", "mem_done",
            "memT_ready", "o_done", "h2_ready", "stats2", "aggr2", "var2", "rstd2_ready",
            "x2_ready", "x2_copied", "ids_ready", "x2T_done", "x2T_ready", "logits_done", "lg_ready",
            "top_ready", "topi_ready", "topf_ready", "dlg_ready", "e2_ready", "e21_ready", "gate1_ready",
            "gate2_ready", "oh1_ready", "oh2_ready", "chosen_ready", "cum_ready", "places_done",
            "place_ready", "placek_ready", "posf_ready", "pos_ready", "count_ready", "start_ready",
            "w_scaled_up", "setup", "table", "tables_ready",
            "pad_sent", "dump_zeroed",
            "xT_done", "hidden_done", "g2_ready", "u_in_ready", "dist_in_ready", "z_in_ready", "th_in_ready",
            "a2_in_ready", "z2_in_ready", "x_in_ready", "y_in_ready", "silu_in_ready", "feat_in_ready",
            "u_mid_ready", "dist_mid_ready", "m_mid_ready", "th_mid_ready", "a2_mid_ready", "z2_mid_ready",
            "x_mid_ready", "y_mid_ready", "silu_mid_ready", "feat_mid_ready", "half_used", "ye_ready", "out_added", "pool_goes_on")}
        x_loaded = [sem(f"x_loaded{p}") for p in range(2)]
        h2_stored = [sem(f"h2_stored{p}") for p in range(2)]
        rows_sent = [sem(f"rows_sent{p}") for p in range(2)]
        row_loaded = [sem(f"row_loaded{p}") for p in range(2)]
        tag_loaded = [sem(f"tag_loaded{p}") for p in range(2)]
        w_loaded = [sem(f"w_loaded{i}") for i in range(3)]
        w_stored = [sem(f"w_stored{i}") for i in range(3)]
        blk_loaded = [sem(f"blk_loaded{k}") for k in range(NBLK)]
        def due(n):
            return not isinstance(n, int) or n > 0

        def nth(n, p, each=1):
            return 8 * each * (n - p + 2)

        NPARAM = 5

        def held(eng):
            eng.wait_ge(n_ld, 16 * NPARAM)

        def sp_group(sp, g, p):
            if due(g - 1):
                sp.wait_ge(s["conv_done"], g - 1)
            if due(g - 1):
                sp.wait_ge(s["x_squared"], g - 1)
            sp.dma_start(xs[p][:], x2[:, bass.ds(g * GB * L, GB * L)]).then_inc(x_loaded[p], 16)

        def sp_weights(sp, g):
            for i in range(WPG):
                n = g * WPG + i
                sp.wait_ge(s["w_scaled_up"], n + 1)
                sp.dma_start(w_scaled[bass.ds(n, 1)].rearrange("o p c -> (o p) c"),
                             wst[i % 3][:, 0:BLK]).then_inc(w_stored[i % 3], 16)
                if isinstance(g, int) and not 3 <= n + 2 < NE * NBLK:
                    continue
                q = (i - 1) % 3
                if due(16 * (g * (WPG // 3) + (i + 2) // 3)):
                    sp.wait_ge(w_stored[q], 16 * (g * (WPG // 3) + (i + 2) // 3))
                sp.dma_start(wst[q][:], wraw[bass.ds(n + 2, 1)].rearrange("o p c -> (o p) c")
                             ).then_inc(w_loaded[q], 16)

        def sp_h2(sp, g, p):
            sp.wait_ge(s["h2_ready"], g + 1)
            sp.dma_start(out[bass.ds(g * GT, GT)].rearrange("(b t) d -> t b d", b=GB), h2[p][:]
                         ).then_inc(h2_stored[p], 16)

        def dve_weights(dve, g):
            for i in range(WPG):
                n = g * WPG + i
                dve.wait_ge(w_loaded[i % 3], 16 * (g * (WPG // 3) + i // 3 + 1))
                w3 = wst[i % 3][:, 0:NB * D].rearrange("p (c o) -> p c o", c=NB)
                scaler = wst[i % 3][:, BLK:RAW].unsqueeze(1).broadcast_to([D, NB, D])
                nc.vector.scalar_tensor_tensor(w3, w3, 1.0 / 6.0 if i < 4 else -1.0 / 6.0, scaler, ALU.mult, ALU.mult
                                               ).then_inc(s["w_scaled_up"], 1)

        def pe_window(pe, g, p):
            pe.wait_ge(s["sq_quads"], g + 1)
            if due(g):
                pe.wait_ge(s["wsq_ready"], g)
            for b in range(GB):
                pe.matmul(wsq_ps[:, b:b + 1], xq4[p][:, b * L:b * L + S], const("ones")[:, 0:1],
                          start=True, stop=False)
                mm = pe.matmul(wsq_ps[:, b:b + 1], xq[p][0:C, b * L + K - 1:b * L + K - 1 + S],
                               const("ones")[0:C, 0:1], start=False, stop=True)
            mm.then_inc(s["window_sums"], 1)

        def pe_conv(pe, g, p, b):
            if b == 0:
                pe.wait_ge(x_loaded[p], nth(g, p))
                if due(g - 1):
                    pe.wait_ge(s["tanh_done"], g - 1)
            for j in range(TAPS2):
                n = D if j < TAPS2 - 1 else C
                mm = pe.matmul(conv_ps[p][:, b, :], xs[p][0:n, b * L + 2 * j:b * L + 2 * j + S],
                               wc[0:n, j * D:(j + 1) * D], start=(j == 0), stop=(j == TAPS2 - 1))
            if b == GB - 1:
                mm.then_inc(s["conv_done"], 1)

        def pe_xnT(pe, g, p):
            pe.wait_ge(s["xn_ready"], g + 1)
            if due(g):
                pe.wait_ge(s["am_ready"], g)
            for b in range(GB):
                mm = pe.transpose(xnT_ps[:, b * S:(b + 1) * S], xn[p][:, b, :], const("ident", S)[:, 0:S])
            mm.then_inc(s["xnT_done"], 1)

        def pe_qkv(pe, g, p):
            pe.wait_ge(s["xnT_ready"], g + 1)
            if due(g):
                pe.wait_ge(s["memT_ready"], g)
            pe.matmul(qT_ps, wa[:, 2 * D:3 * D], xnT[p][:], start=True, stop=True)
            if due(g):
                pe.wait_ge(s["h2_ready"], g)
            pe.matmul(kT_ps, wa[:, 0:D], xnT[p][:], start=True, stop=True)
            if due(g):
                pe.wait_ge(s["v_ready"], g)
            for b in range(GB):
                mm = pe.matmul(v_ps[:, b, :], xnT[p][:, b * S:(b + 1) * S], wa[:, D:2 * D],
                               start=True, stop=True)
            mm.then_inc(s["qkv_done"], 1)

        def pe_scores(pe, g, p):
            pe.wait_ge(s["qT_ready"], g + 1)
            pe.wait_ge(s["kT_ready"], g + 1)
            for b in range(GB):
                mm = pe.matmul(at_ps[:, b, :], kT[p][:, b * S:(b + 1) * S], qT[p][:, b * S:(b + 1) * S],
                               start=True, stop=True)
            mm.then_inc(s["scores_done"], 1)

        def pe_mem(pe, g, p):
            pe.wait_ge(s["am_ready"], g + 1)
            pe.wait_ge(s["v_ready"], g + 1)
            for b in range(GB):
                mm = pe.matmul(memT_ps[:, b * S:(b + 1) * S], v[p][:, b, :], am[p][:, b, :],
                               start=True, stop=True)
            mm.then_inc(s["mem_done"], 1)

        def pe_o(pe, g, p):
            pe.wait_ge(s["memT_ready"], g + 1)
            for b in range(GB):
                mm = pe.matmul(o_ps[:, b, :], memT[p][:, b * S:(b + 1) * S], wa[:, 3 * D:4 * D],
                               start=True, stop=True)
            mm.then_inc(s["o_done"], 1)

        def pe_x2T(pe, g, p):
            pe.wait_ge(s["x2_ready"], g + 1)
            if due(g):
                pe.wait_ge(s["place_ready"], g)
            if due(g):
                pe.wait_ge(s["count_ready"], g)
            for b in range(GB):
                mm = pe.transpose(x2T_ps[:, b * S:(b + 1) * S], rows[p][:, b, 0, 0:D],
                                  const("ident", S)[:, 0:S])
            mm.then_inc(s["x2T_done"], 1)

        def pe_logits(pe, g, p):
            pe.wait_ge(s["x2T_ready"], g + 1)
            for b in range(GB):
                mm = pe.matmul(lg_ps[:, b, :], x2T[p][:, b * S:(b + 1) * S], wg[:], start=True, stop=True)
            mm.then_inc(s["logits_done"], 1)

        def pe_places(pe, g, p):
            pe.wait_ge(s["cum_ready"], g + 1)
            pe.matmul(place_ps[:], const("ones", S), cum[p][:], start=True, stop=True)
            pe.matmul(place_ps[0:S, 0:GB, :], const("before", S), chosen[p][:], start=False, stop=True,
                      skip_group_check=True).then_inc(s["places_done"], 1)

        def act_square(act, g, p):
            act.wait_ge(x_loaded[p], nth(g, p))
            if due(g - 1):
                act.wait_ge(s["window_sums"], g - 1)
            if due(g - 1):
                act.wait_ge(s["sq_pairs"], g - 1)
            nc.scalar.activation(xq[p][:], xs[p][:], ACT.Square).then_inc(s["x_squared"], 1)

        def act_tanh(act, g, p):
            act.wait_ge(s["conv_done"], g + 1)
            act.wait_ge(s["wscale_ready"], g + 1)
            if due(g - 1):
                act.wait_ge(s["y_biased"], g - 1)
            for b in range(GB):
                a = nc.scalar.activation(y[p][:, b, :], conv_ps[p][:, b, :], ACT.Tanh,
                                         scale=wscale[p][:, b:b + 1])
            a.then_inc(s["tanh_done"], 1)

        def act_xnT(act, g, p):
            act.wait_ge(s["xnT_done"], g + 1)
            if due(g - 1):
                act.wait_ge(s["qkv_done"], g - 1)
            nc.scalar.activation(xnT[p][:], xnT_ps, ACT.Copy).then_inc(s["xnT_ready"], 1)

        def act_qk(act, g, p):
            act.wait_ge(s["qkv_done"], g + 1)
            if due(g - 1):
                act.wait_ge(s["scores_done"], g - 1)
            nc.scalar.activation(qT[p][:], qT_ps, ACT.Identity, bias=ba[:, 1:2]).then_inc(s["qT_ready"], 1)
            nc.scalar.activation(kT[p][:], kT_ps, ACT.Identity, bias=ba[:, 0:1]).then_inc(s["kT_ready"], 1)

        def act_memT(act, g, p):
            act.wait_ge(s["mem_done"], g + 1)
            if due(g - 1):
                act.wait_ge(s["o_done"], g - 1)
            nc.scalar.activation(memT[p][:], memT_ps, ACT.Copy).then_inc(s["memT_ready"], 1)

        def act_x2(act, g, p):
            act.wait_ge(s["x2_ready"], g + 1)
            if due(nth(g - 2, p, GB * TOPK)):
                act.wait_ge(rows_sent[p], nth(g - 2, p, GB * TOPK))
            nc.scalar.activation(rows[p][:, :, 1, 0:D], rows[p][:, :, 0, 0:D], ACT.Copy
                                 ).then_inc(s["x2_copied"], 1)

        def act_x2T(act, g, p):
            act.wait_ge(s["x2T_done"], g + 1)
            if due(g - 1):
                act.wait_ge(s["logits_done"], g - 1)
            nc.scalar.activation(x2T[p][:], x2T_ps, ACT.Copy).then_inc(s["x2T_ready"], 1)

        def act_e2(act, g, p):
            act.wait_ge(s["dlg_ready"], g + 1)
            if due(g - 1):
                act.wait_ge(s["gate2_ready"], g - 1)
            nc.scalar.activation(e2[p][:], dlg[p][:], ACT.Exp).then_inc(s["e2_ready"], 1)

        def pool_sq(pool, g, p):
            w2, w4 = GB * L - 2, GB * L - 6
            pool.wait_ge(s["x_squared"], g + 1)
            if due(g - 1):
                pool.wait_ge(s["sq_quads"], g - 1)
            pool.tensor_tensor(xq2[p][:, 0:w2], xq[p][:, 0:w2], xq[p][:, 2:w2 + 2], ALU.add
                               ).then_inc(s["sq_pairs"], 1)
            pool.wait_ge(s["sq_pairs"], g + 1)
            if due(g - 1):
                pool.wait_ge(s["window_sums"], g - 1)
            pool.tensor_tensor(xq4[p][:, 0:w4], xq2[p][:, 0:w4], xq2[p][:, 4:w4 + 4], ALU.add
                               ).then_inc(s["sq_quads"], 1)

        def pool_wnorm(pool, g, p):
            pool.wait_ge(s["wsq_ready"], g + 1)
            if due(g - 1):
                pool.wait_ge(s["wnorm_eps"], g - 1)
            pool.tensor_tensor(wnorm[p][:], wsq[p][:], const("half", S), ALU.pow).then_inc(s["wnorm_ready"], 1)

        def pool_bias(pool, g, p):
            pool.wait_ge(s["tanh_done"], g + 1)
            yb = const("b_tok", S).unsqueeze(1).broadcast_to([S, GB, D])
            pool.tensor_tensor(y[p][:], y[p][:], yb, ALU.add).then_inc(s["y_biased"], 1)

        def pool_rstd1(pool, g, p):
            pool.wait_ge(s["var1"], g + 1)
            if due(g - 1):
                pool.wait_ge(s["xn_ready"], g - 1)
            pool.tensor_tensor(rstd1[p][:], ve1[p][:], const("minushalf", S), ALU.pow
                               ).then_inc(s["rstd1_ready"], 1)

        def pool_hb(pool, g, p):
            pool.wait_ge(s["h_ready"], g + 1)
            if due(g - 1):
                pool.wait_ge(s["h2_ready"], g - 1)
            ob = const("b_o", S).unsqueeze(1).broadcast_to([S, GB, D])
            pool.tensor_tensor(hb[p][:], h[p][:], ob, ALU.add).then_inc(s["hb_ready"], 1)

        def pool_rstd2(pool, g, p):
            pool.wait_ge(s["var2"], g + 1)
            if due(g - 1):
                pool.wait_ge(s["x2_ready"], g - 1)
            pool.tensor_tensor(rstd2[p][:], ve2[p][:], const("minushalf", S), ALU.pow
                               ).then_inc(s["rstd2_ready"], 1)

        def pool_rows(pool, g, p):
            held(pool)
            pool.wait_ge(s["pos_ready"], g + 1)
            pool.wait_ge(s["gate1_ready"], g + 1)
            pool.wait_ge(s["gate2_ready"], g + 1)
            pool.wait_ge(s["x2_ready"], g + 1)
            pool.wait_ge(s["x2_copied"], g + 1)
            pool.wait_ge(s["ids_ready"], g + 1)
            for b in range(GB):
                for k in range(TOPK):
                    i = b * TOPK + k
                    pool.indirect_dma_start(routed, bass.IndirectOffsetOnAxis(pos[p][:, i:i + 1], 0),
                                            rows[p][:, b, k, :], None).then_inc(rows_sent[p], 16)

        def dve_wsq(dve, g, p):
            dve.wait_ge(s["window_sums"], g + 1)
            if due(g - 1):
                dve.wait_ge(s["wnorm_ready"], g - 1)
            nc.vector.tensor_scalar(wsq[p][:], wsq_ps, 0.0, None, ALU.max).then_inc(s["wsq_ready"], 1)

        def dve_wscale(dve, g, p):
            dve.wait_ge(s["wnorm_ready"], g + 1)
            nc.vector.tensor_scalar(wnorm_e[p][:], wnorm[p][:], EPS_TOK, None, ALU.add
                                    ).then_inc(s["wnorm_eps"], 1)
            dve.wait_ge(s["wnorm_eps"], g + 1)
            nc.vector.reciprocal(winv[p][:], wnorm_e[p][:]).then_inc(s["winv_ready"], 1)
            dve.wait_ge(s["winv_ready"], g + 1)
            if due(g - 1):
                dve.wait_ge(s["tanh_done"], g - 1)
            nc.vector.tensor_scalar(wscale[p][:], winv[p][:], 1.0, LAM_HALF, ALU.min, ALU.mult
                                    ).then_inc(s["wscale_ready"], 1)

        def dve_ln(dve, g, p, src, st, mv, ve, stats, aggr, var):
            for b in range(GB):
                i = nc.vector.bn_stats(st[p][:, b, :], src[p][:, b, :])
            i.then_inc(s[stats], 1)
            held(dve)
            dve.wait_ge(s[stats], g + 1)
            for b in range(GB):
                i = nc.vector.bn_aggr(mv[p][:, b, :], st[p][:, b, :])
            i.then_inc(s[aggr], 1)
            dve.wait_ge(s[aggr], g + 1)
            nc.vector.tensor_scalar(ve[p][:], mv[p][:, :, 1], EPS_LN, None, ALU.add).then_inc(s[var], 1)

        def dve_h(dve, g, p):
            dve.wait_ge(s["y_biased"], g + 1)
            if due(g - 1):
                dve.wait_ge(s["hb_ready"], g - 1)
            nc.vector.tensor_scalar(h[p][:], y[p][:], 0.0, None, ALU.max).then_inc(s["h_ready"], 1)
            dve.wait_ge(s["h_ready"], g + 1)
            if due(g - 1):
                dve.wait_ge(s["rstd1_ready"], g - 1)
            dve_ln(dve, g, p, h, st1, mv1, ve1, "stats1", "aggr1", "var1")

        def dve_xn(dve, g, p):
            dve.wait_ge(s["rstd1_ready"], g + 1)
            if due(g - 1):
                dve.wait_ge(s["xnT_done"], g - 1)
            for b in range(GB):
                i = nc.vector.tensor_scalar(xn[p][:, b, :], h[p][:, b, :], mv1[p][:, b, 0:1],
                                            rstd1[p][:, b:b + 1], ALU.subtract, ALU.mult)
            i.then_inc(s["xn_ready"], 1)

        def dve_v(dve, g, p):
            dve.wait_ge(s["qkv_done"], g + 1)
            if due(g - 1):
                dve.wait_ge(s["mem_done"], g - 1)
            nc.vector.tensor_tensor(v[p][:], v_ps, const("b_v", S).unsqueeze(1).broadcast_to([S, GB, D]),
                                    ALU.add).then_inc(s["v_ready"], 1)

        def dve_am(dve, g, p):
            dve.wait_ge(s["scores_done"], g + 1)
            if due(g - 1):
                dve.wait_ge(s["mem_done"], g - 1)
            nc.vector.tensor_tensor(am[p][:], at_ps, const("decay", S).unsqueeze(1).broadcast_to([S, GB, S]),
                                    ALU.mult).then_inc(s["am_ready"], 1)

        def dve_h2(dve, g, p):
            dve.wait_ge(s["o_done"], g + 1)
            dve.wait_ge(s["hb_ready"], g + 1)
            if due(nth(g - 2, p)):
                dve.wait_ge(h2_stored[p], nth(g - 2, p))
            nc.vector.tensor_tensor(h2[p][:], o_ps, hb[p][:], ALU.add).then_inc(s["h2_ready"], 1)
            dve.wait_ge(s["h2_ready"], g + 1)
            if due(g - 1):
                dve.wait_ge(s["rstd2_ready"], g - 1)
            dve_ln(dve, g, p, h2, st2, mv2, ve2, "stats2", "aggr2", "var2")

        def dve_x2(dve, g, p):
            dve.wait_ge(s["rstd2_ready"], g + 1)
            if due(nth(g - 2, p, GB * TOPK)):
                dve.wait_ge(rows_sent[p], nth(g - 2, p, GB * TOPK))
            if due(g - 1):
                dve.wait_ge(s["x2T_done"], g - 1)
            for b in range(GB):
                i = nc.vector.tensor_scalar(rows[p][:, b, 0, 0:D], h2[p][:, b, :], mv2[p][:, b, 0:1],
                                            rstd2[p][:, b:b + 1], ALU.subtract, ALU.mult)
            i.then_inc(s["x2_ready"], 1)
            ids = rows[p][:].bitcast(I32)[:, :, :, D + 1]
            tok = cst[0:S, bass.ds(_cols["token"][0] + g * GB, GB)]
            for k in range(TOPK):
                i = nc.vector.tensor_copy(ids[:, :, k], tok)
            i.then_inc(s["ids_ready"], 1)

        def dve_top(dve, g, p):
            dve.wait_ge(s["logits_done"], g + 1)
            if due(g - 1):
                dve.wait_ge(s["topi_ready"], g - 1)
            nc.vector.tensor_copy(lg[p][:], lg_ps).then_inc(s["lg_ready"], 1)
            held(dve)
            dve.wait_ge(s["lg_ready"], g + 1)
            for b in range(GB):
                i = nc.vector.max(top[p][:, b, :], lg[p][:, b, :])
            i.then_inc(s["top_ready"], 1)
            dve.wait_ge(s["top_ready"], g + 1)
            nc.vector.tensor_tensor(dlg[p][:], top[p][:, :, 1], top[p][:, :, 0], ALU.subtract
                                    ).then_inc(s["dlg_ready"], 1)
            for b in range(GB):
                i = nc.vector.max_index(topi[p][:, b, :], top[p][:, b, :], lg[p][:, b, :])
            i.then_inc(s["topi_ready"], 1)
            dve.wait_ge(s["topi_ready"], g + 1)
            nc.vector.tensor_copy(topf[p][:], topi[p][:, :, 0:TOPK]).then_inc(s["topf_ready"], 1)
            dve.wait_ge(s["topf_ready"], g + 1)
            for k in range(TOPK):
                ex = const("expert", S).unsqueeze(1).broadcast_to([S, GB, NE])
                nc.vector.tensor_tensor(oh[k][p][:], ex, topf[p][:, :, k:k + 1].broadcast_to([S, GB, NE]),
                                        ALU.is_equal).then_inc(s[f"oh{k + 1}_ready"], 1)
            dve.wait_ge(s["oh1_ready"], g + 1)
            dve.wait_ge(s["oh2_ready"], g + 1)
            if due(g - 1):
                dve.wait_ge(s["places_done"], g - 1)
            nc.vector.tensor_tensor(chosen[p][:], oh[0][p][:], oh[1][p][:], ALU.add
                                    ).then_inc(s["chosen_ready"], 1)
            dve.wait_ge(s["chosen_ready"], g + 1)
            for b in range(1, GB + 1):
                if b == 1:
                    i = nc.vector.tensor_copy(cum[p][:, 1, :], chosen[p][:, 0, :])
                else:
                    i = nc.vector.tensor_tensor(cum[p][:, b, :], cum[p][:, b - 1, :], chosen[p][:, b - 1, :],
                                                ALU.add)
                i.then_inc(s["cum_ready"] if b == GB else s["table"], 1)
                if b < GB:
                    dve.wait_ge(s["table"], g * (GB - 1) + b)

        def dve_gates(dve, g, p):
            dve.wait_ge(s["e2_ready"], g + 1)
            nc.vector.tensor_scalar(e21[p][:], e2[p][:], 1.0, None, ALU.add).then_inc(s["e21_ready"], 1)
            dve.wait_ge(s["e21_ready"], g + 1)
            nc.vector.reciprocal(rows[p][:, :, 0, D], e21[p][:]).then_inc(s["gate1_ready"], 1)
            dve.wait_ge(s["gate1_ready"], g + 1)
            nc.vector.tensor_tensor(rows[p][:, :, 1, D], e2[p][:], rows[p][:, :, 0, D], ALU.mult
                                    ).then_inc(s["gate2_ready"], 1)

        def dve_places(dve, g, p):
            q = 1 - p
            dve.wait_ge(s["places_done"], g + 1)
            nc.vector.tensor_tensor(place[p][:], place_ps[0:S, 0:GB, :],
                                    start_at[p][0:S].unsqueeze(1).broadcast_to([S, GB, NE]), ALU.add
                                    ).then_inc(s["place_ready"], 1)
            nc.vector.tensor_tensor(count[q][:], place_ps[:, GB, :], count[p][:], ALU.add
                                    ).then_inc(s["count_ready"], 1)
            dve.wait_ge(s["place_ready"], g + 1)
            for k in range(TOPK):
                i = nc.vector.tensor_tensor(placek[k][p][:], place[p][:], oh[k][p][:], ALU.mult)
            i.then_inc(s["placek_ready"], 1)
            dve.wait_ge(s["count_ready"], g + 1)
            nc.vector.tensor_tensor(start_at[q][:], count[q][:], const("region"), ALU.add
                                    ).then_inc(s["start_ready"], 1)
            dve.wait_ge(s["placek_ready"], g + 1)
            for k in range(TOPK):
                i = nc.vector.tensor_reduce(posf[p][:, :, k], placek[k][p][:], AX.X, ALU.add)
            i.then_inc(s["posf_ready"], 1)
            dve.wait_ge(s["posf_ready"], g + 1)
            if due(nth(g - 2, p, GB * TOPK)):
                dve.wait_ge(rows_sent[p], nth(g - 2, p, GB * TOPK))
            nc.vector.tensor_copy(pos[p][:].rearrange("p (b k) -> p b k", b=GB), posf[p][:]
                                  ).then_inc(s["pos_ready"], 1)

        def steps(engine_step, eng):
            n = NG
            engine_step(0, 0, None, None)
            engine_step(1, 1, 0, None)
            engine_step(0, 2, 1, 0)
            engine_step(1, 3, 2, 1)
            with eng.Fori(2, n // 2) as j:
                engine_step(0, j * 2, j * 2 - 1, j * 2 - 2)
                engine_step(1, j * 2 + 1, j * 2, j * 2 - 1)
            engine_step(0, None, n - 1, n - 2)
            engine_step(1, None, None, n - 1)

        block = ctx.enter_context(nc.Block())

        @block.sync
        def _(sp):
            sp.dma_start(cst[:], consts).then_inc(n_ld, 16)
            sp.dma_start(wc[:], wconv).then_inc(n_ld, 16)
            sp.dma_start(wa[:], wattn).then_inc(n_ld, 16)
            sp.dma_start(ba[:], battn).then_inc(n_ld, 16)
            sp.dma_start(wg[:], wgate).then_inc(n_ld, 16)

            def step(par, g1, g2_, g3):
                if g1 is not None:
                    sp_group(sp, g1, par)
                    if isinstance(g1, int) and g1 == 0:
                        for i in range(3):
                            sp.dma_start(wst[i][:], wraw[i]).then_inc(w_loaded[i], 16)
                if g2_ is not None:
                    sp_weights(sp, g2_)
                if g3 is not None:
                    sp_h2(sp, g3, par)

            steps(step, sp)
            for i in range(3):
                sp.wait_ge(w_stored[i], 16 * NE * NBLK // 3)
            sp.wait_ge(s["tables_ready"], 1)
            for p in range(2):
                sp.wait_ge(rows_sent[p], nth(NG - 2 + p, p, GB * TOPK))
            sp.wait_ge(s["pad_sent"], 16 * (NE + 1))

            def load_rows(t, p):
                if due(t - 1):
                    sp.wait_ge(s["xT_done"], t - 1)
                r = sp.value_load(tile_row[0:1, bass.ds(t, 1)], min_val=0, max_val=NE * REG)
                sp.dma_start(xr[p][:], routed[bass.ds(r, TS), 0:D]).then_inc(row_loaded[p], 16)

            def load_block(k, blk, new):
                src = w_scaled[bass.ds(blk + k, 1)].rearrange("o p c -> (o p) c")
                dst = wb[k][:].rearrange("p c o -> p (c o)")
                if new is None:
                    sp.dma_start(dst, src).then_inc(blk_loaded[k], 16)
                else:
                    sp.dma_start(dst, src, cond=(new > 0)).then_inc(blk_loaded[k], 16)

            def tile_info(t):
                return (sp.value_load(tile_blk[0:1, bass.ds(t, 1)], min_val=0, max_val=(NE - 1) * NBLK),
                        sp.value_load(tile_new[0:1, bass.ds(t, 1)], min_val=0, max_val=1))

            load_rows(0, 0)
            load_rows(1, 1)
            blk0 = sp.value_load(tile_blk[0:1, 0:1], min_val=0, max_val=(NE - 1) * NBLK)
            for k in range(NBLK):
                load_block(k, blk0, None)

            def first_blocks(t):
                blk, new = tile_info(t)
                for k in range(4):
                    sp.wait_ge(s["hidden_done"], 4 * (t - 1) + k + 1)
                    load_block(k, blk, new)

            def last_blocks(t):
                blk, new = tile_info(t)
                for k in range(4, NBLK):
                    sp.wait_ge(s["half_used"], 2 * (t - 1) + k - 3)
                    load_block(k, blk, new)

            load_rows(2, 0)
            for t in range(1, 4):
                load_rows(t + 2, t % 2)
                first_blocks(t)
            with sp.Fori(2, NT // 2 - 1) as j:
                for p in range(2):
                    load_rows(j * 2 + p + 2, p)
                    last_blocks(j * 2 + p - 3)
                    first_blocks(j * 2 + p)
            last_blocks(NT - 5)
            first_blocks(NT - 2)
            last_blocks(NT - 4)
            first_blocks(NT - 1)
            for t in range(NT - 3, NT):
                last_blocks(t)
            for k in range(NBLK):
                sp.wait_ge(blk_loaded[k], 16 * NT)
            for p in range(2):
                sp.wait_ge(h2_stored[p], nth(NG - 2 + p, p))

        @block.tensor
        def _(pe):
            pe.wait_ge(n_ld, 16 * NPARAM)

            def step(par, g1, g2_, g3):
                if g1 is not None:
                    pe_window(pe, g1, par)
                    pe_conv(pe, g1, par, 0)
                if g2_ is not None:
                    pe_xnT(pe, g2_, 1 - par)
                if g1 is not None:
                    pe_conv(pe, g1, par, 1)
                if g2_ is not None:
                    pe_qkv(pe, g2_, 1 - par)
                if g1 is not None:
                    pe_conv(pe, g1, par, 2)
                if g3 is not None:
                    pe_x2T(pe, g3, par)
                if g2_ is not None:
                    pe_scores(pe, g2_, 1 - par)
                if g3 is not None:
                    pe_logits(pe, g3, par)
                if g1 is not None:
                    pe_conv(pe, g1, par, 3)
                if g2_ is not None:
                    pe_mem(pe, g2_, 1 - par)
                    pe_o(pe, g2_, 1 - par)
                if g3 is not None:
                    pe_places(pe, g3, par)

            steps(step, pe)

            def turn_x(t, p):
                pe.wait_ge(row_loaded[p], nth(t, p))
                if due(t - 1):
                    pe.wait_ge(s["u_in_ready"], t - 1)
                pe.transpose(xT_ps[p], xr[p][:], const("ident")).then_inc(s["xT_done"], 1)

            def hidden(t, p):
                pe.wait_ge(s["feat_in_ready"], t + 1)
                pe.wait_ge(s["silu_in_ready"], t + 1)
                if due(t - 1):
                    pe.wait_ge(s["u_mid_ready"], t - 1)
                for k in range(4):
                    pe.wait_ge(blk_loaded[k], 16 * (t + 1))
                    for c in range(KC):
                        mm = pe.matmul(hid_ps[p][k // 2][:, k % 2, :], wb[k][:, c, :], feat_in[p][:, c, :],
                                       start=(c == 0), stop=(c == KC - 1))
                    mm.then_inc(s["hidden_done"], 1)

            def last_layer(t, p):
                pe.wait_ge(s["feat_mid_ready"], t + 1)
                pe.wait_ge(s["silu_mid_ready"], t + 1)
                if due(t - 1):
                    pe.wait_ge(s["ye_ready"], t - 1)
                for f in range(2):
                    pe.wait_ge(blk_loaded[4 + f], 16 * (t + 1))
                    for c in range(KC):
                        mm = pe.matmul(y_ps[p], feat_mid[p][:, c, f, :], wb[4 + f][:, c, :],
                                       start=(f == 0 and c == 0), stop=(f == 1 and c == KC - 1))
                    mm.then_inc(s["half_used"], 1)

            def tile_step(t, p):
                turn_x(t + 2, p)
                if due(t - 2):
                    last_layer(t - 3, 1 - p)
                hidden(t, p)

            turn_x(0, 0)
            turn_x(1, 1)
            for t in range(4):
                tile_step(t, t % 2)
            with pe.Fori(2, NT // 2 - 1) as j:
                tile_step(j * 2, 0)
                tile_step(j * 2 + 1, 1)
            for t in range(NT - 2, NT):
                last_layer(t - 3, (t - 3) % 2)
                hidden(t, t % 2)
            for t in range(NT - 3, NT):
                last_layer(t, t % 2)

        @block.scalar
        def _(act):
            act.wait_ge(n_ld, 16 * NPARAM)

            def step(par, g1, g2_, g3):
                if g1 is not None:
                    act_square(act, g1, par)
                if g2_ is not None:
                    act_xnT(act, g2_, 1 - par)
                if g3 is not None:
                    act_x2T(act, g3, par)
                if g2_ is not None:
                    act_qk(act, g2_, 1 - par)
                if g3 is not None:
                    act_x2(act, g3, par)
                    act_e2(act, g3, par)
                if g1 is not None:
                    act_tanh(act, g1, par)
                if g2_ is not None:
                    act_memT(act, g2_, 1 - par)

            steps(step, act)

            def turn(t, p):
                act.wait_ge(s["xT_done"], t + 1)
                if due(t - 1):
                    act.wait_ge(s["silu_in_ready"], t - 1)
                nc.scalar.activation(u_in[p][:], xT_ps[p], ACT.Copy, scale=0.5).then_inc(s["u_in_ready"], 1)

            def distances(u, dist):
                for i in range(NB):
                    a = nc.scalar.activation(dist[:, i], u[:], ACT.Abs, scale=2.0 / H_GRID,
                                             bias=1.0 / H_GRID - (i - 1))
                return a

            def start_in(t, p):
                act.wait_ge(s["u_in_ready"], t + 1)
                if due(t):
                    act.wait_ge(s["z_in_ready"], t)
                distances(u_in[p], dist_in).then_inc(s["dist_in_ready"], 1)
                if due(t):
                    act.wait_ge(s["silu_in_ready"], t)
                nc.scalar.activation(th_in[:], u_in[p][:], ACT.Tanh).then_inc(s["th_in_ready"], 1)
                act.wait_ge(s["dist_in_ready"], t + 1)
                if due(t):
                    act.wait_ge(s["y_in_ready"], t)
                nc.scalar.activation(z_in[:], dist_in[:], ACT.Relu, scale=-1.0, bias=2.0
                                     ).then_inc(s["z_in_ready"], 1)

            def squares_in(t):
                act.wait_ge(s["z_in_ready"], t + 1)
                if due(t):
                    act.wait_ge(s["feat_in_ready"], t)
                nc.scalar.activation(a2_in[:], z_in[:], ACT.Square, scale=-ROOT3, bias=2 * ROOT3
                                     ).then_inc(s["a2_in_ready"], 1)
                nc.scalar.activation(z2_in[:], z_in[:], ACT.Square).then_inc(s["z2_in_ready"], 1)

            def half_of_h2(t, p):
                act.wait_ge(s["hidden_done"], 4 * t + 4)
                if due(t):
                    act.wait_ge(s["u_mid_ready"], t)
                nc.scalar.activation(g2[:], hid_ps[p][1], ACT.Copy, scale=0.5).then_inc(s["g2_ready"], 1)

            def start_mid(t):
                act.wait_ge(s["u_mid_ready"], t + 1)
                if due(t):
                    act.wait_ge(s["m_mid_ready"], t)
                distances(u_mid, dist_mid).then_inc(s["dist_mid_ready"], 1)
                if due(t):
                    act.wait_ge(s["silu_mid_ready"], t)
                nc.scalar.activation(th_mid[:], u_mid[:], ACT.Tanh).then_inc(s["th_mid_ready"], 1)

            def squares_mid(t):
                act.wait_ge(s["m_mid_ready"], t + 1)
                if due(t):
                    act.wait_ge(s["feat_mid_ready"], t)
                nc.scalar.activation(a2_mid[:], m_mid[:], ACT.Square, scale=ROOT3, bias=2 * ROOT3
                                     ).then_inc(s["a2_mid_ready"], 1)
                nc.scalar.activation(z2_mid[:], m_mid[:], ACT.Square).then_inc(s["z2_mid_ready"], 1)

            def gated(t, p):
                act.wait_ge(s["half_used"], 2 * t + 2)
                act.wait_ge(tag_loaded[p], nth(t, p))
                if due(t - 1):
                    act.wait_ge(s["out_added"], 16 * (t - 1))
                nc.scalar.activation(ye[p][:], y_ps[p], ACT.Copy, scale=tag[p][:, 0:1]
                                     ).then_inc(s["ye_ready"], 1)

            def tile_step(t, p):
                if due(t):
                    half_of_h2(t - 1, 1 - p)
                if due(t - 1):
                    squares_mid(t - 2)
                if due(t):
                    start_mid(t - 1)
                if not isinstance(t, int) or t + 2 < NT:
                    turn(t + 2, p)
                    start_in(t + 2, p)
                    squares_in(t + 2)
                if due(t - 2):
                    gated(t - 3, 1 - p)

            for t in range(2):
                turn(t, t)
                start_in(t, t)
                squares_in(t)
            for t in range(4):
                tile_step(t, t % 2)
            with act.Fori(2, NT // 2 - 1) as j:
                tile_step(j * 2, 0)
                tile_step(j * 2 + 1, 1)
            tile_step(NT - 2, 0)
            tile_step(NT - 1, 1)
            half_of_h2(NT - 1, 1)
            squares_mid(NT - 2)
            start_mid(NT - 1)
            gated(NT - 3, 1)
            squares_mid(NT - 1)
            gated(NT - 2, 0)
            gated(NT - 1, 1)

        @block.gpsimd
        def _(pool):
            pool.wait_ge(n_ld, 16 * NPARAM)

            def step(par, g1, g2_, g3):
                if g1 is not None:
                    pool_sq(pool, g1, par)
                    pool_wnorm(pool, g1, par)
                if g3 is not None:
                    pool_rstd2(pool, g3, par)
                if g1 is not None:
                    pool_bias(pool, g1, par)
                    pool_hb(pool, g1, par)
                    pool_rstd1(pool, g1, par)
                if g3 is not None:
                    pool_rows(pool, g3, par)

            steps(step, pool)
            pool.wait_ge(s["table"], NG * (GB - 1) + 2)
            for e in range(NE):
                pool.indirect_dma_start(routed, bass.IndirectOffsetOnAxis(padi[:, e:e + 1], 0),
                                        padrow[:], None).then_inc(s["pad_sent"], 16)
            pool.dma_start(routed[NE * REG:NE * REG + TS], padrow[:]).then_inc(s["pad_sent"], 16)
            pool.dma_start(out[TOK:TOK + TS], padrow[:, 0:D]).then_inc(s["dump_zeroed"], 16)
            pool.wait_ge(s["dump_zeroed"], 16)
            for p in range(2):
                pool.wait_ge(h2_stored[p], nth(NG - 2 + p, p))

            def add(t, p):
                pool.wait_ge(s["ye_ready"], t + 1)
                if due(t):
                    pool.wait_ge(s["out_added"], 16 * t)
                pool.sem_inc(s["pool_goes_on"], 1)
                pool.indirect_dma_start(out, bass.IndirectOffsetOnAxis(tag[p][:, 1:2].bitcast(I32), 0),
                                        ye[p][:], None, compute_op=ALU.add).then_inc(s["out_added"], 16)

            def load_tags(t, p):
                r = pool.value_load(tile_row[0:1, bass.ds(t, 1)], min_val=0, max_val=NE * REG)
                if due(t - 1):
                    pool.wait_ge(s["out_added"], 16 * (t - 1))
                pool.sem_inc(s["pool_goes_on"], 1)
                pool.dma_start(tag[p][:], routed[bass.ds(r, TS), D:RW]).then_inc(tag_loaded[p], 16)

            for i in range(2):
                pool.wait_ge(rows_sent[i], nth(NG - 2 + i, i, GB * TOPK))
            pool.wait_ge(s["pad_sent"], 16 * (NE + 1))
            pool.wait_ge(s["tables_ready"], 1)
            load_tags(0, 0)
            load_tags(1, 1)
            add(0, 0)
            load_tags(2, 0)
            add(1, 1)
            load_tags(3, 1)
            with pool.Fori(1, NT // 2 - 1) as j:
                for p in range(2):
                    add(j * 2 + p, p)
                    load_tags(j * 2 + p + 2, p)
            add(NT - 2, 0)
            add(NT - 1, 1)
            pool.wait_ge(s["out_added"], 16 * NT)

        @block.vector
        def _(dve):
            dve.wait_ge(n_ld, 16 * NPARAM)
            for p in range(2):
                nc.vector.memset(cum[p][:, 0, :], 0.0).then_inc(s["setup"], 1)
            nc.vector.memset(count[0][:], 0.0).then_inc(s["setup"], 1)
            nc.vector.tensor_copy(start_at[0][:], const("region")).then_inc(s["setup"], 1)
            nc.vector.memset(padrow[:, 0:D + 1], 0.0).then_inc(s["setup"], 1)
            nc.vector.tensor_copy(padrow[:].bitcast(I32)[:, D + 1:D + 2], const("dump")).then_inc(s["setup"], 1)
            nc.vector.memset(expert9[:, NE:NE + 1], float(NE)).then_inc(s["setup"], 1)
            nc.vector.tensor_copy(expert9[:, 0:NE], const("expert", 1)).then_inc(s["setup"], 1)
            nc.vector.memset(base[:, NE:NE + 1], 0.0).then_inc(s["setup"], 1)
            dve.wait_ge(s["setup"], 9)

            def step(par, g1, g2_, g3):
                if g1 is not None:
                    dve_wsq(dve, g1, par)
                if g3 is not None:
                    dve_x2(dve, g3, par)
                if g1 is not None:
                    dve_wscale(dve, g1, par)
                if g2_ is not None:
                    dve_v(dve, g2_, 1 - par)
                if g3 is not None:
                    dve_top(dve, g3, par)
                if g2_ is not None:
                    dve_am(dve, g2_, 1 - par)
                if g3 is not None:
                    dve_gates(dve, g3, par)
                if g1 is not None:
                    dve_h(dve, g1, par)
                if g3 is not None:
                    dve_places(dve, g3, par)
                if g2_ is not None:
                    dve_weights(dve, g2_)
                    dve_h2(dve, g2_, 1 - par)
                if g1 is not None:
                    dve_xn(dve, g1, par)

            steps(step, dve)

            done = [NG * (GB - 1)]

            def link(i):
                i.then_inc(s["table"], 1)
                done[0] += 1
                dve.wait_ge(s["table"], done[0])

            tot = count[0]
            link(nc.vector.tensor_tensor(padf[:], const("padrow"), tot[:], ALU.add))
            link(nc.vector.tensor_copy(padi[:], padf[:]))
            link(nc.vector.tensor_scalar(cnt_i[:], tot[:], float(TS - 1), None, ALU.add))
            link(nc.vector.tensor_scalar(nt_i[:], cnt_i[:], TS.bit_length() - 1, None, ALU.logical_shift_right))
            link(nc.vector.tensor_copy(nt_f[:], nt_i[:]))
            link(nc.vector.tensor_copy(end_a[:], nt_f[:]))
            a, b = end_a, end_b
            for d in (1, 2, 4):
                link(nc.vector.tensor_copy(b[:, 0:d], a[:, 0:d]))
                link(nc.vector.tensor_tensor(b[:, d:NE], a[:, d:NE], a[:, 0:NE - d], ALU.add))
                a, b = b, a
            end = a
            link(nc.vector.tensor_tensor(first[:], end[:], nt_f[:], ALU.subtract))
            link(nc.vector.scalar_tensor_tensor(base[:, 0:NE], first[:], -float(TS), const("region"),
                                                ALU.mult, ALU.add))
            tiles = const("tile", 1)
            n1 = NT + 1
            link(nc.vector.tensor_tensor(past[:], tiles.unsqueeze(2).broadcast_to([1, n1, NE]),
                                         end[0:1].unsqueeze(1).broadcast_to([1, n1, NE]), ALU.is_ge))
            link(nc.vector.tensor_reduce(past_n[:], past[:], AX.X, ALU.add))
            link(nc.vector.tensor_tensor(is_e[:], expert9[:].unsqueeze(1).broadcast_to([1, n1, NE + 1]),
                                         past_n[:].unsqueeze(2).broadcast_to([1, n1, NE + 1]), ALU.is_equal))
            link(nc.vector.tensor_tensor(rs_e[:], is_e[:], base[0:1].unsqueeze(1).broadcast_to([1, n1, NE + 1]),
                                         ALU.mult))
            link(nc.vector.scalar_tensor_tensor(rs_e[:, :, NE], tiles, -float(TS), is_e[:, :, NE],
                                                ALU.mult, ALU.mult))
            link(nc.vector.scalar_tensor_tensor(rs_e[:, :, NE], is_e[:, :, NE], float(NE * REG),
                                                rs_e[:, :, NE], ALU.mult, ALU.add))
            link(nc.vector.tensor_reduce(rs_f[:], rs_e[:], AX.X, ALU.add))
            link(nc.vector.scalar_tensor_tensor(rs_f[:], tiles, float(TS), rs_f[:], ALU.mult, ALU.add))
            link(nc.vector.tensor_copy(tile_row[:], rs_f[:]))
            link(nc.vector.tensor_scalar(eidx[:], past_n[:], float(NE - 1), float(NBLK), ALU.min, ALU.mult))
            link(nc.vector.tensor_copy(tile_blk[:], eidx[:]))
            link(nc.vector.memset(tile_new[:, 0:1], 1))
            nc.vector.tensor_tensor(tile_new[:, 1:n1], eidx[:, 1:n1], eidx[:, 0:n1 - 1], ALU.not_equal
                                    ).then_inc(s["tables_ready"], 1)

            def silu(th, u, feat):
                return nc.vector.scalar_tensor_tensor(feat, th, 1.0, u, ALU.add, ALU.mult)

            def finish_in(t, p):
                dve.wait_ge(s["th_in_ready"], t + 1)
                if due(t - 1):
                    dve.wait_ge(s["hidden_done"], 4 * (t - 1))
                silu(th_in[:], u_in[p][:], feat_in[p][:, NB]).then_inc(s["silu_in_ready"], 1)
                dve.wait_ge(s["a2_in_ready"], t + 1)
                nc.vector.tensor_tensor(a2_in[:], a2_in[:], z_in[:], ALU.mult).then_inc(s["x_in_ready"], 1)
                dve.wait_ge(s["z2_in_ready"], t + 1)
                nc.vector.tensor_tensor(z2_in[:], z2_in[:], z_in[:], ALU.mult).then_inc(s["y_in_ready"], 1)
                dve.wait_ge(s["x_in_ready"], t + 1)
                dve.wait_ge(s["y_in_ready"], t + 1)
                nc.vector.scalar_tensor_tensor(feat_in[p][:, 0:NB], a2_in[:], 4.0, z2_in[:], ALU.subtract,
                                               ALU.min, reverse0=True).then_inc(s["feat_in_ready"], 1)

            def product(t, p):
                dve.wait_ge(s["g2_ready"], t + 1)
                if due(t):
                    dve.wait_ge(s["silu_mid_ready"], t)
                nc.vector.tensor_tensor(u_mid[:], hid_ps[p][0], g2[:], ALU.mult).then_inc(s["u_mid_ready"], 1)

            def cut_mid(t, p):
                dve.wait_ge(s["dist_mid_ready"], t + 1)
                nc.vector.tensor_scalar(m_mid[:], dist_mid[:], 2.0, 2.0, ALU.min, ALU.subtract
                                        ).then_inc(s["m_mid_ready"], 1)
                dve.wait_ge(s["th_mid_ready"], t + 1)
                if due(t - 1):
                    dve.wait_ge(s["half_used"], 2 * (t - 1))
                silu(th_mid[:], u_mid[:], feat_mid[p][:, NB]).then_inc(s["silu_mid_ready"], 1)

            def finish_mid(t, p):
                dve.wait_ge(s["a2_mid_ready"], t + 1)
                nc.vector.tensor_tensor(a2_mid[:], a2_mid[:], m_mid[:], ALU.mult).then_inc(s["x_mid_ready"], 1)
                dve.wait_ge(s["z2_mid_ready"], t + 1)
                nc.vector.tensor_tensor(z2_mid[:], z2_mid[:], m_mid[:], ALU.mult).then_inc(s["y_mid_ready"], 1)
                dve.wait_ge(s["x_mid_ready"], t + 1)
                dve.wait_ge(s["y_mid_ready"], t + 1)
                nc.vector.scalar_tensor_tensor(feat_mid[p][:, 0:NB], a2_mid[:], -4.0, z2_mid[:], ALU.subtract,
                                               ALU.max, reverse0=True).then_inc(s["feat_mid_ready"], 1)

            def tile_step(t, p):
                if not isinstance(t, int) or t + 1 < NT:
                    finish_in(t + 1, 1 - p)
                if due(t):
                    product(t - 1, 1 - p)
                if due(t - 1):
                    finish_mid(t - 2, p)
                if due(t):
                    cut_mid(t - 1, 1 - p)

            finish_in(0, 0)
            for t in range(4):
                tile_step(t, t % 2)
            with dve.Fori(2, NT // 2 - 1) as j:
                tile_step(j * 2, 0)
                tile_step(j * 2 + 1, 1)
            tile_step(NT - 2, 0)
            tile_step(NT - 1, 1)
            product(NT - 1, 1)
            finish_mid(NT - 2, 0)
            cut_mid(NT - 1, 1)
            finish_mid(NT - 1, 1)


def kernel(x, L0_tok_kernel, L0_tok_bias, L0_attn_Wk, L0_attn_bk, L0_attn_Wv, L0_attn_bv, L0_attn_Wq, L0_attn_bq,
           L0_attn_Wo, L0_attn_bo, L0_ffn_gate_w, L0_ffn_base_w1, L0_ffn_spline_w1, L0_ffn_scaler_w1,
           L0_ffn_base_w2, L0_ffn_spline_w2, L0_ffn_scaler_w2, L0_ffn_base_w3, L0_ffn_spline_w3,
           L0_ffn_scaler_w3):
    import concourse.bacc as bacc
    from concourse.bass_utils import run_bass_kernel_spmd

    xt = np.asarray(x).transpose(2, 0, 1).reshape(C, B * L)
    x2 = np.zeros((2 * C, B * L), xt.dtype)
    x2[:C] = xt
    x2[C:, :-1] = xt[:, 1:]
    taps = np.zeros((2 * TAPS2, C, D), xt.dtype)
    taps[:K] = np.asarray(L0_tok_kernel)
    wconv = taps.reshape(TAPS2, 2 * C, D).transpose(1, 0, 2).reshape(2 * C, TAPS2 * D)
    wattn = np.concatenate([np.asarray(w) for w in (L0_attn_Wk, L0_attn_Wv, L0_attn_Wq, L0_attn_Wo)], axis=1)
    battn = np.stack([np.asarray(L0_attn_bk), np.asarray(L0_attn_bq)], axis=1)
    wgate = np.asarray(L0_ffn_gate_w).T
    consts = constants()
    for name, bias in (("b_tok", L0_tok_bias), ("b_v", L0_attn_bv), ("b_o", L0_attn_bo)):
        consts[:, _cols[name][0]:_cols[name][1]] = np.asarray(bias)[None, :]

    def blocks(w1, w2, w3, tail):
        def first(w, half):
            return w[:, half * D:(half + 1) * D]

        parts = [first(w1, 0), first(w1, 1), first(w2, 0), first(w2, 1), w3[:, :, :D], w3[:, :, D:]]
        a = np.stack([p.reshape(NE, D, D, tail).transpose(0, 2, 3, 1) for p in parts], axis=1)
        return a.reshape(NE * NBLK, D, tail * D)

    wraw = np.concatenate([
        blocks(*(np.asarray(w) for w in (L0_ffn_spline_w1, L0_ffn_spline_w2, L0_ffn_spline_w3)), NB),
        blocks(*(np.asarray(w) for w in (L0_ffn_base_w1, L0_ffn_base_w2, L0_ffn_base_w3)), 1),
        blocks(*(np.asarray(w) for w in (L0_ffn_scaler_w1, L0_ffn_scaler_w2, L0_ffn_scaler_w3)), 1),
    ], axis=2)

    nc = bacc.Bacc("TRN2", target_bir_lowering=False, num_devices=1)
    arrays, args = {}, []
    for name, a in (("x2", x2), ("wconv", wconv), ("wattn", wattn), ("battn", battn), ("wgate", wgate),
                    ("wraw", wraw), ("consts", consts)):
        arrays[name] = np.ascontiguousarray(a)
        args.append(nc.dram_tensor(name, a.shape, mybir.dt.from_np(arrays[name].dtype), kind="ExternalInput").ap())
    out = nc.dram_tensor("out_0", (TOK + TS, D), F32, kind="ExternalOutput").ap()
    audio_tower(nc, *args, out)
    r = run_bass_kernel_spmd(nc, [arrays], core_ids=[0])
    return r.results[0]["out_0"][:TOK].reshape(B, S, D)
```

```python
from contextlib import ExitStack

import numpy as np
import concourse.bass as bass
from concourse import mybir
from concourse.alu_op_type import AluOpType as ALU

ACT = mybir.ActivationFunctionType
AX = mybir.AxisListType
F32 = mybir.dt.float32
I32 = mybir.dt.int32
U32 = mybir.dt.uint32

B, L, C = 32, 125, 64
K, D = 9, 128
S = L - K + 1
TOK = B * S
NE, TOPK, FF = 8, 2, 256
NB = 8
KC = NB + 1
NBLK = 3 * FF // D
BLK = NB * D
RAW = BLK + D
GB = 4
NG = B // GB
GT = GB * S
TAPS2 = (K + 1) // 2
TS = 128
NT = (TOK * TOPK + NE * (TS - 1)) // TS
REG = TOK + TS
RW = D + 2
NSTEP = NG + 2
NWB = NE * NBLK
WPS = -(-NWB // NSTEP)
AHEAD = 6
EPS_LN = 1e-5
EPS_TOK = 1e-7
LAM_HALF = 1.0 / (1.0 + EPS_TOK)
H_GRID = 2.0 / 5
ROOT3 = 3.0 ** 0.5
assert NT % 2 == 0 and NG % 2 == 0

_cols = {}
_at = 0
for _name, _n in (("ident", D), ("decay", S), ("before", S), ("ones", D), ("expert", NE),
                  ("dump", 1), ("token", B), ("tile", NT + 1), ("half", GB), ("minushalf", GB),
                  ("b_tok", D), ("b_v", D), ("b_o", D), ("region", NE)):
    _cols[_name] = (_at, _at + _n)
    _at += _n
NCONST = _at


def constants():
    c = np.zeros((D, NCONST), np.float32)

    def put(name, a):
        c[:a.shape[0], _cols[name][0]:_cols[name][1]] = a

    put("ident", np.eye(D))
    s, t = np.arange(S)[:, None], np.arange(S)[None, :]
    put("decay", np.where(t > s, 0.1 * 0.9 ** np.maximum(t - 1 - s, 0), 0.0))
    put("before", (s < t).astype(np.float32))
    put("ones", np.ones((D, D)))
    put("expert", np.tile(np.arange(NE), (D, 1)))
    put("dump", TOK + np.arange(D)[:, None])
    put("token", np.arange(B)[None, :] * S + np.arange(D)[:, None])
    put("tile", np.tile(np.arange(NT + 1), (D, 1)))
    put("half", np.full((D, GB), 0.5))
    put("minushalf", np.full((D, GB), -0.5))
    put("region", np.tile(np.arange(NE) * REG, (D, 1)))
    return c


def audio_tower(nc, x2, wconv, wattn, battn, wgate, wraw, wbase, consts, out):
    with ExitStack() as ctx:
        groups_memory = ExitStack()
        held_by = [ctx]

        def sb(name, shape, dt=F32):
            return held_by[0].enter_context(nc.sbuf_tensor(name, shape, dt))

        def ps(name, shape):
            return ctx.enter_context(nc.psum_tensor(name, shape, F32))

        def sem(name):
            return ctx.enter_context(nc.semaphore(name))

        w_scaled = nc.dram_tensor("w_scaled", (NWB, D, BLK), F32).ap()
        routed = nc.dram_tensor("routed", (NE * REG + TS, RW), F32).ap()

        cst = sb("cst", [D, NCONST])

        def const(name, rows=D):
            return cst[0:rows, _cols[name][0]:_cols[name][1]]

        wc = sb("wc", [D, TAPS2 * D])
        wa = sb("wa", [D, 4 * D])
        ba = sb("ba", [D, 2])
        wg = sb("wg", [D, NE])

        count = sb("count", [D, NE])
        padrow = sb("padrow", [D, RW])
        pad_at = sb("pad_at", [1, NE], I32)
        cnt_i = sb("cnt_i", [D, NE], I32)
        nt_i = sb("nt_i", [D, NE], I32)
        nt_f = sb("nt_f", [D, NE])
        end_a = sb("end_a", [D, NE])
        end_b = sb("end_b", [D, NE])
        first = sb("first", [D, NE])
        base = sb("base", [D, NE + 1])
        past = sb("past", [1, NT + 1, NE])
        past_n = sb("past_n", [1, NT + 1])
        is_e = sb("is_e", [1, NT + 1, NE + 1])
        rs_e = sb("rs_e", [1, NT + 1, NE + 1])
        rs_f = sb("rs_f", [1, NT + 1])
        eidx = sb("eidx", [1, NT + 1])
        expert9 = sb("expert9", [1, NE + 1])
        tile_row = sb("tile_row", [1, NT + 1], I32)
        tile_blk = sb("tile_blk", [1, NT + 1], I32)
        tile_new = sb("tile_new", [1, NT + 1], I32)
        held_by[0] = groups_memory
        xs = [sb(f"xs{p}", [D, GB * L]) for p in range(2)]
        xq2 = [sb(f"xq2{p}", [D, GB * L]) for p in range(2)]
        xq4 = [sb(f"xq4{p}", [D, GB * L]) for p in range(2)]
        xq = [sb(f"xq{p}", [D, GB * L]) for p in range(2)]
        wsq = [sb(f"wsq{p}", [S, GB]) for p in range(2)]
        wnorm = [sb(f"wnorm{p}", [S, GB]) for p in range(2)]
        wnorm_e = [sb(f"wnorm_e{p}", [S, GB]) for p in range(2)]
        winv = [sb(f"winv{p}", [S, GB]) for p in range(2)]
        wscale = [sb(f"wscale{p}", [S, GB]) for p in range(2)]
        y = [sb(f"y{p}", [S, GB, D]) for p in range(2)]
        h = [sb(f"h{p}", [S, GB, D]) for p in range(2)]
        hb = [sb(f"hb{p}", [S, GB, D]) for p in range(2)]
        st1 = [sb(f"st1{p}", [S, GB, 6]) for p in range(2)]
        mv1 = [sb(f"mv1{p}", [S, GB, 2]) for p in range(2)]
        ve1 = [sb(f"ve1{p}", [S, GB]) for p in range(2)]
        rstd1 = [sb(f"rstd1{p}", [S, GB]) for p in range(2)]
        xn = [sb(f"xn{p}", [S, GB, D]) for p in range(2)]
        xnT = [sb(f"xnT{p}", [D, GT]) for p in range(2)]
        qT = [sb(f"qT{p}", [D, GT]) for p in range(2)]
        kT = [sb(f"kT{p}", [D, GT]) for p in range(2)]
        v = [sb(f"v{p}", [S, GB, D]) for p in range(2)]
        am = [sb(f"am{p}", [S, GB, S]) for p in range(2)]
        memT = [sb(f"memT{p}", [D, GT]) for p in range(2)]
        h2 = [sb(f"h2{p}", [S, GB, D]) for p in range(2)]
        st2 = [sb(f"st2{p}", [S, GB, 6]) for p in range(2)]
        mv2 = [sb(f"mv2{p}", [S, GB, 2]) for p in range(2)]
        ve2 = [sb(f"ve2{p}", [S, GB]) for p in range(2)]
        rstd2 = [sb(f"rstd2{p}", [S, GB]) for p in range(2)]
        rows = [sb(f"rows{p}", [S, GB, TOPK, RW]) for p in range(2)]
        x2T = [sb(f"x2T{p}", [D, GT]) for p in range(2)]
        lg = [sb(f"lg{p}", [S, GB, NE]) for p in range(2)]
        top = [sb(f"top{p}", [S, GB, 8]) for p in range(2)]
        topi = [sb(f"topi{p}", [S, GB, 8], U32) for p in range(2)]
        dlg = [sb(f"dlg{p}", [S, GB]) for p in range(2)]
        e2 = [sb(f"e2{p}", [S, GB]) for p in range(2)]
        e21 = [sb(f"e21{p}", [S, GB]) for p in range(2)]
        hot = [sb(f"hot{p}", [S, GB, TOPK, NE]) for p in range(2)]
        chosen = [sb(f"chosen{p}", [S, GB, NE]) for p in range(2)]
        place = [sb(f"place{p}", [S, GB, NE]) for p in range(2)]
        placek = [sb(f"placek{p}", [S, GB, TOPK, NE]) for p in range(2)]
        pos = [sb(f"pos{p}", [S, GB * TOPK], I32) for p in range(2)]
        start_at = [sb(f"start_at{p}", [D, NE]) for p in range(2)]

        wst = [sb(f"wst{q}", [D, RAW]) for q in range(2 * WPS)]

        groups_memory.close()
        held_by[0] = ctx
        wb = [sb(f"wb{k}", [D, KC, D]) for k in range(NBLK)]
        xr = [sb(f"xr{p}", [TS, D]) for p in range(2)]
        tag = [sb(f"tag{p}", [TS, 2]) for p in range(2)]
        u_in = [sb(f"u_in{p}", [D, TS]) for p in range(2)]
        th_in = sb("th_in", [D, TS])
        feat_in = [sb(f"feat_in{p}", [D, KC, TS]) for p in range(2)]
        dist_in = sb("dist_in", [D, NB, TS])
        z_in = sb("z_in", [D, NB, TS])
        a2_in = sb("a2_in", [D, NB, TS])
        z2_in = sb("z2_in", [D, NB, TS])
        u_mid = sb("u_mid", [D, 2, TS])
        th_mid = sb("th_mid", [D, 2, TS])
        feat_mid = [sb(f"feat_mid{p}", [D, KC, 2, TS]) for p in range(2)]
        dist_mid = sb("dist_mid", [D, NB, 2, TS])
        m_mid = sb("m_mid", [D, NB, 2, TS])
        a2_mid = sb("a2_mid", [D, NB, 2, TS])
        z2_mid = sb("z2_mid", [D, NB, 2, TS])
        g2 = sb("g2", [D, 2, TS])
        ye = [sb(f"ye{p}", [TS, D]) for p in range(2)]

        bank = [ps(f"bank{i}", [D, 512]) for i in range(8)]

        def tokens(b, n):
            return b[0:S, 0:GB * n].rearrange("p (b n) -> p b n", b=GB)

        conv_ps = [tokens(bank[p], D) for p in range(2)]
        xnT_ps = bank[2][:, 0:GT]
        at_ps = tokens(bank[2], S)
        qT_ps = bank[3][:, 0:GT]
        memT_ps = bank[3][:, 0:GT]
        kT_ps = bank[4][:, 0:GT]
        o_ps = tokens(bank[4], D)
        v_ps = tokens(bank[5], D)
        x2T_ps = bank[6][:, 0:GT]
        wsq_ps = bank[7][0:S, 0:GB]
        lg_ps = bank[6][0:S, 0:GB * NE].rearrange("p (b n) -> p b n", b=GB)
        place_ps = bank[6][:, 64:64 + (GB + 1) * NE].rearrange("p (b n) -> p b n", b=GB + 1)
        hid_ps = [[bank[2 * p + i][:, 0:2 * TS].rearrange("p (k n) -> p k n", k=2) for i in range(2)]
                  for p in range(2)]
        y_ps = [bank[4 + p][:, 0:D] for p in range(2)]
        xT_ps = [bank[6 + p][:, 0:TS] for p in range(2)]

        n_ld = sem("params_loaded")
        s = {n: sem(n) for n in (
            "x_squared", "sq_pairs", "sq_quads", "window_sums", "wsq_ready", "wnorm_ready",
            "wnorm_eps", "winv_ready", "wscale_ready", "conv_done", "tanh_done", "y_biased", "h_ready",
            "hb_ready", "stats1", "aggr1", "var1", "rstd1_ready", "xn_ready", "xnT_done", "xnT_ready",
            "qkv_done", "qT_ready", "kT_ready", "v_ready", "scores_done", "am_ready", "mem_done",
            "memT_ready", "o_done", "h2_ready", "stats2", "aggr2", "var2", "rstd2_ready",
            "x2_ready", "x2_copied", "ids_ready", "x2T_done", "x2T_ready", "logits_done", "lg_ready",
            "top_ready", "topi_ready", "dlg_ready", "e2_ready", "e21_ready", "gate1_ready",
            "gate2_ready", "hot_ready", "chosen_ready", "places_done",
            "place_ready", "placek_ready", "pos_ready", "start_ready",
            "w_scaled_up", "setup", "table", "pad_rows", "tables_ready",
            "pad_sent", "zeros_sent",
            "xT_done", "hidden_done", "g2_ready", "u_in_ready", "dist_in_ready", "z_in_ready", "th_in_ready",
            "a2_in_ready", "z2_in_ready", "x_in_ready", "y_in_ready", "silu_in_ready", "feat_in_ready",
            "u_mid_ready", "dist_mid_ready", "m_mid_ready", "th_mid_ready", "a2_mid_ready", "z2_mid_ready",
            "x_mid_ready", "y_mid_ready", "silu_mid_ready", "feat_mid_ready", "half_used",
            "ye_ready", "out_added", "pool_goes_on")}
        x_loaded = [sem(f"x_loaded{p}") for p in range(2)]
        h2_stored = [sem(f"h2_stored{p}") for p in range(2)]
        rows_sent = [sem(f"rows_sent{p}") for p in range(2)]
        row_loaded = [sem(f"row_loaded{p}") for p in range(2)]
        tag_loaded = [sem(f"tag_loaded{p}") for p in range(2)]
        w_loaded = [sem(f"w_loaded{q}") for q in range(2 * WPS)]
        w_stored = [sem(f"w_stored{q}") for q in range(2 * WPS)]
        blk_loaded = [sem(f"blk_loaded{k}") for k in range(NBLK)]

        def due(n):
            return not isinstance(n, int) or n > 0

        def nth(n, p, each=1):
            return 8 * each * (n - p + 2)

        NPARAM = 5

        def held(eng):
            eng.wait_ge(n_ld, 16 * NPARAM)

        def sp_group(sp, g, p):
            if due(g - 1):
                sp.wait_ge(s["conv_done"], g - 1)
            if due(g - 1):
                sp.wait_ge(s["x_squared"], g - 1)
            sp.dma_start(xs[p][:], x2[:, bass.ds(g * GB * L, GB * L)]).then_inc(x_loaded[p], 16)

        def sp_weights(sp, it, p):
            for i in range(WPS):
                n, q = it * WPS + i, p * WPS + i
                if isinstance(n, int) and n >= NWB:
                    break
                sp.wait_ge(s["w_scaled_up"], n + 1)
                sp.dma_start(w_scaled[bass.ds(n, 1)].rearrange("o p c -> (o p) c"),
                             wst[q][:, 0:BLK]).then_inc(w_stored[q], 16)
                if isinstance(n, int) and n + AHEAD >= NWB:
                    continue
                stores, r = divmod(q + AHEAD, 2 * WPS)
                left = 8 * (it - p) + 16 * stores
                if due(left):
                    sp.wait_ge(w_stored[r], left)
                sp.dma_start(wst[r][:], wraw[bass.ds(n + AHEAD, 1)].rearrange("o p c -> (o p) c")
                             ).then_inc(w_loaded[r], 16)

        def sp_h2(sp, g, p):
            sp.wait_ge(s["h2_ready"], g + 1)
            sp.dma_start(out[bass.ds(g * GT, GT)].rearrange("(b t) d -> t b d", b=GB), h2[p][:]
                         ).then_inc(h2_stored[p], 16)

        def dve_weight(dve, it, p, i):
            n, q = it * WPS + i, p * WPS + i
            if isinstance(n, int) and n >= NWB:
                return
            dve.wait_ge(w_loaded[q], 8 * (it - p) + 16)
            w3 = wst[q][:, 0:BLK].rearrange("p (c o) -> p c o", c=NB)
            scaler = wst[q][:, BLK:RAW].unsqueeze(1).broadcast_to([D, NB, D])
            nc.vector.scalar_tensor_tensor(w3, w3, 1.0 / 6.0, scaler, ALU.mult, ALU.mult
                                           ).then_inc(s["w_scaled_up"], 1)

        def pe_window(pe, g, p):
            pe.wait_ge(s["sq_quads"], g + 1)
            if due(g):
                pe.wait_ge(s["wsq_ready"], g)
            for b in range(GB):
                pe.matmul(wsq_ps[:, b:b + 1], xq4[p][:, b * L:b * L + S], const("ones")[:, 0:1],
                          start=True, stop=False)
                mm = pe.matmul(wsq_ps[:, b:b + 1], xq[p][0:C, b * L + K - 1:b * L + K - 1 + S],
                               const("ones")[0:C, 0:1], start=False, stop=True)
            mm.then_inc(s["window_sums"], 1)

        def pe_conv(pe, g, p, b):
            if b == 0:
                pe.wait_ge(x_loaded[p], nth(g, p))
                if due(g - 1):
                    pe.wait_ge(s["tanh_done"], g - 1)
            for j in range(TAPS2):
                n = 2 * C if j < TAPS2 - 1 else C
                mm = pe.matmul(conv_ps[p][:, b, :], xs[p][0:n, b * L + 2 * j:b * L + 2 * j + S],
                               wc[0:n, j * D:(j + 1) * D], start=(j == 0), stop=(j == TAPS2 - 1))
            if b == GB - 1:
                mm.then_inc(s["conv_done"], 1)

        def pe_xnT(pe, g, p):
            pe.wait_ge(s["xn_ready"], g + 1)
            if due(g):
                pe.wait_ge(s["am_ready"], g)
            for b in range(GB):
                mm = pe.transpose(xnT_ps[:, b * S:(b + 1) * S], xn[p][:, b, :], const("ident", S)[:, 0:S])
            mm.then_inc(s["xnT_done"], 1)

        def pe_qkv(pe, g, p):
            pe.wait_ge(s["xnT_ready"], g + 1)
            if due(g):
                pe.wait_ge(s["memT_ready"], g)
            pe.matmul(qT_ps, wa[:, 2 * D:3 * D], xnT[p][:], start=True, stop=True)
            if due(g):
                pe.wait_ge(s["h2_ready"], g)
            pe.matmul(kT_ps, wa[:, 0:D], xnT[p][:], start=True, stop=True)
            if due(g):
                pe.wait_ge(s["v_ready"], g)
            for b in range(GB):
                mm = pe.matmul(v_ps[:, b, :], xnT[p][:, b * S:(b + 1) * S], wa[:, D:2 * D],
                               start=True, stop=True)
            mm.then_inc(s["qkv_done"], 1)

        def pe_scores(pe, g, p):
            pe.wait_ge(s["qT_ready"], g + 1)
            pe.wait_ge(s["kT_ready"], g + 1)
            for b in range(GB):
                mm = pe.matmul(at_ps[:, b, :], kT[p][:, b * S:(b + 1) * S], qT[p][:, b * S:(b + 1) * S],
                               start=True, stop=True)
            mm.then_inc(s["scores_done"], 1)

        def pe_mem(pe, g, p):
            pe.wait_ge(s["am_ready"], g + 1)
            pe.wait_ge(s["v_ready"], g + 1)
            for b in range(GB):
                mm = pe.matmul(memT_ps[:, b * S:(b + 1) * S], v[p][:, b, :], am[p][:, b, :],
                               start=True, stop=True)
            mm.then_inc(s["mem_done"], 1)

        def pe_o(pe, g, p):
            pe.wait_ge(s["memT_ready"], g + 1)
            for b in range(GB):
                mm = pe.matmul(o_ps[:, b, :], memT[p][:, b * S:(b + 1) * S], wa[:, 3 * D:4 * D],
                               start=True, stop=True)
            mm.then_inc(s["o_done"], 1)

        def pe_x2T(pe, g, p):
            pe.wait_ge(s["x2_ready"], g + 1)
            if due(g):
                pe.wait_ge(s["start_ready"], g)
            for b in range(GB):
                mm = pe.transpose(x2T_ps[:, b * S:(b + 1) * S], rows[p][:, b, 0, 0:D],
                                  const("ident", S)[:, 0:S])
            mm.then_inc(s["x2T_done"], 1)

        def pe_logits(pe, g, p):
            pe.wait_ge(s["x2T_ready"], g + 1)
            for b in range(GB):
                mm = pe.matmul(lg_ps[:, b, :], x2T[p][:, b * S:(b + 1) * S], wg[:], start=True, stop=True)
            mm.then_inc(s["logits_done"], 1)

        def pe_places(pe, g, p):
            pe.wait_ge(s["chosen_ready"], g + 1)
            for b in range(GB):
                later = chosen[p][:, b, :].unsqueeze(1).broadcast_to([S, GB - b, NE])
                pe.matmul(place_ps[:, b + 1:, :], const("ones", S), later, start=(b == 0), stop=True,
                          skip_group_check=True)
            pe.matmul(place_ps[0:S, 0:GB, :], const("before", S), chosen[p][:], start=False, stop=True,
                      skip_group_check=True).then_inc(s["places_done"], 1)

        def act_square(act, g, p):
            act.wait_ge(x_loaded[p], nth(g, p))
            if due(g - 1):
                act.wait_ge(s["window_sums"], g - 1)
            if due(g - 1):
                act.wait_ge(s["sq_pairs"], g - 1)
            nc.scalar.activation(xq[p][:], xs[p][:], ACT.Square).then_inc(s["x_squared"], 1)

        def act_tanh(act, g, p):
            act.wait_ge(s["conv_done"], g + 1)
            act.wait_ge(s["wscale_ready"], g + 1)
            if due(g - 1):
                act.wait_ge(s["y_biased"], g - 1)
            for b in range(GB):
                a = nc.scalar.activation(y[p][:, b, :], conv_ps[p][:, b, :], ACT.Tanh,
                                         scale=wscale[p][:, b:b + 1])
            a.then_inc(s["tanh_done"], 1)

        def act_xnT(act, g, p):
            act.wait_ge(s["xnT_done"], g + 1)
            if due(g - 1):
                act.wait_ge(s["qkv_done"], g - 1)
            nc.scalar.activation(xnT[p][:], xnT_ps, ACT.Copy).then_inc(s["xnT_ready"], 1)

        def act_qk(act, g, p):
            act.wait_ge(s["qkv_done"], g + 1)
            if due(g - 1):
                act.wait_ge(s["scores_done"], g - 1)
            nc.scalar.activation(qT[p][:], qT_ps, ACT.Identity, bias=ba[:, 1:2]).then_inc(s["qT_ready"], 1)
            nc.scalar.activation(kT[p][:], kT_ps, ACT.Identity, bias=ba[:, 0:1]).then_inc(s["kT_ready"], 1)

        def act_memT(act, g, p):
            act.wait_ge(s["mem_done"], g + 1)
            if due(g - 1):
                act.wait_ge(s["o_done"], g - 1)
            nc.scalar.activation(memT[p][:], memT_ps, ACT.Copy).then_inc(s["memT_ready"], 1)

        def act_x2(act, g, p):
            act.wait_ge(s["x2_ready"], g + 1)
            if due(nth(g - 2, p, GB * TOPK)):
                act.wait_ge(rows_sent[p], nth(g - 2, p, GB * TOPK))
            nc.scalar.activation(rows[p][:, :, 1, 0:D], rows[p][:, :, 0, 0:D], ACT.Copy
                                 ).then_inc(s["x2_copied"], 1)

        def act_x2T(act, g, p):
            act.wait_ge(s["x2T_done"], g + 1)
            if due(g - 1):
                act.wait_ge(s["logits_done"], g - 1)
            nc.scalar.activation(x2T[p][:], x2T_ps, ACT.Copy).then_inc(s["x2T_ready"], 1)

        def act_e2(act, g, p):
            act.wait_ge(s["dlg_ready"], g + 1)
            if due(g - 1):
                act.wait_ge(s["gate2_ready"], g - 1)
            nc.scalar.activation(e2[p][:], dlg[p][:], ACT.Exp).then_inc(s["e2_ready"], 1)

        def pool_sq(pool, g, p):
            w2, w4 = GB * L - 2, GB * L - 6
            pool.wait_ge(s["x_squared"], g + 1)
            if due(g - 1):
                pool.wait_ge(s["sq_quads"], g - 1)
            pool.tensor_tensor(xq2[p][:, 0:w2], xq[p][:, 0:w2], xq[p][:, 2:w2 + 2], ALU.add
                               ).then_inc(s["sq_pairs"], 1)
            pool.wait_ge(s["sq_pairs"], g + 1)
            if due(g - 1):
                pool.wait_ge(s["window_sums"], g - 1)
            pool.tensor_tensor(xq4[p][:, 0:w4], xq2[p][:, 0:w4], xq2[p][:, 4:w4 + 4], ALU.add
                               ).then_inc(s["sq_quads"], 1)

        def pool_wnorm(pool, g, p):
            pool.wait_ge(s["wsq_ready"], g + 1)
            if due(g - 1):
                pool.wait_ge(s["wnorm_eps"], g - 1)
            pool.tensor_tensor(wnorm[p][:], wsq[p][:], const("half", S), ALU.pow).then_inc(s["wnorm_ready"], 1)

        def pool_bias(pool, g, p):
            pool.wait_ge(s["tanh_done"], g + 1)
            yb = const("b_tok", S).unsqueeze(1).broadcast_to([S, GB, D])
            pool.tensor_tensor(y[p][:], y[p][:], yb, ALU.add).then_inc(s["y_biased"], 1)

        def pool_rstd1(pool, g, p):
            pool.wait_ge(s["var1"], g + 1)
            if due(g - 1):
                pool.wait_ge(s["xn_ready"], g - 1)
            pool.tensor_tensor(rstd1[p][:], ve1[p][:], const("minushalf", S), ALU.pow
                               ).then_inc(s["rstd1_ready"], 1)

        def pool_hb(pool, g, p):
            pool.wait_ge(s["h_ready"], g + 1)
            if due(g - 1):
                pool.wait_ge(s["h2_ready"], g - 1)
            ob = const("b_o", S).unsqueeze(1).broadcast_to([S, GB, D])
            pool.tensor_tensor(hb[p][:], h[p][:], ob, ALU.add).then_inc(s["hb_ready"], 1)

        def pool_rstd2(pool, g, p):
            pool.wait_ge(s["var2"], g + 1)
            if due(g - 1):
                pool.wait_ge(s["x2_ready"], g - 1)
            pool.tensor_tensor(rstd2[p][:], ve2[p][:], const("minushalf", S), ALU.pow
                               ).then_inc(s["rstd2_ready"], 1)

        def pool_rows(pool, g, p):
            pool.wait_ge(s["pos_ready"], g + 1)
            pool.wait_ge(s["gate1_ready"], g + 1)
            pool.wait_ge(s["gate2_ready"], g + 1)
            pool.wait_ge(s["x2_ready"], g + 1)
            pool.wait_ge(s["x2_copied"], g + 1)
            pool.wait_ge(s["ids_ready"], g + 1)
            pool.sem_inc(s["pool_goes_on"], 1)
            for b in range(GB):
                for k in range(TOPK):
                    i = b * TOPK + k
                    pool.indirect_dma_start(routed, bass.IndirectOffsetOnAxis(pos[p][:, i:i + 1], 0),
                                            rows[p][:, b, k, :], None).then_inc(rows_sent[p], 16)

        def dve_wsq(dve, g, p):
            dve.wait_ge(s["window_sums"], g + 1)
            if due(g - 1):
                dve.wait_ge(s["wnorm_ready"], g - 1)
            nc.vector.tensor_scalar(wsq[p][:], wsq_ps, 0.0, None, ALU.max).then_inc(s["wsq_ready"], 1)

        def dve_wscale(dve, g, p):
            dve.wait_ge(s["wnorm_ready"], g + 1)
            nc.vector.tensor_scalar(wnorm_e[p][:], wnorm[p][:], EPS_TOK, None, ALU.add
                                    ).then_inc(s["wnorm_eps"], 1)
            dve.wait_ge(s["wnorm_eps"], g + 1)
            nc.vector.reciprocal(winv[p][:], wnorm_e[p][:]).then_inc(s["winv_ready"], 1)
            dve.wait_ge(s["winv_ready"], g + 1)
            if due(g - 1):
                dve.wait_ge(s["tanh_done"], g - 1)
            nc.vector.tensor_scalar(wscale[p][:], winv[p][:], 1.0, LAM_HALF, ALU.min, ALU.mult
                                    ).then_inc(s["wscale_ready"], 1)

        def dve_ln(dve, g, p, src, st, mv, ve, stats, aggr, var):
            for b in range(GB):
                i = nc.vector.bn_stats(st[p][:, b, :], src[p][:, b, :])
            i.then_inc(s[stats], 1)
            held(dve)
            dve.wait_ge(s[stats], g + 1)
            for b in range(GB):
                i = nc.vector.bn_aggr(mv[p][:, b, :], st[p][:, b, :])
            i.then_inc(s[aggr], 1)
            dve.wait_ge(s[aggr], g + 1)
            nc.vector.tensor_scalar(ve[p][:], mv[p][:, :, 1], EPS_LN, None, ALU.add).then_inc(s[var], 1)

        def dve_h(dve, g, p):
            dve.wait_ge(s["y_biased"], g + 1)
            if due(g - 1):
                dve.wait_ge(s["hb_ready"], g - 1)
            nc.vector.tensor_scalar(h[p][:], y[p][:], 0.0, None, ALU.max).then_inc(s["h_ready"], 1)
            dve.wait_ge(s["h_ready"], g + 1)
            if due(g - 1):
                dve.wait_ge(s["rstd1_ready"], g - 1)
            dve_ln(dve, g, p, h, st1, mv1, ve1, "stats1", "aggr1", "var1")

        def dve_xn(dve, g, p):
            dve.wait_ge(s["rstd1_ready"], g + 1)
            if due(g - 1):
                dve.wait_ge(s["xnT_done"], g - 1)
            for b in range(GB):
                i = nc.vector.tensor_scalar(xn[p][:, b, :], h[p][:, b, :], mv1[p][:, b, 0:1],
                                            rstd1[p][:, b:b + 1], ALU.subtract, ALU.mult)
            i.then_inc(s["xn_ready"], 1)

        def dve_v(dve, g, p):
            dve.wait_ge(s["qkv_done"], g + 1)
            if due(g - 1):
                dve.wait_ge(s["mem_done"], g - 1)
            nc.vector.tensor_tensor(v[p][:], v_ps, const("b_v", S).unsqueeze(1).broadcast_to([S, GB, D]),
                                    ALU.add).then_inc(s["v_ready"], 1)

        def dve_am(dve, g, p):
            dve.wait_ge(s["scores_done"], g + 1)
            if due(g - 1):
                dve.wait_ge(s["mem_done"], g - 1)
            nc.vector.tensor_tensor(am[p][:], at_ps, const("decay", S).unsqueeze(1).broadcast_to([S, GB, S]),
                                    ALU.mult).then_inc(s["am_ready"], 1)

        def dve_h2(dve, g, p):
            dve.wait_ge(s["o_done"], g + 1)
            dve.wait_ge(s["hb_ready"], g + 1)
            if due(nth(g - 2, p)):
                dve.wait_ge(h2_stored[p], nth(g - 2, p))
            nc.vector.tensor_tensor(h2[p][:], o_ps, hb[p][:], ALU.add).then_inc(s["h2_ready"], 1)
            dve.wait_ge(s["h2_ready"], g + 1)
            if due(g - 1):
                dve.wait_ge(s["rstd2_ready"], g - 1)
            dve_ln(dve, g, p, h2, st2, mv2, ve2, "stats2", "aggr2", "var2")

        def dve_x2(dve, g, p):
            dve.wait_ge(s["rstd2_ready"], g + 1)
            if due(nth(g - 2, p, GB * TOPK)):
                dve.wait_ge(rows_sent[p], nth(g - 2, p, GB * TOPK))
            if due(g - 1):
                dve.wait_ge(s["x2T_done"], g - 1)
            for b in range(GB):
                i = nc.vector.tensor_scalar(rows[p][:, b, 0, 0:D], h2[p][:, b, :], mv2[p][:, b, 0:1],
                                            rstd2[p][:, b:b + 1], ALU.subtract, ALU.mult)
            i.then_inc(s["x2_ready"], 1)
            ids = rows[p][:].bitcast(I32)[:, :, :, D + 1]
            tok = cst[0:S, bass.ds(_cols["token"][0] + g * GB, GB)]
            for k in range(TOPK):
                i = nc.vector.tensor_copy(ids[:, :, k], tok)
            i.then_inc(s["ids_ready"], 1)

        def dve_logits(dve, g, p):
            dve.wait_ge(s["logits_done"], g + 1)
            if due(g - 1):
                dve.wait_ge(s["topi_ready"], g - 1)
            nc.vector.tensor_copy(lg[p][:], lg_ps).then_inc(s["lg_ready"], 1)

        def dve_max(dve, g, p):
            held(dve)
            dve.wait_ge(s["lg_ready"], g + 1)
            for b in range(GB):
                i = nc.vector.max(top[p][:, b, :], lg[p][:, b, :])
            i.then_inc(s["top_ready"], 1)

        def dve_index(dve, g, p):
            dve.wait_ge(s["top_ready"], g + 1)
            nc.vector.tensor_tensor(dlg[p][:], top[p][:, :, 1], top[p][:, :, 0], ALU.subtract
                                    ).then_inc(s["dlg_ready"], 1)
            if due(g - 1):
                held(dve)
                dve.wait_ge(s["hot_ready"], g - 1)
            for b in range(GB):
                i = nc.vector.max_index(topi[p][:, b, :], top[p][:, b, :], lg[p][:, b, :])
            i.then_inc(s["topi_ready"], 1)

        def dve_hot(dve, g, p):
            dve.wait_ge(s["topi_ready"], g + 1)
            if due(g - 1):
                dve.wait_ge(s["placek_ready"], g - 1)
            shape = [S, GB, TOPK, NE]
            nc.vector.tensor_tensor(hot[p][:], const("expert", S).unsqueeze(1).unsqueeze(1).broadcast_to(shape),
                                    topi[p][:, :, 0:TOPK].unsqueeze(3).broadcast_to(shape), ALU.is_equal
                                    ).then_inc(s["hot_ready"], 1)

        def dve_chosen(dve, g, p):
            dve.wait_ge(s["hot_ready"], g + 1)
            if due(g - 1):
                dve.wait_ge(s["places_done"], g - 1)
            nc.vector.tensor_tensor(chosen[p][:], hot[p][:, :, 0, :], hot[p][:, :, 1, :], ALU.add
                                    ).then_inc(s["chosen_ready"], 1)

        def dve_gates(dve, g, p):
            dve.wait_ge(s["e2_ready"], g + 1)
            nc.vector.tensor_scalar(e21[p][:], e2[p][:], 1.0, None, ALU.add).then_inc(s["e21_ready"], 1)
            dve.wait_ge(s["e21_ready"], g + 1)
            nc.vector.reciprocal(rows[p][:, :, 0, D], e21[p][:]).then_inc(s["gate1_ready"], 1)
            dve.wait_ge(s["gate1_ready"], g + 1)
            nc.vector.tensor_tensor(rows[p][:, :, 1, D], e2[p][:], rows[p][:, :, 0, D], ALU.mult
                                    ).then_inc(s["gate2_ready"], 1)

        def dve_place(dve, g, p):
            dve.wait_ge(s["places_done"], g + 1)
            nc.vector.tensor_tensor(place[p][:], place_ps[0:S, 0:GB, :],
                                    start_at[p][0:S].unsqueeze(1).broadcast_to([S, GB, NE]), ALU.add
                                    ).then_inc(s["place_ready"], 1)
            nc.vector.tensor_tensor(start_at[1 - p][:], place_ps[:, GB, :], start_at[p][:], ALU.add
                                    ).then_inc(s["start_ready"], 1)

        def dve_rows(dve, g, p):
            dve.wait_ge(s["place_ready"], g + 1)
            nc.vector.tensor_tensor(placek[p][:], hot[p][:],
                                    place[p][:].unsqueeze(2).broadcast_to([S, GB, TOPK, NE]), ALU.mult
                                    ).then_inc(s["placek_ready"], 1)
            dve.wait_ge(s["placek_ready"], g + 1)
            if due(g - 1):
                dve.wait_ge(rows_sent[p], nth(g - 2, p, GB * TOPK))
            nc.vector.tensor_reduce(pos[p][:], placek[p][:].rearrange("p b k e -> p (b k) e"), AX.X, ALU.max
                                    ).then_inc(s["pos_ready"], 1)

        def steps(engine_step, eng):
            n = NG
            engine_step(0, 0, None, None)
            engine_step(1, 1, 0, None)
            engine_step(0, 2, 1, 0)
            engine_step(1, 3, 2, 1)
            with eng.Fori(2, n // 2) as j:
                engine_step(0, j * 2, j * 2 - 1, j * 2 - 2)
                engine_step(1, j * 2 + 1, j * 2, j * 2 - 1)
            engine_step(0, None, n - 1, n - 2)
            engine_step(1, None, None, n - 1)

        block = ctx.enter_context(nc.Block())

        @block.sync
        def _(sp):
            sp.dma_start(cst[:], consts).then_inc(n_ld, 16)
            sp.dma_start(wc[:], wconv).then_inc(n_ld, 16)
            sp.dma_start(wa[:], wattn).then_inc(n_ld, 16)
            sp.dma_start(ba[:], battn).then_inc(n_ld, 16)
            sp.dma_start(wg[:], wgate).then_inc(n_ld, 16)

            def step(it, p):
                def has(g):
                    return not isinstance(g, int) or 0 <= g < NG

                if has(it + 1):
                    sp_group(sp, it + 1, 1 - p)
                if has(it - 2):
                    sp_h2(sp, it - 2, p)
                sp_weights(sp, it, p)

            sp_group(sp, 0, 0)
            for n in range(AHEAD):
                sp.dma_start(wst[n][:], wraw[n]).then_inc(w_loaded[n], 16)
            for it in range(3):
                step(it, it % 2)
            with sp.Fori(1, NG // 2 - 1) as j:
                step(j * 2 + 1, 1)
                step(j * 2 + 2, 0)
            for it in range(NG - 1, NSTEP):
                step(it, it % 2)
            sp.wait_ge(s["pad_rows"], 1)
            for e in range(NE):
                r = sp.value_load(pad_at[0:1, e:e + 1], min_val=0, max_val=NE * REG)
                sp.dma_start(routed[bass.ds(r, TS)], padrow[:]).then_inc(s["pad_sent"], 16)
            for q in range(2 * WPS):
                sp.wait_ge(w_stored[q], 16 * len(range(q, NWB, 2 * WPS)))
            sp.wait_ge(s["tables_ready"], 1)

            def load_rows(t, p):
                if due(t - 1):
                    sp.wait_ge(s["xT_done"], t - 1)
                r = sp.value_load(tile_row[0:1, bass.ds(t, 1)], min_val=0, max_val=NE * REG)
                sp.dma_start(xr[p][:], routed[bass.ds(r, TS), 0:D]).then_inc(row_loaded[p], 16)

            def load_block(k, blk, new):
                for src, dst in ((w_scaled, wb[k][:, 0:NB]), (wbase, wb[k][:, NB:KC])):
                    src = src[bass.ds(blk + k, 1)].rearrange("o p c -> (o p) c")
                    dst = dst.rearrange("p c o -> p (c o)")
                    if new is None:
                        sp.dma_start(dst, src).then_inc(blk_loaded[k], 16)
                    else:
                        sp.dma_start(dst, src, cond=(new > 0)).then_inc(blk_loaded[k], 16)

            def tile_info(t):
                return (sp.value_load(tile_blk[0:1, bass.ds(t, 1)], min_val=0, max_val=(NE - 1) * NBLK),
                        sp.value_load(tile_new[0:1, bass.ds(t, 1)], min_val=0, max_val=1))

            blk0 = sp.value_load(tile_blk[0:1, 0:1], min_val=0, max_val=(NE - 1) * NBLK)
            load_block(0, blk0, None)
            for p in range(2):
                sp.wait_ge(rows_sent[p], nth(NG - 2 + p, p, GB * TOPK))
            sp.wait_ge(s["pad_sent"], 16 * NE)
            sp.wait_ge(s["zeros_sent"], 32)
            load_rows(0, 0)
            load_rows(1, 1)
            load_block(1, blk0, None)
            load_rows(2, 0)
            for k in range(2, NBLK):
                load_block(k, blk0, None)

            def first_blocks(t):
                blk, new = tile_info(t)
                for k in range(4):
                    sp.wait_ge(s["hidden_done"], 4 * (t - 1) + k + 1)
                    load_block(k, blk, new)

            def last_blocks(t):
                blk, new = tile_info(t)
                for k in range(4, NBLK):
                    sp.wait_ge(s["half_used"], 2 * (t - 1) + k - 3)
                    load_block(k, blk, new)

            for t in range(1, 4):
                load_rows(t + 2, t % 2)
                first_blocks(t)
            with sp.Fori(2, NT // 2 - 1) as j:
                for p in range(2):
                    load_rows(j * 2 + p + 2, p)
                    last_blocks(j * 2 + p - 3)
                    first_blocks(j * 2 + p)
            last_blocks(NT - 5)
            first_blocks(NT - 2)
            last_blocks(NT - 4)
            first_blocks(NT - 1)
            for t in range(NT - 3, NT):
                last_blocks(t)
            for k in range(NBLK):
                sp.wait_ge(blk_loaded[k], 32 * NT)
            for p in range(2):
                sp.wait_ge(h2_stored[p], nth(NG - 2 + p, p))

        @block.tensor
        def _(pe):
            pe.wait_ge(n_ld, 16 * NPARAM)

            def step(par, g1, g2_, g3):
                if g1 is not None:
                    pe_conv(pe, g1, par, 0)
                    pe_conv(pe, g1, par, 1)
                if g2_ is not None:
                    pe_xnT(pe, g2_, 1 - par)
                if g1 is not None:
                    pe_window(pe, g1, par)
                if g2_ is not None:
                    pe_qkv(pe, g2_, 1 - par)
                if g3 is not None:
                    pe_x2T(pe, g3, par)
                if g1 is not None:
                    pe_conv(pe, g1, par, 2)
                if g3 is not None:
                    pe_logits(pe, g3, par)
                if g1 is not None:
                    pe_conv(pe, g1, par, 3)
                if g2_ is not None:
                    pe_scores(pe, g2_, 1 - par)
                if g3 is not None:
                    pe_places(pe, g3, par)
                if g2_ is not None:
                    pe_mem(pe, g2_, 1 - par)
                    pe_o(pe, g2_, 1 - par)

            steps(step, pe)

            def turn_x(t, p):
                pe.wait_ge(row_loaded[p], nth(t, p))
                if due(t - 1):
                    pe.wait_ge(s["u_in_ready"], t - 1)
                pe.transpose(xT_ps[p], xr[p][:], const("ident")).then_inc(s["xT_done"], 1)

            def hidden(t, p):
                pe.wait_ge(s["feat_in_ready"], t + 1)
                pe.wait_ge(s["silu_in_ready"], t + 1)
                if due(t - 1):
                    pe.wait_ge(s["u_mid_ready"], t - 1)
                for k in range(4):
                    pe.wait_ge(blk_loaded[k], 32 * (t + 1))
                    for c in range(KC):
                        mm = pe.matmul(hid_ps[p][k // 2][:, k % 2, :], wb[k][:, c, :], feat_in[p][:, c, :],
                                       start=(c == 0), stop=(c == KC - 1))
                    mm.then_inc(s["hidden_done"], 1)

            def last_layer(t, p):
                pe.wait_ge(s["feat_mid_ready"], t + 1)
                pe.wait_ge(s["silu_mid_ready"], t + 1)
                if due(t - 1):
                    pe.wait_ge(s["ye_ready"], t - 1)
                for f in range(2):
                    pe.wait_ge(blk_loaded[4 + f], 32 * (t + 1))
                    for c in range(KC):
                        mm = pe.matmul(y_ps[p], feat_mid[p][:, c, f, :], wb[4 + f][:, c, :],
                                       start=(f == 0 and c == 0), stop=(f == 1 and c == KC - 1))
                    mm.then_inc(s["half_used"], 1)

            def tile_step(t, p):
                turn_x(t + 2, p)
                if due(t - 2):
                    last_layer(t - 3, 1 - p)
                hidden(t, p)

            turn_x(0, 0)
            turn_x(1, 1)
            for t in range(4):
                tile_step(t, t % 2)
            with pe.Fori(2, NT // 2 - 1) as j:
                tile_step(j * 2, 0)
                tile_step(j * 2 + 1, 1)
            for t in range(NT - 2, NT):
                last_layer(t - 3, (t - 3) % 2)
                hidden(t, t % 2)
            for t in range(NT - 3, NT):
                last_layer(t, t % 2)

        @block.scalar
        def _(act):
            act.wait_ge(n_ld, 16 * NPARAM)

            def step(par, g1, g2_, g3):
                if g1 is not None:
                    act_square(act, g1, par)
                if g2_ is not None:
                    act_xnT(act, g2_, 1 - par)
                    act_qk(act, g2_, 1 - par)
                if g3 is not None:
                    act_x2T(act, g3, par)
                    act_x2(act, g3, par)
                if g1 is not None:
                    act_tanh(act, g1, par)
                if g3 is not None:
                    act_e2(act, g3, par)
                if g2_ is not None:
                    act_memT(act, g2_, 1 - par)

            steps(step, act)

            def turn(t, p):
                act.wait_ge(s["xT_done"], t + 1)
                if due(t - 1):
                    act.wait_ge(s["silu_in_ready"], t - 1)
                nc.scalar.activation(u_in[p][:], xT_ps[p], ACT.Copy, scale=0.5).then_inc(s["u_in_ready"], 1)

            def distances(u, dist):
                for i in range(NB):
                    a = nc.scalar.activation(dist[:, i], u[:], ACT.Abs, scale=2.0 / H_GRID,
                                             bias=1.0 / H_GRID - (i - 1))
                return a

            def start_in(t, p):
                act.wait_ge(s["u_in_ready"], t + 1)
                if due(t):
                    act.wait_ge(s["z_in_ready"], t)
                distances(u_in[p], dist_in).then_inc(s["dist_in_ready"], 1)
                if due(t):
                    act.wait_ge(s["silu_in_ready"], t)
                nc.scalar.activation(th_in[:], u_in[p][:], ACT.Tanh).then_inc(s["th_in_ready"], 1)
                act.wait_ge(s["dist_in_ready"], t + 1)
                if due(t):
                    act.wait_ge(s["y_in_ready"], t)
                nc.scalar.activation(z_in[:], dist_in[:], ACT.Relu, scale=-1.0, bias=2.0
                                     ).then_inc(s["z_in_ready"], 1)

            def squares_in(t):
                act.wait_ge(s["z_in_ready"], t + 1)
                if due(t):
                    act.wait_ge(s["feat_in_ready"], t)
                nc.scalar.activation(a2_in[:], z_in[:], ACT.Square, scale=-ROOT3, bias=2 * ROOT3
                                     ).then_inc(s["a2_in_ready"], 1)
                nc.scalar.activation(z2_in[:], z_in[:], ACT.Square).then_inc(s["z2_in_ready"], 1)

            def half_of_h2(t, p):
                act.wait_ge(s["hidden_done"], 4 * t + 4)
                if due(t):
                    act.wait_ge(s["u_mid_ready"], t)
                nc.scalar.activation(g2[:], hid_ps[p][1], ACT.Copy, scale=0.5).then_inc(s["g2_ready"], 1)

            def start_mid(t):
                act.wait_ge(s["u_mid_ready"], t + 1)
                if due(t):
                    act.wait_ge(s["m_mid_ready"], t)
                distances(u_mid, dist_mid).then_inc(s["dist_mid_ready"], 1)
                if due(t):
                    act.wait_ge(s["silu_mid_ready"], t)
                nc.scalar.activation(th_mid[:], u_mid[:], ACT.Tanh).then_inc(s["th_mid_ready"], 1)

            def squares_mid(t):
                act.wait_ge(s["m_mid_ready"], t + 1)
                if due(t):
                    act.wait_ge(s["feat_mid_ready"], t)
                nc.scalar.activation(a2_mid[:], m_mid[:], ACT.Square, scale=ROOT3, bias=2 * ROOT3
                                     ).then_inc(s["a2_mid_ready"], 1)
                nc.scalar.activation(z2_mid[:], m_mid[:], ACT.Square).then_inc(s["z2_mid_ready"], 1)

            def gated(t, p):
                act.wait_ge(s["half_used"], 2 * t + 2)
                act.wait_ge(tag_loaded[p], nth(t, p))
                if due(t - 1):
                    act.wait_ge(s["out_added"], 16 * (t - 1))
                nc.scalar.activation(ye[p][:], y_ps[p], ACT.Copy, scale=tag[p][:, 0:1]
                                     ).then_inc(s["ye_ready"], 1)

            def tile_step(t, p):
                if due(t):
                    half_of_h2(t - 1, 1 - p)
                if due(t - 1):
                    squares_mid(t - 2)
                if due(t):
                    start_mid(t - 1)
                if not isinstance(t, int) or t + 2 < NT:
                    turn(t + 2, p)
                    start_in(t + 2, p)
                    squares_in(t + 2)
                if due(t - 2):
                    gated(t - 3, 1 - p)

            for t in range(2):
                turn(t, t)
                start_in(t, t)
                squares_in(t)
            for t in range(4):
                tile_step(t, t % 2)
            with act.Fori(2, NT // 2 - 1) as j:
                tile_step(j * 2, 0)
                tile_step(j * 2 + 1, 1)
            tile_step(NT - 2, 0)
            tile_step(NT - 1, 1)
            half_of_h2(NT - 1, 1)
            squares_mid(NT - 2)
            start_mid(NT - 1)
            gated(NT - 3, 1)
            squares_mid(NT - 1)
            gated(NT - 2, 0)
            gated(NT - 1, 1)

        @block.gpsimd
        def _(pool):
            pool.wait_ge(n_ld, 16 * NPARAM)

            def step(par, g1, g2_, g3):
                if g1 is not None:
                    pool_sq(pool, g1, par)
                if g3 is not None:
                    pool_rstd2(pool, g3, par)
                if g1 is not None:
                    pool_wnorm(pool, g1, par)
                if g3 is not None and due(g3):
                    pool_rows(pool, g3 - 1, 1 - par)
                if g1 is not None:
                    pool_bias(pool, g1, par)
                    pool_hb(pool, g1, par)
                    pool_rstd1(pool, g1, par)

            pool.wait_ge(s["setup"], 6)
            pool.dma_start(routed[NE * REG:NE * REG + TS], padrow[:]).then_inc(s["zeros_sent"], 16)
            pool.dma_start(out[TOK:TOK + TS], padrow[:, 0:D]).then_inc(s["zeros_sent"], 16)
            steps(step, pool)
            pool_rows(pool, NG - 1, (NG - 1) % 2)
            pool.wait_ge(s["zeros_sent"], 32)
            for p in range(2):
                pool.wait_ge(h2_stored[p], nth(NG - 2 + p, p))

            def add(t, p):
                pool.wait_ge(s["ye_ready"], t + 1)
                if due(t):
                    pool.wait_ge(s["out_added"], 16 * t)
                pool.sem_inc(s["pool_goes_on"], 1)
                pool.indirect_dma_start(out, bass.IndirectOffsetOnAxis(tag[p][:, 1:2].bitcast(I32), 0),
                                        ye[p][:], None, compute_op=ALU.add).then_inc(s["out_added"], 16)

            def load_tags(t, p):
                r = pool.value_load(tile_row[0:1, bass.ds(t, 1)], min_val=0, max_val=NE * REG)
                if due(t - 1):
                    pool.wait_ge(s["out_added"], 16 * (t - 1))
                pool.sem_inc(s["pool_goes_on"], 1)
                pool.dma_start(tag[p][:], routed[bass.ds(r, TS), D:RW]).then_inc(tag_loaded[p], 16)

            for i in range(2):
                pool.wait_ge(rows_sent[i], nth(NG - 2 + i, i, GB * TOPK))
            pool.wait_ge(s["pad_sent"], 16 * NE)
            pool.wait_ge(s["tables_ready"], 1)
            load_tags(0, 0)
            load_tags(1, 1)
            add(0, 0)
            load_tags(2, 0)
            add(1, 1)
            load_tags(3, 1)
            with pool.Fori(1, NT // 2 - 1) as j:
                for p in range(2):
                    add(j * 2 + p, p)
                    load_tags(j * 2 + p + 2, p)
            add(NT - 2, 0)
            add(NT - 1, 1)
            pool.wait_ge(s["out_added"], 16 * NT)

        @block.vector
        def _(dve):
            dve.wait_ge(n_ld, 16 * NPARAM)
            nc.vector.tensor_copy(start_at[0][:], const("region")).then_inc(s["setup"], 1)
            nc.vector.memset(padrow[:, 0:D + 1], 0.0).then_inc(s["setup"], 1)
            nc.vector.tensor_copy(padrow[:].bitcast(I32)[:, D + 1:D + 2], const("dump")).then_inc(s["setup"], 1)
            nc.vector.memset(expert9[:, NE:NE + 1], float(NE)).then_inc(s["setup"], 1)
            nc.vector.tensor_copy(expert9[:, 0:NE], const("expert", 1)).then_inc(s["setup"], 1)
            nc.vector.memset(base[:, NE:NE + 1], 0.0).then_inc(s["setup"], 1)
            dve.wait_ge(s["setup"], 6)

            def step(par, g1, g2_, g3):
                def weight(i):
                    dve_weight(dve, g1 if g1 is not None else NG + par, par, i)

                if g1 is not None:
                    dve_wsq(dve, g1, par)
                if g3 is not None:
                    dve_x2(dve, g3, par)
                weight(0)
                if g1 is not None:
                    dve_wscale(dve, g1, par)
                weight(1)
                if g2_ is not None:
                    dve_v(dve, g2_, 1 - par)
                weight(2)
                if g3 is not None:
                    dve_logits(dve, g3, par)
                    dve_max(dve, g3, par)
                    dve_index(dve, g3, par)
                if g2_ is not None:
                    dve_am(dve, g2_, 1 - par)
                if g3 is not None:
                    dve_hot(dve, g3, par)
                    dve_chosen(dve, g3, par)
                    dve_gates(dve, g3, par)
                weight(3)
                if g3 is not None:
                    dve_place(dve, g3, par)
                if g1 is not None:
                    dve_h(dve, g1, par)
                if g3 is not None:
                    dve_rows(dve, g3, par)
                if g1 is not None:
                    dve_xn(dve, g1, par)
                if g2_ is not None:
                    dve_h2(dve, g2_, 1 - par)
                weight(4)

            steps(step, dve)

            done = [0]

            def link(i):
                i.then_inc(s["table"], 1)
                done[0] += 1
                dve.wait_ge(s["table"], done[0])

            dve.wait_ge(s["start_ready"], NG)
            nc.vector.tensor_copy(pad_at[:], start_at[0][0:1]).then_inc(s["pad_rows"], 1)
            link(nc.vector.tensor_tensor(count[:], start_at[0][:], const("region"), ALU.subtract))
            link(nc.vector.tensor_scalar(cnt_i[:], count[:], float(TS - 1), None, ALU.add))
            link(nc.vector.tensor_scalar(nt_i[:], cnt_i[:], TS.bit_length() - 1, None, ALU.logical_shift_right))
            link(nc.vector.tensor_copy(nt_f[:], nt_i[:]))
            link(nc.vector.tensor_copy(end_a[:], nt_f[:]))
            a, b = end_a, end_b
            for d in (1, 2, 4):
                link(nc.vector.tensor_copy(b[:, 0:d], a[:, 0:d]))
                link(nc.vector.tensor_tensor(b[:, d:NE], a[:, d:NE], a[:, 0:NE - d], ALU.add))
                a, b = b, a
            end = a
            link(nc.vector.tensor_tensor(first[:], end[:], nt_f[:], ALU.subtract))
            link(nc.vector.scalar_tensor_tensor(base[:, 0:NE], first[:], -float(TS), const("region"),
                                                ALU.mult, ALU.add))
            tiles = const("tile", 1)
            n1 = NT + 1
            link(nc.vector.tensor_tensor(past[:], tiles.unsqueeze(2).broadcast_to([1, n1, NE]),
                                         end[0:1].unsqueeze(1).broadcast_to([1, n1, NE]), ALU.is_ge))
            link(nc.vector.tensor_reduce(past_n[:], past[:], AX.X, ALU.add))
            link(nc.vector.tensor_tensor(is_e[:], expert9[:].unsqueeze(1).broadcast_to([1, n1, NE + 1]),
                                         past_n[:].unsqueeze(2).broadcast_to([1, n1, NE + 1]), ALU.is_equal))
            link(nc.vector.tensor_tensor(rs_e[:], is_e[:], base[0:1].unsqueeze(1).broadcast_to([1, n1, NE + 1]),
                                         ALU.mult))
            link(nc.vector.scalar_tensor_tensor(rs_e[:, :, NE], tiles, -float(TS), is_e[:, :, NE],
                                                ALU.mult, ALU.mult))
            link(nc.vector.scalar_tensor_tensor(rs_e[:, :, NE], is_e[:, :, NE], float(NE * REG),
                                                rs_e[:, :, NE], ALU.mult, ALU.add))
            link(nc.vector.tensor_reduce(rs_f[:], rs_e[:], AX.X, ALU.add))
            link(nc.vector.scalar_tensor_tensor(rs_f[:], tiles, float(TS), rs_f[:], ALU.mult, ALU.add))
            link(nc.vector.tensor_copy(tile_row[:], rs_f[:]))
            link(nc.vector.tensor_scalar(eidx[:], past_n[:], float(NE - 1), float(NBLK), ALU.min, ALU.mult))
            link(nc.vector.tensor_copy(tile_blk[:], eidx[:]))
            link(nc.vector.memset(tile_new[:, 0:1], 1))
            nc.vector.tensor_tensor(tile_new[:, 1:n1], eidx[:, 1:n1], eidx[:, 0:n1 - 1], ALU.not_equal
                                    ).then_inc(s["tables_ready"], 1)

            def silu(th, u, feat):
                return nc.vector.scalar_tensor_tensor(feat, th, 1.0, u, ALU.add, ALU.mult)

            def finish_in(t, p):
                dve.wait_ge(s["a2_in_ready"], t + 1)
                nc.vector.tensor_tensor(a2_in[:], a2_in[:], z_in[:], ALU.mult).then_inc(s["x_in_ready"], 1)
                dve.wait_ge(s["z2_in_ready"], t + 1)
                nc.vector.tensor_tensor(z2_in[:], z2_in[:], z_in[:], ALU.mult).then_inc(s["y_in_ready"], 1)
                dve.wait_ge(s["th_in_ready"], t + 1)
                if due(t - 1):
                    dve.wait_ge(s["hidden_done"], 4 * (t - 1))
                silu(th_in[:], u_in[p][:], feat_in[p][:, NB]).then_inc(s["silu_in_ready"], 1)
                dve.wait_ge(s["x_in_ready"], t + 1)
                dve.wait_ge(s["y_in_ready"], t + 1)
                nc.vector.scalar_tensor_tensor(feat_in[p][:, 0:NB], a2_in[:], 4.0, z2_in[:], ALU.subtract,
                                               ALU.min, reverse0=True).then_inc(s["feat_in_ready"], 1)

            def product(t, p):
                dve.wait_ge(s["g2_ready"], t + 1)
                if due(t):
                    dve.wait_ge(s["silu_mid_ready"], t)
                nc.vector.tensor_tensor(u_mid[:], hid_ps[p][0], g2[:], ALU.mult).then_inc(s["u_mid_ready"], 1)

            def silu_mid(t, p):
                dve.wait_ge(s["th_mid_ready"], t + 1)
                if due(t - 1):
                    dve.wait_ge(s["half_used"], 2 * (t - 1))
                silu(th_mid[:], u_mid[:], feat_mid[p][:, NB]).then_inc(s["silu_mid_ready"], 1)

            def cut_mid(t):
                dve.wait_ge(s["dist_mid_ready"], t + 1)
                nc.vector.tensor_scalar(m_mid[:], dist_mid[:], 2.0, 2.0, ALU.min, ALU.subtract
                                        ).then_inc(s["m_mid_ready"], 1)

            def cubes_mid(t):
                dve.wait_ge(s["a2_mid_ready"], t + 1)
                nc.vector.tensor_tensor(a2_mid[:], a2_mid[:], m_mid[:], ALU.mult).then_inc(s["x_mid_ready"], 1)
                dve.wait_ge(s["z2_mid_ready"], t + 1)
                nc.vector.scalar_tensor_tensor(z2_mid[:], z2_mid[:], -1.0, m_mid[:], ALU.mult, ALU.mult
                                               ).then_inc(s["y_mid_ready"], 1)

            def bases_mid(t, p):
                dve.wait_ge(s["x_mid_ready"], t + 1)
                dve.wait_ge(s["y_mid_ready"], t + 1)
                nc.vector.scalar_tensor_tensor(feat_mid[p][:, 0:NB], a2_mid[:], 4.0, z2_mid[:], ALU.add, ALU.min
                                               ).then_inc(s["feat_mid_ready"], 1)

            def tile_step(t, p):
                if not isinstance(t, int) or t + 1 < NT:
                    finish_in(t + 1, 1 - p)
                if due(t):
                    product(t - 1, 1 - p)
                if due(t - 1):
                    cubes_mid(t - 2)
                if due(t):
                    silu_mid(t - 1, 1 - p)
                if due(t - 1):
                    bases_mid(t - 2, p)
                if due(t):
                    cut_mid(t - 1)

            finish_in(0, 0)
            for t in range(4):
                tile_step(t, t % 2)
            with dve.Fori(2, NT // 2 - 1) as j:
                tile_step(j * 2, 0)
                tile_step(j * 2 + 1, 1)
            tile_step(NT - 2, 0)
            tile_step(NT - 1, 1)
            product(NT - 1, 1)
            cubes_mid(NT - 2)
            silu_mid(NT - 1, 1)
            bases_mid(NT - 2, 0)
            cut_mid(NT - 1)
            cubes_mid(NT - 1)
            bases_mid(NT - 1, 1)


def kernel(x, L0_tok_kernel, L0_tok_bias, L0_attn_Wk, L0_attn_bk, L0_attn_Wv, L0_attn_bv, L0_attn_Wq, L0_attn_bq,
           L0_attn_Wo, L0_attn_bo, L0_ffn_gate_w, L0_ffn_base_w1, L0_ffn_spline_w1, L0_ffn_scaler_w1,
           L0_ffn_base_w2, L0_ffn_spline_w2, L0_ffn_scaler_w2, L0_ffn_base_w3, L0_ffn_spline_w3,
           L0_ffn_scaler_w3):
    import concourse.bacc as bacc
    from concourse.bass_utils import run_bass_kernel_spmd

    xt = np.asarray(x).transpose(2, 0, 1).reshape(C, B * L)
    x2 = np.zeros((2 * C, B * L), xt.dtype)
    x2[:C] = xt
    x2[C:, :-1] = xt[:, 1:]
    taps = np.zeros((2 * TAPS2, C, D), xt.dtype)
    taps[:K] = np.asarray(L0_tok_kernel)
    wconv = taps.reshape(TAPS2, 2 * C, D).transpose(1, 0, 2).reshape(2 * C, TAPS2 * D)
    wattn = np.concatenate([np.asarray(w) for w in (L0_attn_Wk, L0_attn_Wv, L0_attn_Wq, L0_attn_Wo)], axis=1)
    battn = np.stack([np.asarray(L0_attn_bk), np.asarray(L0_attn_bq)], axis=1)
    wgate = np.asarray(L0_ffn_gate_w).T
    consts = constants()
    for name, bias in (("b_tok", L0_tok_bias), ("b_v", L0_attn_bv), ("b_o", L0_attn_bo)):
        consts[:, _cols[name][0]:_cols[name][1]] = np.asarray(bias)[None, :]

    def blocks(w1, w2, w3, tail):
        def first(w, half):
            return w[:, half * D:(half + 1) * D]

        parts = [first(w1, 0), first(w1, 1), first(w2, 0), first(w2, 1), w3[:, :, :D], w3[:, :, D:]]
        a = np.stack([p.reshape(NE, D, D, tail).transpose(0, 2, 3, 1) for p in parts], axis=1)
        return a.reshape(NE * NBLK, D, tail * D)

    wraw = np.concatenate([
        blocks(*(np.asarray(w) for w in (L0_ffn_spline_w1, L0_ffn_spline_w2, L0_ffn_spline_w3)), NB),
        blocks(*(np.asarray(w) for w in (L0_ffn_scaler_w1, L0_ffn_scaler_w2, L0_ffn_scaler_w3)), 1),
    ], axis=2)
    wbase = blocks(*(np.asarray(w) for w in (L0_ffn_base_w1, L0_ffn_base_w2, L0_ffn_base_w3)), 1)

    nc = bacc.Bacc("TRN2", target_bir_lowering=False, num_devices=1)
    arrays, args = {}, []
    for name, a in (("x2", x2), ("wconv", wconv), ("wattn", wattn), ("battn", battn), ("wgate", wgate),
                    ("wraw", wraw), ("wbase", wbase), ("consts", consts)):
        arrays[name] = np.ascontiguousarray(a)
        args.append(nc.dram_tensor(name, a.shape, mybir.dt.from_np(arrays[name].dtype), kind="ExternalInput").ap())
    out = nc.dram_tensor("out_0", (TOK + TS, D), F32, kind="ExternalOutput").ap()
    audio_tower(nc, *args, out)
    r = run_bass_kernel_spmd(nc, [arrays], core_ids=[0])
    return r.results[0]["out_0"][:TOK].reshape(B, S, D)
```
